# Optimizing a Trainium2 kernel written in Bass

```python
import numpy as np
import jax
import jax.numpy as jnp

def _softmax(x, axis=-1):
    return jax.nn.softmax(x, axis=axis)

def _gelu(x):
    return jax.nn.gelu(x, approximate=True)

def _silu(x):
    return jax.nn.silu(x)

def _sigmoid(x):
    return jax.nn.sigmoid(x)

def _layernorm(x, axis=-1, eps=1e-05):
    m = jnp.mean(x, axis=axis, keepdims=True)
    v = jnp.var(x, axis=axis, keepdims=True)
    return (x - m) / jnp.sqrt(v + eps)

def _scatter_add(tgt, idx, src, axis=0):
    return tgt.at[idx].add(src)

def _segment_sum(src, seg, n):
    return jax.ops.segment_sum(src, seg, n)
kernel_name = 'mk_perceiver_d2_seqx_r8_664da6'

def setup_inputs(seed: int=0):
    np.random.seed(seed)
    _w = jnp.asarray

    def _rec_inputs():
        import jax
        import jax.numpy as jnp
        _rk = jax.random.key(seed)
        x = 7.22e-05 + 1 * jax.random.normal(jax.random.fold_in(_rk, 1), (8, 64, 128), jnp.float32)
        _lenS = 64 - jax.random.randint(jax.random.fold_in(_rk, 7), (8,), 0, max(1, 64 // 4) + 1, jnp.int32)
        _lenS2 = 1601 - jax.random.randint(jax.random.fold_in(_rk, 8), (8,), 0, max(1, 1601 // 4) + 1, jnp.int32)
        _ctx_768P = jax.random.normal(jax.random.fold_in(_rk, 11), (8, 16, 96), jnp.float32)
        _ctx_768c = jax.random.dirichlet(jax.random.fold_in(_rk, 511), 0.3 * jnp.ones((16,), jnp.float32), (8, 1601))
        _ctx_768t = jnp.einsum('bsk,bkd->bsd', _ctx_768c, _ctx_768P)
        _ctx_768t = _ctx_768t * jax.lax.rsqrt(jnp.mean(jnp.square(_ctx_768t)) + 1e-12) * 0.953939
        ctx_768 = -0.000191848 + 0.999787 * (_ctx_768t + 0.3 * jax.random.normal(jax.random.fold_in(_rk, 611), (8, 1601, 96), jnp.float32))
        _validS = jnp.arange(64)[None, :] < _lenS[:, None]
        _validS2 = jnp.arange(1601)[None, :] < _lenS2[:, None]
        _causal = jnp.tril(jnp.ones((64, 64), dtype=bool))
        mask_1x1xSxS2_bk0 = jnp.logical_not(jnp.broadcast_to(_validS2[0:1, None, None, :], (1, 1, 64, 1601)))
        return (x, ctx_768, mask_1x1xSxS2_bk0)
    x, ctx_768, mask_1x1xSxS2_bk0 = _rec_inputs()

    def _L0_xattn_setup():
        import jax, jax.numpy as jnp
        import numpy as np
        B, T, Q_DIM, KV_DIM = (4, 256, 128, 96)
        HEADS, DIM_HEAD = (16, 64)
        INNER = HEADS * DIM_HEAD
        NUM_FRAMES, NUM_PATCHES = (8, 32)
        LN_EPS = 1e-05

        def diagonal_frame_mask(num_patches, num_frames):
            fid = np.repeat(np.arange(num_frames), num_patches)
            m = fid[:, None] == fid[None, :]
            return jnp.asarray(m[None, None])
        key = jax.random.key(seed)
        ks = jax.random.split(key, 6)
        s = lambda d: 1.0 / np.sqrt(d)
        return {'x': jax.random.normal(ks[0], (B, T, Q_DIM), jnp.float32), 'context': jax.random.normal(ks[1], (B, T, KV_DIM), jnp.float32), 'ln_gamma': jnp.ones((Q_DIM,), jnp.float32), 'ln_beta': jnp.zeros((Q_DIM,), jnp.float32), 'Wq': jax.random.normal(ks[2], (Q_DIM, INNER), jnp.float32) * s(Q_DIM), 'Wkv': jax.random.normal(ks[3], (KV_DIM, 2 * INNER), jnp.float32) * s(KV_DIM), 'Wo': jax.random.normal(ks[4], (INNER, Q_DIM), jnp.float32) * s(INNER), 'bo': jnp.zeros((Q_DIM,), jnp.float32), 'mask': diagonal_frame_mask(NUM_PATCHES, NUM_FRAMES)}
    _L0_xattn_all = _L0_xattn_setup()
    _L0_xattn_in = {k: v for k, v in _L0_xattn_all.items() if k in ('ln_gamma', 'ln_beta', 'Wq', 'Wkv', 'Wo', 'bo')}
    del _L0_xattn_all

    def _L0_attn_setup():
        import jax, jax.numpy as jnp
        import numpy as np
        NUM_HEADS = 32
        EPS = 1e-15
        key = jax.random.key(seed)
        k1, k2, k3, k4 = jax.random.split(key, 4)
        B, N, C = (8, 512, 128)
        x = jax.random.normal(k1, (B, N, C), dtype=jnp.float32)
        qkv_weight = jax.random.normal(k2, (3 * C, C), dtype=jnp.float32) * C ** (-0.5)
        proj_weight = jax.random.normal(k3, (C, C), dtype=jnp.float32) * C ** (-0.5)
        proj_bias = jax.random.normal(k4, (C,), dtype=jnp.float32) * 0.01
        return {'x': x, 'qkv_weight': qkv_weight, 'proj_weight': proj_weight, 'proj_bias': proj_bias}
    _L0_attn_all = _L0_attn_setup()
    _L0_attn_in = {k: v for k, v in _L0_attn_all.items() if k in ('qkv_weight', 'proj_weight', 'proj_bias')}
    del _L0_attn_all

    def _L0_ffn_setup():
        import jax, jax.numpy as jnp
        import numpy as np
        BLOCK = 32
        W_BITS = 4
        ACT_BITS = 16

        def act_qdq(x):
            qmax = 2.0 ** (ACT_BITS - 1) - 1.0
            scale = jnp.maximum(jnp.max(jnp.abs(x)) / qmax, 1e-12)
            return jnp.clip(jnp.round(x / scale), -qmax - 1.0, qmax) * scale

        def fixed_qdq_u16(x):
            scale = 1.0 / 65536.0
            return jnp.clip(jnp.round(x / scale), 0.0, 65535.0) * scale

        def lpbq_dequant(w):
            O, I = w.shape
            qmax = 2.0 ** (W_BITS - 1) - 1.0
            wb = w.reshape(O, I // BLOCK, BLOCK)
            s = jnp.maximum(jnp.max(jnp.abs(wb), axis=-1, keepdims=True) / qmax, 1e-12)
            wq = jnp.clip(jnp.round(wb / s), -qmax - 1.0, qmax) * s
            return wq.reshape(O, I)
        key = jax.random.key(seed)
        k1, k2, k3, k4 = jax.random.split(key, 4)
        B, S, H, I = (2, 512, 128, 384)
        x = jax.random.normal(k1, (B, S, H), jnp.float32)
        w_gate = jax.random.normal(k2, (I, H), jnp.float32) * 0.02
        w_up = jax.random.normal(k3, (I, H), jnp.float32) * 0.02
        w_down = jax.random.normal(k4, (H, I), jnp.float32) * 0.02
        return {'x': x, 'w_gate': w_gate, 'w_up': w_up, 'w_down': w_down}
    _L0_ffn_all = _L0_ffn_setup()
    _L0_ffn_in = {k: v for k, v in _L0_ffn_all.items() if k in ('w_gate', 'w_up', 'w_down')}
    del _L0_ffn_all

    def _L1_xattn_setup():
        import jax, jax.numpy as jnp
        import numpy as np
        HEADS = 16
        DIM_HEAD = 64
        key = jax.random.key(seed)
        ks = jax.random.split(key, 7)
        b, n, m = (2, 256, 128)
        query_dim, context_dim = (128, 96)
        inner = HEADS * DIM_HEAD
        s_q = 1.0 / np.sqrt(query_dim)
        s_c = 1.0 / np.sqrt(context_dim)
        s_i = 1.0 / np.sqrt(inner)
        return {'x': jax.random.normal(ks[0], (b, n, query_dim), jnp.float32), 'context': jax.random.normal(ks[1], (b, m, context_dim), jnp.float32), 'Wq': jax.random.normal(ks[2], (query_dim, inner), jnp.float32) * s_q, 'Wk': jax.random.normal(ks[3], (context_dim, inner), jnp.float32) * s_c, 'Wv': jax.random.normal(ks[4], (context_dim, inner), jnp.float32) * s_c, 'Wo': jax.random.normal(ks[5], (inner, query_dim), jnp.float32) * s_i, 'bo': jax.random.normal(ks[6], (query_dim,), jnp.float32) * 0.01}
    _L1_xattn_all = _L1_xattn_setup()
    _L1_xattn_in = {k: v for k, v in _L1_xattn_all.items() if k in ('Wq', 'Wk', 'Wv', 'Wo', 'bo')}
    del _L1_xattn_all

    def _L1_attn_setup():
        import math
        import jax, jax.numpy as jnp
        import numpy as np
        DIM = 128
        DIM_QK = 128
        DIM_V = 128
        NUM_BUCKETS = 32
        MAX_DISTANCE = 128

        def _rel_pos_bucket_causal(seq_len):
            q = np.arange(seq_len)
            n = np.maximum(q[:, None] - q[None, :], 0)
            max_exact = NUM_BUCKETS // 2
            is_small = n < max_exact
            nf = np.maximum(n, 1).astype(np.float32)
            val_if_large = max_exact + (np.log(nf / max_exact) / math.log(MAX_DISTANCE / max_exact) * (NUM_BUCKETS - max_exact)).astype(np.int32)
            val_if_large = np.minimum(val_if_large, NUM_BUCKETS - 1)
            return jnp.asarray(np.where(is_small, n, val_if_large), dtype=jnp.int32)

        def laplacian_attn_fn(x):
            mu = math.sqrt(0.5)
            std = math.sqrt(0.25 * math.pi)
            return (1.0 + jax.lax.erf((x - mu) / (std * math.sqrt(2.0)))) * 0.5
        key = jax.random.key(seed)
        ks = jax.random.split(key, 8)
        B, S = (8, 256)
        x = jax.random.normal(ks[0], (B, S, DIM), dtype=jnp.float32)
        Wqk = jax.random.normal(ks[1], (DIM, DIM_QK), dtype=jnp.float32) * (1.0 / math.sqrt(DIM))
        bqk = jnp.zeros((DIM_QK,), dtype=jnp.float32)
        gamma = jax.random.normal(ks[2], (2, DIM_QK), dtype=jnp.float32) * 0.02
        beta = jnp.zeros((2, DIM_QK), dtype=jnp.float32)
        Wv = jax.random.normal(ks[3], (DIM, DIM_V), dtype=jnp.float32) * (1.0 / math.sqrt(DIM))
        bv = jnp.zeros((DIM_V,), dtype=jnp.float32)
        rel_emb = jax.random.normal(ks[4], (NUM_BUCKETS, 1), dtype=jnp.float32) * 0.02
        return {'x': x, 'Wqk': Wqk, 'bqk': bqk, 'gamma': gamma, 'beta': beta, 'Wv': Wv, 'bv': bv, 'rel_emb': rel_emb}
    _L1_attn_all = _L1_attn_setup()
    _L1_attn_in = {k: v for k, v in _L1_attn_all.items() if k in ('Wqk', 'bqk', 'gamma', 'beta', 'Wv', 'bv', 'rel_emb')}
    del _L1_attn_all

    def _L1_ffn_setup():
        import jax, jax.numpy as jnp
        import numpy as np
        E = 8
        C = 160
        D = 128
        H = 512
        B, S = (4, 256)
        key = jax.random.key(seed)
        ks = jax.random.split(key, 12)
        sc = 0.02
        return {'input': jax.random.normal(ks[0], (B, S, D), jnp.float32), 'router_w': jax.random.normal(ks[1], (D, E), jnp.float32) * sc, 'router_b': jnp.zeros((E,), jnp.float32), 'w1': jax.random.normal(ks[2], (E, D, H), jnp.float32) * sc, 'b1': jnp.zeros((E, H), jnp.float32), 'w2': jax.random.normal(ks[3], (E, H, D), jnp.float32) * sc, 'b2': jnp.zeros((E, D), jnp.float32), 'ow1': jax.random.normal(ks[4], (D, H), jnp.float32) * sc, 'ob1': jnp.zeros((H,), jnp.float32), 'ow2': jax.random.normal(ks[5], (H, D), jnp.float32) * sc, 'ob2': jnp.zeros((D,), jnp.float32)}
    _L1_ffn_all = _L1_ffn_setup()
    _L1_ffn_in = {k: v for k, v in _L1_ffn_all.items() if k in ('router_w', 'router_b', 'w1', 'b1', 'w2', 'b2', 'ow1', 'ob1', 'ow2', 'ob2')}
    del _L1_ffn_all
    return {'x': x, 'ctx_768': ctx_768, 'mask_1x1xSxS2_bk0': mask_1x1xSxS2_bk0, 'L0_xattn_ln_gamma': _L0_xattn_in['ln_gamma'], 'L0_xattn_ln_beta': _L0_xattn_in['ln_beta'], 'L0_xattn_Wq': _L0_xattn_in['Wq'], 'L0_xattn_Wkv': _L0_xattn_in['Wkv'], 'L0_xattn_Wo': _L0_xattn_in['Wo'], 'L0_xattn_bo': _L0_xattn_in['bo'], 'L0_attn_qkv_weight': _L0_attn_in['qkv_weight'], 'L0_attn_proj_weight': _L0_attn_in['proj_weight'], 'L0_attn_proj_bias': _L0_attn_in['proj_bias'], 'L0_ffn_w_gate': _L0_ffn_in['w_gate'], 'L0_ffn_w_up': _L0_ffn_in['w_up'], 'L0_ffn_w_down': _L0_ffn_in['w_down'], 'L1_xattn_Wq': _L1_xattn_in['Wq'], 'L1_xattn_Wk': _L1_xattn_in['Wk'], 'L1_xattn_Wv': _L1_xattn_in['Wv'], 'L1_xattn_Wo': _L1_xattn_in['Wo'], 'L1_xattn_bo': _L1_xattn_in['bo'], 'L1_attn_Wqk': _L1_attn_in['Wqk'], 'L1_attn_bqk': _L1_attn_in['bqk'], 'L1_attn_gamma': _L1_attn_in['gamma'], 'L1_attn_beta': _L1_attn_in['beta'], 'L1_attn_Wv': _L1_attn_in['Wv'], 'L1_attn_bv': _L1_attn_in['bv'], 'L1_attn_rel_emb': _L1_attn_in['rel_emb'], 'L1_ffn_router_w': _L1_ffn_in['router_w'], 'L1_ffn_router_b': _L1_ffn_in['router_b'], 'L1_ffn_w1': _L1_ffn_in['w1'], 'L1_ffn_b1': _L1_ffn_in['b1'], 'L1_ffn_w2': _L1_ffn_in['w2'], 'L1_ffn_b2': _L1_ffn_in['b2'], 'L1_ffn_ow1': _L1_ffn_in['ow1'], 'L1_ffn_ob1': _L1_ffn_in['ob1'], 'L1_ffn_ow2': _L1_ffn_in['ow2'], 'L1_ffn_ob2': _L1_ffn_in['ob2']}

def reference(x, ctx_768, mask_1x1xSxS2_bk0, L0_xattn_ln_gamma, L0_xattn_ln_beta, L0_xattn_Wq, L0_xattn_Wkv, L0_xattn_Wo, L0_xattn_bo, L0_attn_qkv_weight, L0_attn_proj_weight, L0_attn_proj_bias, L0_ffn_w_gate, L0_ffn_w_up, L0_ffn_w_down, L1_xattn_Wq, L1_xattn_Wk, L1_xattn_Wv, L1_xattn_Wo, L1_xattn_bo, L1_attn_Wqk, L1_attn_bqk, L1_attn_gamma, L1_attn_beta, L1_attn_Wv, L1_attn_bv, L1_attn_rel_emb, L1_ffn_router_w, L1_ffn_router_b, L1_ffn_w1, L1_ffn_b1, L1_ffn_w2, L1_ffn_b2, L1_ffn_ow1, L1_ffn_ob1, L1_ffn_ow2, L1_ffn_ob2):
    import jax
    import jax.numpy as jnp

    def _L0_xattn_ref(x, context, ln_gamma, ln_beta, Wq, Wkv, Wo, bo, mask):
        import jax, jax.numpy as jnp
        import numpy as np
        B, T, Q_DIM, KV_DIM = (4, 256, 128, 96)
        HEADS, DIM_HEAD = (16, 64)
        INNER = HEADS * DIM_HEAD
        NUM_FRAMES, NUM_PATCHES = (8, 32)
        LN_EPS = 1e-05

        def diagonal_frame_mask(num_patches, num_frames):
            fid = np.repeat(np.arange(num_frames), num_patches)
            m = fid[:, None] == fid[None, :]
            return jnp.asarray(m[None, None])
        mu = jnp.mean(x, axis=-1, keepdims=True)
        var = jnp.mean(jnp.square(x - mu), axis=-1, keepdims=True)
        xn = (x - mu) * jax.lax.rsqrt(var + LN_EPS) * ln_gamma + ln_beta
        scale = DIM_HEAD ** (-0.5)
        q = xn @ Wq
        kv = context @ Wkv
        k, v = jnp.split(kv, 2, axis=-1)
        split_heads = lambda t: t.reshape(t.shape[0], t.shape[1], HEADS, DIM_HEAD).transpose(0, 2, 1, 3)
        q, k, v = (split_heads(q), split_heads(k), split_heads(v))
        dots = jnp.einsum('bhnd,bhmd->bhnm', q, k) * scale
        dots = jnp.where(mask, dots, -jnp.inf)
        attn = jax.nn.softmax(dots, axis=-1)
        out = jnp.einsum('bhnm,bhmd->bhnd', attn, v)
        out = out.transpose(0, 2, 1, 3).reshape(x.shape[0], x.shape[1], INNER)
        return out @ Wo + bo

    def _L0_attn_ref(x, qkv_weight, proj_weight, proj_bias):
        import jax, jax.numpy as jnp
        import numpy as np
        NUM_HEADS = 32
        EPS = 1e-15
        B, N, C = x.shape
        H = NUM_HEADS
        D = C // H
        qkv = jax.nn.relu(jnp.einsum('bnc,oc->bno', x, qkv_weight))
        qkv = qkv.reshape(B, N, 3, H, D)
        q, k, v = (qkv[:, :, 0], qkv[:, :, 1], qkv[:, :, 2])
        v_pad = jnp.concatenate([v, jnp.ones((B, N, H, 1), dtype=v.dtype)], axis=-1)
        vk = jnp.einsum('bnhe,bnhd->bhed', v_pad.astype(jnp.float32), k.astype(jnp.float32))
        vk_q = jnp.einsum('bhed,bnhd->bnhe', vk, q.astype(jnp.float32))
        proj_input = (vk_q[..., :D] / (vk_q[..., D:] + EPS)).astype(qkv.dtype)
        proj_input = proj_input.reshape(B, N, C)
        y = jnp.einsum('bnc,oc->bno', proj_input, proj_weight) + proj_bias
        return y

    def _L0_ffn_ref(x, w_gate, w_up, w_down):
        import jax, jax.numpy as jnp
        import numpy as np
        BLOCK = 32
        W_BITS = 4
        ACT_BITS = 16

        def act_qdq(x):
            qmax = 2.0 ** (ACT_BITS - 1) - 1.0
            scale = jnp.maximum(jnp.max(jnp.abs(x)) / qmax, 1e-12)
            return jnp.clip(jnp.round(x / scale), -qmax - 1.0, qmax) * scale

        def fixed_qdq_u16(x):
            scale = 1.0 / 65536.0
            return jnp.clip(jnp.round(x / scale), 0.0, 65535.0) * scale

        def lpbq_dequant(w):
            O, I = w.shape
            qmax = 2.0 ** (W_BITS - 1) - 1.0
            wb = w.reshape(O, I // BLOCK, BLOCK)
            s = jnp.maximum(jnp.max(jnp.abs(wb), axis=-1, keepdims=True) / qmax, 1e-12)
            wq = jnp.clip(jnp.round(wb / s), -qmax - 1.0, qmax) * s
            return wq.reshape(O, I)
        x = act_qdq(x)
        up = act_qdq(x @ lpbq_dequant(w_up).T)
        gate = act_qdq(x @ lpbq_dequant(w_gate).T)
        sig = fixed_qdq_u16(jax.nn.sigmoid(gate))
        gate = act_qdq(gate * sig)
        o = act_qdq(gate * up)
        return o @ lpbq_dequant(w_down).T

    def _L1_xattn_ref(x, context, Wq, Wk, Wv, Wo, bo):
        import jax, jax.numpy as jnp
        import numpy as np
        HEADS = 16
        DIM_HEAD = 64
        b, n, _ = x.shape
        h, d = (HEADS, DIM_HEAD)
        scale = d ** (-0.5)
        q = (x @ Wq).reshape(b, n, h, d).transpose(0, 2, 1, 3)
        k = (context @ Wk).reshape(b, -1, h, d).transpose(0, 2, 1, 3)
        v = (context @ Wv).reshape(b, -1, h, d).transpose(0, 2, 1, 3)
        sim = jnp.einsum('bhid,bhjd->bhij', q, k) * scale
        attn = jax.nn.softmax(sim, axis=-1)
        out = jnp.einsum('bhij,bhjd->bhid', attn, v)
        out = out.transpose(0, 2, 1, 3).reshape(b, n, h * d)
        return out @ Wo + bo

    def _L1_attn_ref(x, Wqk, bqk, gamma, beta, Wv, bv, rel_emb):
        import math
        import jax, jax.numpy as jnp
        import numpy as np
        DIM = 128
        DIM_QK = 128
        DIM_V = 128
        NUM_BUCKETS = 32
        MAX_DISTANCE = 128

        def _rel_pos_bucket_causal(seq_len):
            q = np.arange(seq_len)
            n = np.maximum(q[:, None] - q[None, :], 0)
            max_exact = NUM_BUCKETS // 2
            is_small = n < max_exact
            nf = np.maximum(n, 1).astype(np.float32)
            val_if_large = max_exact + (np.log(nf / max_exact) / math.log(MAX_DISTANCE / max_exact) * (NUM_BUCKETS - max_exact)).astype(np.int32)
            val_if_large = np.minimum(val_if_large, NUM_BUCKETS - 1)
            return jnp.asarray(np.where(is_small, n, val_if_large), dtype=jnp.int32)

        def laplacian_attn_fn(x):
            mu = math.sqrt(0.5)
            std = math.sqrt(0.25 * math.pi)
            return (1.0 + jax.lax.erf((x - mu) / (std * math.sqrt(2.0)))) * 0.5
        B, S, _ = x.shape
        qk = jax.nn.swish(jnp.einsum('bsd,de->bse', x, Wqk) + bqk)
        q = qk * gamma[0] + beta[0]
        k = qk * gamma[1] + beta[1]
        v = jax.nn.swish(jnp.einsum('bsd,de->bse', x, Wv) + bv)
        scale = 1.0 / S
        sim = jnp.einsum('bid,bjd->bij', q, k) * scale
        buckets = _rel_pos_bucket_causal(S)
        bias = rel_emb[buckets, 0] * DIM_QK ** 0.5
        sim = sim + bias
        attn = laplacian_attn_fn(sim)
        i = jnp.arange(S)
        future = i[None, :] > i[:, None]
        attn = jnp.where(future, 0.0, attn)
        return jnp.einsum('bij,bjd->bid', attn, v)

    def _L1_ffn_ref(input, router_w, router_b, w1, b1, w2, b2, ow1, ob1, ow2, ob2):
        import jax, jax.numpy as jnp
        import numpy as np
        E = 8
        C = 160
        D = 128
        H = 512
        B, S = (4, 256)
        Bq, Sq, Dq = input.shape
        N = Bq * Sq
        xf = input.reshape(N, Dq)
        probs = jax.nn.softmax(xf @ router_w + router_b, axis=-1)
        eid = jnp.argmax(probs, axis=-1)
        onehot = jax.nn.one_hot(eid, E, dtype=xf.dtype)
        rank = (jnp.cumsum(onehot, axis=0)[jnp.arange(N), eid] - 1.0).astype(jnp.int32)
        valid = rank < C
        pos = jnp.where(valid, rank, 0)
        vmask = valid.astype(xf.dtype)[:, None]
        buf = jnp.zeros((E, C, Dq), xf.dtype).at[eid, pos].add(xf * vmask)
        h = jax.nn.relu(jnp.einsum('ecd,edh->ech', buf, w1) + b1[:, None, :])
        y = jnp.einsum('ech,ehd->ecd', h, w2) + b2[:, None, :]
        y_tok = y[eid, pos] * vmask
        yov = jax.nn.relu(xf @ ow1 + ob1) @ ow2 + ob2
        out = y_tok + yov * (1.0 - vmask)
        return out.reshape(Bq, Sq, Dq)
    x = x + _L0_xattn_ref(_layernorm(x, axis=-1), ctx_768, L0_xattn_ln_gamma, L0_xattn_ln_beta, L0_xattn_Wq, L0_xattn_Wkv, L0_xattn_Wo, L0_xattn_bo, mask_1x1xSxS2_bk0)
    x = x + _L0_attn_ref(_layernorm(x, axis=-1), L0_attn_qkv_weight, L0_attn_proj_weight, L0_attn_proj_bias)
    x = x + _L0_ffn_ref(_layernorm(x, axis=-1), L0_ffn_w_gate, L0_ffn_w_up, L0_ffn_w_down)
    x = x + _L1_xattn_ref(_layernorm(x, axis=-1), ctx_768, L1_xattn_Wq, L1_xattn_Wk, L1_xattn_Wv, L1_xattn_Wo, L1_xattn_bo)
    x = x + _L1_attn_ref(_layernorm(x, axis=-1), L1_attn_Wqk, L1_attn_bqk, L1_attn_gamma, L1_attn_beta, L1_attn_Wv, L1_attn_bv, L1_attn_rel_emb)
    x = x + _L1_ffn_ref(_layernorm(x, axis=-1), L1_ffn_router_w, L1_ffn_router_b, L1_ffn_w1, L1_ffn_b1, L1_ffn_w2, L1_ffn_b2, L1_ffn_ow1, L1_ffn_ob1, L1_ffn_ow2, L1_ffn_ob2)
    return x

_drawn_inputs = setup_inputs


def setup_inputs(seed=0):
    import zlib

    import numpy as np

    out = dict(_drawn_inputs(seed))
    spreads = {'L0_xattn_ln_gamma': (1.0, 0.6),
     'L0_xattn_ln_beta': (0.0, 0.317),
     'L0_xattn_bo': (0.0, 0.1),
     'L1_attn_bqk': (0.0, 2.0),
     'L1_attn_beta': (0.0, 0.8),
     'L1_attn_bv': (0.0, 0.1),
     'L1_ffn_router_b': (0.0, 0.1),
     'L1_ffn_b1': (0.0, 2.0),
     'L1_ffn_b2': (0.0, 0.289),
     'L1_ffn_ob1': (0.0, 0.8),
     'L1_ffn_ob2': (0.0, 0.515)}
    factors = {'L0_attn_proj_bias': 5.214,
     'L0_ffn_w_gate': 8.0,
     'L0_ffn_w_up': 7.96,
     'L0_ffn_w_down': 8.0,
     'L1_xattn_bo': 26.757,
     'L1_attn_Wqk': 8.0,
     'L1_attn_gamma': 8.0,
     'L1_ffn_w1': 3.465,
     'L1_ffn_ow1': 5.587,
     'L1_ffn_ow2': 4.161}
    for name, (base, spread) in spreads.items():
        noise = np.random.default_rng([zlib.crc32(name.encode()), seed]).standard_normal(out[name].shape)
        drawn = base * np.exp(spread * noise) if base else spread * noise
        out[name] = jnp.asarray(drawn.astype(out[name].dtype))
    for name, factor in factors.items():
        out[name] = (out[name] * factor).astype(out[name].dtype)
    return out
```

```python
from contextlib import ExitStack

import numpy as np

import concourse.bass as bass
from concourse import mybir

F32 = mybir.dt.float32
F16 = mybir.dt.float16
U8 = mybir.dt.uint8
I32 = mybir.dt.int32
ALU = mybir.AluOpType
ACT = mybir.ActivationFunctionType
X = mybir.AxisListType.X

P = 128
B, S, D = 8, 64, 128
TOK = B * S
TILES = TOK // P
KEYS, CD = 1601, 96
HEADS, DH = 16, 64
ROWS = HEADS * S
BLOCKS = ROWS // P
HALF = 512
KPAD = 1602
NCH = -(-KEYS // P)
CPAD = CD + 2
SHIFT = CD
NSH = BLOCKS
KS = CD + NSH
TAIL0 = 9
FF = 384
FC = FF // P
WBLK = 32
EXPERTS, CAP, HID = 8, 160, 512
HC = HID // P
SELS = EXPERTS + 1
NEG = -60000.0
BIG = 32768.0
MAGIC = 12582912.0
LN_EPS = 1e-5
BUCKETS, MAXD = 32, 128
MU = float(np.sqrt(0.5))
ERF_A = 1.0 / float(np.sqrt(0.25 * np.pi) * np.sqrt(2.0))
ERF_P = 0.3275911
ERF_C = (0.254829592, -0.284496736, 1.421413741, -1.453152027, 1.061405429)

C_ID, C_BLK, C_CAUSAL, C_NDELTA, C_FIRST, C_ONE, C_ONEHOT, C_FLIP = np.cumsum(
    [0, 128, 128, 128, 8, 8, 128, 128]).tolist()
C_END = C_FLIP + 128
H_ID, H_ONES, H_TRI, H_IND, H_ROW = np.cumsum([0, 128, 128, 128, 512]).tolist()
H_END = H_ROW + SELS * 128


def constants():
    c = np.zeros((P, C_END), np.float32)
    h = np.zeros((P, H_END), np.float16)
    i = np.arange(P)
    c[:, C_ID:C_ID + P] = np.eye(P)
    c[:, C_BLK:C_BLK + P] = i[:, None] // 4 == i[None] // 4
    key, query = i[:, None], i[None]
    c[:, C_CAUSAL:C_CAUSAL + P] = (key // S == query // S) & (key <= query)
    c[SHIFT:SHIFT + NSH, C_NDELTA:C_NDELTA + NSH] = -np.eye(NSH)
    c[:, C_FIRST:C_FIRST + EXPERTS] = EXPERTS - np.arange(EXPERTS)
    c[:, C_ONE:C_ONE + P] = 1.0
    n = np.maximum(np.arange(2 * S) - (S - 1), 0)
    exact = BUCKETS // 2
    large = exact + (np.log(np.maximum(n, 1).astype(np.float32) / exact) / np.log(MAXD / exact)
                     * (BUCKETS - exact)).astype(np.int32)
    bucket = np.where(n < exact, n, np.minimum(large, BUCKETS - 1))
    c[:BUCKETS, C_ONEHOT:C_ONEHOT + 2 * S] = np.arange(BUCKETS)[:, None] == bucket[None]
    c[:S, C_FLIP:C_FLIP + P] = np.arange(S)[:, None] == S - 1 - i[None] % S
    h[:, H_ID:H_ID + P] = np.eye(P)
    h[:, H_ONES:H_ONES + P] = 1.0
    h[:, H_TRI:H_TRI + P] = i[:, None] <= i[None]
    h[:S, H_IND:H_IND + HALF] = (np.arange(HALF)[None] % S == np.arange(S)[:, None]) * BIG
    for e in range(SELS):
        h[e, H_ROW + e * P:H_ROW + (e + 1) * P] = BIG
    return c, h


def chunk(c):
    return c * P, min(P, KEYS - c * P)


def slices(lo, hi, most=HALF):
    n = -(-(hi - lo) // most)
    cuts = [lo + (hi - lo) * i // n for i in range(n + 1)]
    return [(a, b - a) for a, b in zip(cuts, cuts[1:])]


def perceiver(nc, a, out):
    ctx = ExitStack()
    with ctx:
        def sb(name, shape, dt=F32):
            return ctx.enter_context(nc.sbuf_tensor(name, shape, dt))

        sems = {}

        def sem(name):
            if name not in sems:
                sems[name] = ctx.enter_context(nc.semaphore(name))
            return sems[name]

        ctxTh = sb("ctxTh", [P, B * KPAD], F16)
        ctxTl = sb("ctxTl", [P, B * KPAD], F16)
        ctxNh = sb("ctxNh", [P, B * NCH * CPAD], F16)
        ctxNl = sb("ctxNl", [P, B * NCH * CPAD], F16)
        Qh = sb("Qh", [P, B * ROWS], F16)
        Ql = sb("Ql", [P, B * ROWS], F16)
        maskb = sb("maskb", [P, KPAD], F16)
        pool32 = sb("pool32", [P, 11 * 1024])
        P32 = pool32[:, 0:2048]
        rawO = pool32[:, 2048:3072]
        Ph = sb("Ph", [P, 2 * ROWS], F16)
        Pl = sb("Pl", [P, 2 * ROWS], F16)
        On = pool32[:, 3072:3072 + HEADS * TOK].rearrange("p (h t) -> p h t", h=HEADS)
        wraw = pool32[:, 3072:]
        Wq = wraw[:, 0:1024]
        Wk = wraw[:, 1024:2048]
        Wv = wraw[:, 2048:3072]
        Wo = wraw[:, 3072:4096].rearrange("p (g n) -> p g n", g=8)
        WqT = wraw[:, 4096:5120].rearrange("p (g n) -> p g n", g=8)
        WkT = wraw[:, 5120:5120 + 8 * CD].rearrange("p (g n) -> p g n", g=8)
        WvT = wraw[:, 6144:6144 + 8 * CD].rearrange("p (g n) -> p g n", g=8)
        NR = 3
        ring = Qh[:, :].bitcast(F32)[:, 0:NR * NCH * CD].rearrange("p (r c d) -> p r c d", r=NR, c=NCH)
        Ah = wraw[:, 0:HEADS * CD].rearrange("p (h n) -> p h n", h=HEADS)
        Bh = sb("Bh", [P, HEADS, D])
        xs = sb("xs", [P, TILES, D])
        yn = sb("yn", [P, TILES, D])
        yT = sb("yT", [P, TOK])
        cf = sb("cf", [P, C_END])
        ch = sb("ch", [P, H_END], F16)
        vecs = sb("vecs", [64, D])
        vcol = sb("vcol", [P, 64])
        rows1 = sb("rows1", [1, 5 * D])
        mask8 = Pl[0:S, :].bitcast(U8)[:, 0:KEYS]
        st = sb("st", [P, TILES, 6])
        mv = sb("mv", [P, TILES, 2])
        ve = sb("ve", [P, TILES])
        mhalf = sb("mhalf", [P, TILES])
        rstd = sb("rstd", [P, TILES])
        mx = sb("mx", [P, BLOCKS * 4])
        m8 = sb("m8", [P, BLOCKS])
        m16 = sb("m16", [P, BLOCKS], F16)
        qkvT = P32[:, 1152:1536]
        projT = P32[:, 1536:1664]
        ffraw = wraw[:, 6912:8064].rearrange("p (g n) -> p g n", n=P)
        ffT = P32[:, 0:1152].rearrange("p (g n) -> p g n", n=P)
        fsc = sb("fsc", [P, 36])
        fin = sb("fin", [P, 36])
        sraw = rawO[:, 0:512].rearrange("p (g n) -> p g n", n=P)
        wqk1 = sb("wqk1", [P, 2, D])
        rw = sb("rw", [P, EXPERTS])
        rb = sb("rb", [1, EXPERTS])
        b2r = sb("b2r", [SELS, D])
        emb = sb("emb", [BUCKETS, 1])
        gp = sb("gp", [1, 2 * S])
        hank = sb("hank", [S, S])
        biasz = sb("biasz", [P, P])
        gq = sb("gq", [P, 8])
        gr = sb("gr", [2, 8])
        tq = Qh[:, :].bitcast(F32)
        tl = Ql[:, :].bitcast(F32)
        tp = Ph[:, :].bitcast(F32)
        w1 = ctxTh[:, 0:2 * SELS * HID].bitcast(F32).rearrange("p (e n) -> p e n", e=SELS)
        w2 = ctxTl[:, 0:2 * SELS * HID].bitcast(F32).rearrange("p (e c n) -> p e c n", e=SELS, c=HC)
        scratch = nc.dram_tensor("bias_row", (2 * S,), F32, kind="Internal").ap()

        PS = ctx.enter_context(nc.psum_tensor("PS", [P, 8 * HALF], F32))
        PO = PS[:, 2048:3072]

        def bank(k):
            return PS[:, k * HALF:(k + 1) * HALF]

        MISC = [bank(6), bank(7)]
        ident = cf[:, C_ID:C_ID + P]
        ident16 = ch[:, H_ID:H_ID + P]
        ones1 = cf[0:1, C_ONE:C_ONE + P]

        block = ctx.enter_context(nc.Block())

        class Att:

            def __init__(self, name, chunks, masked):
                self.name, self.chunks, self.masked = name, chunks, masked
                self.n = len(chunks)
                self.slices = slices(chunks[0] * P, KEYS)
                self.units = BLOCKS * len(self.slices)
                slots = max(1, self.n - 2 if self.n < 6 else self.n - 4)
                self.per = [self.units * (s + 1) // slots - self.units * s // slots if s < slots else 0
                            for s in range(self.n)]
                self.recip_slot = 1
                self.norm_slot = 2

            def sem(self, what):
                return sem(f"{self.name}_{what}")

            def base(self, b):
                first = self.units + 1
                if isinstance(b, int) and b == 0:
                    return first
                return 2 * first + (b - 1) * (first + 2)

        def pe_max_unit(pe, t, nb, u, full_wait):
            j, s = divmod(u, len(t.slices))
            k0, n = t.slices[s]
            if full_wait is not None:
                pe.wait_ge(t.sem("spare_read"), full_wait)
            o = MISC[u % 2][:, 0:n]
            ins = nc.tensor.matmul(o, Qh[0:CD, bass.ds(nb * ROWS + j * P, P)],
                                   ctxTh[0:CD, bass.ds(nb * KPAD + k0, n)], start=True, stop=not t.masked)
            if t.masked:
                ins = nc.tensor.matmul(o, ch[:, H_IND:H_IND + P], maskb[:, k0:k0 + n], start=False, stop=True)
            ins.then_inc(t.sem("spare_written"), 1)

        def pe_shift(pe, t, nb, full_wait):
            pe.wait_ge(t.sem("max_ready"), nb + 1)
            pe.wait_ge(t.sem("spare_read"), full_wait)
            nc.tensor.transpose(MISC[0].bitcast(F16)[SHIFT:SHIFT + NSH, 0:P], m16[:, :], ident16)\
                .then_inc(t.sem("spare_written"), 1)

        def pe_scores(pe, t, nb, c, par, half):
            k0, n = chunk(c)
            o = PS[0:n, bass.ds(par * ROWS + half * HALF, HALF)]
            q = nb * ROWS + half * HALF
            hi = ctxTh[0:KS, bass.ds(nb * KPAD + k0, n)]
            nc.tensor.matmul(o, hi, Qh[0:KS, bass.ds(q, HALF)], start=True, stop=False)
            nc.tensor.matmul(o, ctxTh[0:CD, bass.ds(nb * KPAD + k0, n)], Ql[0:CD, bass.ds(q, HALF)],
                             start=False, stop=False)
            ins = nc.tensor.matmul(o, ctxTl[0:CD, bass.ds(nb * KPAD + k0, n)], Qh[0:CD, bass.ds(q, HALF)],
                                   start=False, stop=not t.masked)
            if t.masked:
                ins = nc.tensor.matmul(o, maskb[:, k0:k0 + n], ch[:, H_IND:H_IND + HALF], start=False, stop=True)
            if half == 1:
                ins.then_inc(t.sem("scores"), 1)

        def pe_out(pe, t, nb, c, par, half, first, last):
            _, n = chunk(c)
            o = PO[0:CD + 1, half * HALF:(half + 1) * HALF]
            at = nb * (NCH * CPAD) + c * CPAD
            hi = ctxNh[0:n, bass.ds(at, CD + 1)]
            ph = Ph[0:n, bass.ds(par * ROWS + half * HALF, HALF)]
            nc.tensor.matmul(o, hi, ph, start=first, stop=False)
            nc.tensor.matmul(o, ctxNl[0:n, bass.ds(at, CD + 1)], ph, start=False, stop=False)
            return nc.tensor.matmul(o, hi, Pl[0:n, bass.ds(par * ROWS + half * HALF, HALF)],
                                    start=False, stop=last)

        def pe_sequence(pe, t, b, pars, first=False, last=False):
            g0 = b * t.n
            used = 0
            unit = 0

            def spare_wait(n):
                return t.base(b) + (n - 1 if n else 0)

            for i, c in enumerate(t.chunks):
                pi = pars[i % 2]
                ahead = i + 2
                nb, ci = (b, ahead) if ahead < t.n else (b + 1, ahead - t.n)
                units = list(range(unit, unit + t.per[i])) if not last else []
                unit += len(units)
                if i == t.norm_slot and not first:
                    pe.wait_ge(t.sem("rden"), b)
                    for half in range(2):
                        pe.wait_ge(t.sem("spare_read"), spare_wait(used))
                        nc.tensor.matmul(MISC[used % 2][0:CD, :], cf[CD:CD + 1, C_ONE:C_ONE + CD],
                                         rawO[CD:CD + 1, half * HALF:(half + 1) * HALF],
                                         start=True, stop=True).then_inc(t.sem("spare_written"), 1)
                        used += 1
                if i == t.n - 2 and not last:
                    pe_shift(pe, t, b + 1, t.base(b) + used)
                    pe.wait_ge(t.sem("shift"), b + 2)

                def some_units():
                    nonlocal used
                    if units:
                        k = units.pop(0)
                        assert used % 2 == k % 2
                        pe_max_unit(pe, t, b + 1, k, spare_wait(used))
                        used += 1

                some_units()
                if not (last and nb is not b):
                    pe.wait_ge(t.sem("exp"), g0 + i + 1)
                    pe_scores(pe, t, nb, t.chunks[ci], pi, 0)
                    some_units()
                    pe_scores(pe, t, nb, t.chunks[ci], pi, 1)
                some_units()
                pe.wait_ge(t.sem("p_high"), g0 + i + 1)
                pe.wait_ge(t.sem("p_low"), g0 + i + 1)
                if i == 0 and not first:
                    pe.wait_ge(t.sem("out_copied"), b)
                pe_out(pe, t, b, c, pi, 0, i == 0, i == t.n - 1)
                some_units()
                ins = pe_out(pe, t, b, c, pi, 1, i == 0, i == t.n - 1)
                ins.then_inc(t.sem("out"), 1)
                while units:
                    some_units()

        def pe_attention(pe, t):
            for u in range(t.units):
                pe_max_unit(pe, t, 0, u, u - 1 if u >= 2 else None)
            pe_shift(pe, t, 0, t.units)
            pe.wait_ge(t.sem("shift"), 1)
            for i in range(2):
                for half in range(2):
                    pe_scores(pe, t, 0, t.chunks[i], i, half)
            pe_sequence(pe, t, 0, (0, 1), first=True)
            with pe.Fori(1, B - 1) as b:
                pe_sequence(pe, t, b, parities(pe, t, b))
            pe_sequence(pe, t, B - 1, parities(pe, t, B - 1), last=True)
            base = t.base(B - 1) + 2
            pe.wait_ge(t.sem("rden"), B)
            for half in range(2):
                pe.wait_ge(t.sem("spare_read"), base - 1 + half)
                nc.tensor.matmul(MISC[half][0:CD, :], cf[CD:CD + 1, C_ONE:C_ONE + CD],
                                 rawO[CD:CD + 1, half * HALF:(half + 1) * HALF],
                                 start=True, stop=True).then_inc(t.sem("spare_written"), 1)

        def parities(eng, t, b):
            if isinstance(b, int):
                return b * t.n % 2, (b * t.n + 1) % 2
            even = eng.snap((b * t.n) % 2)
            return even, eng.snap(1 - even)

        def act_sequence(act, t, b, pars, first=False):
            g0 = b * t.n
            for i, c in enumerate(t.chunks):
                pi = pars[i % 2]
                _, n = chunk(c)
                at = bass.ds(pi * ROWS, ROWS)
                act.wait_ge(t.sem("scores"), g0 + i + 1)
                if not (first and i < 2):
                    act.wait_ge(t.sem("p_low"), g0 + i - 1)
                nc.scalar.activation(P32[0:n, at], PS[0:n, at], ACT.Exp).then_inc(t.sem("exp"), 1)
                act.wait_ge(t.sem("exp"), g0 + i + 1)
                if not (first and i < 2):
                    act.wait_ge(t.sem("out"), g0 + i - 1)
                nc.scalar.activation(Ph[0:n, at], P32[0:n, at], ACT.Copy).then_inc(t.sem("p_high"), 1)
                if i == 1 and not first:
                    act_copy_out(act, t, b)

        def act_copy_out(act, t, b):
            act.wait_ge(t.sem("out"), b * t.n)
            if not (isinstance(b, int) and b == 1):
                act.wait_ge(t.sem("normed"), b - 1)
            nc.scalar.activation(rawO[0:CD + 1, :], PO[0:CD + 1, :], ACT.Copy).then_inc(t.sem("out_copied"), 1)

        def act_attention(act, t):
            act_sequence(act, t, 0, (0, 1), first=True)
            act_sequence(act, t, 1, parities(act, t, 1))
            with act.Fori(0, (B - 2) // 2) as pair:
                b = pair * 2 + 2
                act_sequence(act, t, b, (0, 1))
                act_sequence(act, t, b + 1, parities(act, t, 1))
            act_copy_out(act, t, B)

        def dve_max_unit(dve, t, u, count):
            j, s = divmod(u, len(t.slices))
            dve.wait_ge(t.sem("spare_written"), count)
            nc.vector.tensor_reduce(mx[:, u:u + 1], MISC[u % 2][:, 0:t.slices[s][1]], X, ALU.max)\
                .then_inc(t.sem("spare_read"), 1)

        def dve_shift(dve, t, nb, count, read):
            dve.wait_ge(t.sem("spare_read"), read)
            src = mx[:, 0:BLOCKS]
            if len(t.slices) > 1:
                nc.vector.tensor_reduce(m8[:, :], mx[:, 0:t.units].rearrange("p (j s) -> p j s", j=BLOCKS),
                                        X, ALU.max).then_inc(t.sem("max_whole"), 1)
                dve.wait_ge(t.sem("max_whole"), nb + 1)
                src = m8[:, :]
            nc.vector.tensor_scalar(m16[:, :], src, NEG, -NEG, ALU.max, ALU.min).then_inc(t.sem("max_ready"), 1)
            dve.wait_ge(t.sem("spare_written"), count)
            mt = MISC[0].bitcast(F16)[SHIFT:SHIFT + NSH, 0:P]
            nc.vector.tensor_tensor(
                Qh[SHIFT:SHIFT + NSH, bass.ds(nb * ROWS, ROWS)].rearrange("p (j r) -> p j r", j=BLOCKS),
                mt.unsqueeze(1).to_broadcast([NSH, BLOCKS, P]),
                cf[SHIFT:SHIFT + NSH, C_NDELTA:C_NDELTA + NSH].unsqueeze(2).to_broadcast([NSH, BLOCKS, P]),
                ALU.mult).then_inc(t.sem("spare_read"), 1)
            dve.wait_ge(t.sem("spare_read"), read + 1)
            nc.vector.tensor_copy(ve[0:1, 0:1], ve[0:1, 0:1]).then_inc(t.sem("shift"), 1)

        def dve_norm(dve, t, b, half, spare, count):
            dve.wait_ge(t.sem("spare_written"), count)
            nc.vector.tensor_tensor(
                On[0:CD, half * 8:(half + 1) * 8, bass.ds((b - 1) * S, S)],
                spare[0:CD, :].rearrange("p (h s) -> p h s", h=8),
                rawO[0:CD, half * HALF:(half + 1) * HALF].rearrange("p (h s) -> p h s", h=8),
                ALU.mult).then_inc(t.sem("spare_read"), 1)

        def dve_recip(dve, t, b):
            dve.wait_ge(t.sem("out_copied"), b)
            nc.vector.reciprocal(rawO[CD:CD + 1, :], rawO[CD:CD + 1, :]).then_inc(t.sem("rden"), 1)

        def dve_sequence(dve, t, b, pars, first=False, last=False):
            g0 = b * t.n
            used = 0
            unit = 0
            for i, c in enumerate(t.chunks):
                pi = pars[i % 2]
                _, n = chunk(c)
                if i == t.norm_slot and not first:
                    for half in range(2):
                        dve_norm(dve, t, b, half, MISC[used % 2], t.base(b) + used + 1)
                        used += 1
                    dve.wait_ge(t.sem("spare_read"), t.base(b) + used)
                    nc.vector.tensor_copy(ve[0:1, 0:1], ve[0:1, 0:1]).then_inc(t.sem("normed"), 1)
                if i == t.n - 2 and not last:
                    dve_shift(dve, t, b + 1, t.base(b) + used + 1, t.base(b) + used)
                    used += 1
                dve.wait_ge(t.sem("p_high"), g0 + i + 1)
                if not (first and i < 2):
                    dve.wait_ge(t.sem("out"), g0 + i - 1)
                at = bass.ds(pi * ROWS, ROWS)
                nc.vector.tensor_tensor(Pl[0:n, at], P32[0:n, at], Ph[0:n, at], ALU.subtract)\
                    .then_inc(t.sem("p_low"), 1)
                for u in range(unit, unit + (t.per[i] if not last else 0)):
                    used += 1
                    dve_max_unit(dve, t, u, t.base(b) + used)
                unit += t.per[i]
                if i == t.recip_slot and not first:
                    dve_recip(dve, t, b)

        def dve_attention(dve, t):
            for u in range(t.units):
                dve_max_unit(dve, t, u, u + 1)
            dve_shift(dve, t, 0, t.units + 1, t.units)
            dve_sequence(dve, t, 0, (0, 1), first=True)
            with dve.Fori(0, (B - 2) // 2) as pair:
                b = pair * 2 + 1
                dve_sequence(dve, t, b, parities(dve, t, 1))
                dve_sequence(dve, t, b + 1, (0, 1))
            dve_sequence(dve, t, B - 1, parities(dve, t, B - 1), last=True)
            dve_recip(dve, t, B)
            base = t.base(B - 1) + 2
            for half in range(2):
                dve_norm(dve, t, B, half, MISC[half], base + 1 + half)

        att0 = Att("x0", list(range(NCH)), True)
        att0s = Att("x0", list(range(TAIL0, NCH)), True)
        att1 = Att("x1", list(range(NCH)), False)

        def either(eng, run):
            eng.wait_ge(sem("flag"), 1)
            v = eng.value_load(flag_i[0:1, 0:1], min_val=0, max_val=1)
            with eng.If(v > 0):
                run(eng, att0)
            with eng.Else():
                run(eng, att0s)

        flag_i = sb("flag_i", [1, 1], I32)
        flag_c = sb("flag_c", [S, 1])
        flag_r = sb("flag_r", [1, 1])

        LNS = ["l0a", "l0b", "l1", "l2", "l3", "l4", "l5"]

        def nth(tag):
            return LNS.index(tag) + 1

        def dve_ln(dve, tag, src, ready):
            dve.wait_ge(*ready)
            for t in range(TILES):
                ins = nc.vector.bn_stats(st[:, t, :], src[:, t, :])
            ins.then_inc(sem("ln_stats"), 1)
            dve.wait_ge(sem("ln_stats"), 2 * nth(tag) - 1)
            for t in range(TILES):
                ins = nc.vector.bn_aggr(mv[:, t, :], st[:, t, :])
            ins.then_inc(sem("ln_stats"), 1)
            dve.wait_ge(sem("ln_stats"), 2 * nth(tag))
            nc.vector.tensor_scalar(ve[:, :], mv[:, :, 1], LN_EPS, None, ALU.add).then_inc(sem("ln_var"), 1)
            dve.wait_ge(sem("ln_rstd"), nth(tag))
            for t in range(TILES):
                ins = nc.vector.tensor_scalar(yn[:, t, :], src[:, t, :], mv[:, t, 0:1], rstd[:, t:t + 1],
                                              ALU.subtract, ALU.mult)
            ins.then_inc(sem("ln_rows"), 1)

        def pool_ln(pool, tag):
            pool.wait_ge(sem("ln_var"), nth(tag))
            nc.gpsimd.tensor_tensor(rstd[:, :], ve[:, :], mhalf[:, :], ALU.pow).then_inc(sem("ln_rstd"), 1)

        def pe_rows_T(pe, src, dst, done):
            for t in range(TILES):
                ins = nc.tensor.transpose(dst[:, t * P:(t + 1) * P], src[:, t, :], ident)
            ins.then_inc(done, 1)

        def dve_residual(dve, tag, o):
            dve.wait_ge(sem(tag + "_y"), 1)
            nc.vector.tensor_tensor(xs[:, :, :], xs[:, :, :], o.rearrange("p (t n) -> p t n", t=TILES), ALU.add)\
                .then_inc(sem("x_" + tag), 1)

        def pe_heads_out(pe, tag, t, bias, o):
            for u in range(TILES):
                for h in range(HEADS):
                    nc.tensor.matmul(o[:, u * P:(u + 1) * P], On[0:CD, h, u * P:(u + 1) * P], Bh[0:CD, h, :],
                                     start=(h == 0), stop=False)
                ins = nc.tensor.matmul(o[:, u * P:(u + 1) * P], ones1, bias, start=False, stop=True)
            ins.then_inc(sem(tag + "_y"), 1)

        def layer(tag):
            return int(tag[1])

        def pe_absorb(pe, tag):
            for i in range(24):
                g, which = i % 8, i // 8
                src, rows = ((Wq, P), (Wk, CD), (Wv, CD))[which]
                k = i // 4
                nc.tensor.transpose(bank(k)[:, (i % 4) * P:(i % 4) * P + rows],
                                    src[0:rows, g * P:(g + 1) * P], ident[0:rows, 0:rows])\
                    .then_inc(sem("wT"), 1)
            for which in range(2):
                for k in range(4):
                    if k < 2:
                        pe.wait_ge(sem("wTs"), 6 * layer(tag) + 6)
                    else:
                        pe.wait_ge(sem("wTs"), 6 * layer(tag) + 6)
                    o = bank(6 + k % 2)
                    if which or k >= 2:
                        pe.wait_ge(sem("abs"), 8 * layer(tag) + 4 * which + k - 1)
                    for i in range(4):
                        h = 8 * (k // 2) + 2 * i + k % 2
                        r = slice(DH * (h % 2), DH * (h % 2) + DH)
                        if which == 0:
                            ins = nc.tensor.matmul(o[:, i * P:i * P + CD], WqT[r, h // 2, :], WkT[r, h // 2, :],
                                                   start=True, stop=True)
                        else:
                            ins = nc.tensor.matmul(o[0:CD, i * P:(i + 1) * P], WvT[r, h // 2, :], Wo[r, h // 2, :],
                                                   start=True, stop=True)
                    ins.then_inc(sem("absp"), 1)

        def act_absorb(act, tag):
            for i in range(6):
                act.wait_ge(sem("wT"), 24 * layer(tag) + 4 * (i + 1))
                dst, rows = ((WqT, P), (WkT, CD), (WvT, CD))[i // 2]
                src = bank(i).rearrange("p (g n) -> p g n", g=4)[:, :, 0:rows]
                nc.scalar.activation(dst[:, 4 * (i % 2):4 * (i % 2) + 4, :], src, ACT.Copy)\
                    .then_inc(sem("wTs"), 1)

        def dve_absorb(dve, tag):
            for k in range(8):
                dve.wait_ge(sem("absp"), 8 * layer(tag) + k + 1)
                h0 = 8 * (k % 4 // 2) + k % 2
                src = bank(6 + k % 2).rearrange("p (g n) -> p g n", g=4)
                if k < 4:
                    nc.vector.tensor_scalar(Ah[:, h0:h0 + 7:2, :], src[:, :, 0:CD], DH ** -0.5, None, ALU.mult)\
                        .then_inc(sem("abs"), 1)
                else:
                    nc.vector.tensor_copy(Bh[0:CD, h0:h0 + 7:2, :], src[0:CD, :, :]).then_inc(sem("abs"), 1)

        def pe_queries(pe, tag, rdy):
            pe.wait_ge(*rdy)
            pe.wait_ge(sem("abs"), 8 * layer(tag) + 8)
            for h in range(HEADS):
                if h >= 4:
                    pe.wait_ge(sem("ql"), 16 * layer(tag) + h - 3)
                nc.tensor.matmul(bank(h % 4)[0:CD, :], Ah[:, h, :], yT[:, :], start=True, stop=True)\
                    .then_inc(sem("q"), 1)

        def q_view(t, h):
            return t[0:CD, :].rearrange("p (b r) -> p b r", b=B)[:, :, h * S:(h + 1) * S]

        def act_queries(act, tag):
            for h in range(HEADS):
                act.wait_ge(sem("q"), 16 * layer(tag) + h + 1)
                nc.scalar.activation(q_view(Qh, h), bank(h % 4)[0:CD, :].rearrange("p (b s) -> p b s", b=B), ACT.Copy)\
                    .then_inc(sem("qh"), 1)

        def dve_queries(dve, tag):
            for h in range(HEADS):
                dve.wait_ge(sem("qh"), 16 * layer(tag) + h + 1)
                nc.vector.tensor_tensor(q_view(Ql, h), bank(h % 4)[0:CD, :].rearrange("p (b s) -> p b s", b=B),
                                        q_view(Qh, h), ALU.subtract).then_inc(sem("ql"), 1)

        def load_absorb(eng, tag, wq, wk, wv, wo):
            eng.dma_start(Wq, wq).then_inc(sem(tag + "_w"), 16)
            eng.dma_start(Wk[0:CD, :], wk).then_inc(sem(tag + "_w"), 16)
            eng.dma_start(Wv[0:CD, :], wv).then_inc(sem(tag + "_w"), 16)
            eng.dma_start(Wo, wo.rearrange("(g p) n -> p g n", p=P)).then_inc(sem(tag + "_w"), 16)

        def dve_scales(dve, tag, n, count):
            dve.wait_ge(sem("gT"), count)
            nc.vector.tensor_reduce(gr[0:n, 0:1], bank(7)[0:n, 0:P], X, ALU.max).then_inc(sem("g1"), 1)
            dve.wait_ge(sem("g1"), count)
            nc.vector.tensor_scalar(gr[0:n, 1:1 + n], ident[0:n, 0:n], gr[0:n, 0:1], None, ALU.mult)\
                .then_inc(sem("g2"), 1)
            dve.wait_ge(sem("gB"), count)
            nc.vector.tensor_scalar(gq[:, 2:2 + n], bank(7)[:, 256:256 + n], 1.0 / 32767.0, 1e-12,
                                    ALU.mult, ALU.max).then_inc(sem("g3"), 1)
            dve.wait_ge(sem("g3"), count)
            nc.vector.reciprocal(gq[:, 4:4 + n], gq[:, 2:2 + n]).then_inc(sem("g4"), 1)
            dve.wait_ge(sem("g4"), count)

        def pe_scales(pe, n, count):
            pe.wait_ge(sem("g0"), count)
            nc.tensor.transpose(bank(7)[0:n, 0:P], gq[:, 0:n], ident).then_inc(sem("gT"), 1)
            pe.wait_ge(sem("g2"), count)
            nc.tensor.matmul(bank(7)[:, 256:256 + n], cf[0:n, C_ONE:C_ONE + P], gr[0:n, 1:1 + n],
                             start=True, stop=True).then_inc(sem("gB"), 1)

        @block.sync
        def _(sp):
            sp.dma_start(xs[:, :, :], a["x"].rearrange("b s d -> (b s) d").rearrange("(t p) d -> p t d", p=P))\
                .then_inc(sem("x_in"), 16)
            sp.dma_start(cf[:, :], a["cf"]).then_inc(sem("consts"), 16)
            sp.dma_start(ch[:, :], a["ch"]).then_inc(sem("consts"), 16)
            v = [a["L0_xattn_ln_gamma"], a["L0_xattn_ln_beta"], a["L1_attn_bqk"]]
            for i, r in enumerate(v):
                sp.dma_start(vecs[i:i + 1, :], r.unsqueeze(0)).then_inc(sem("vecs"), 16)
            sp.dma_start(vecs[3:5, :], a["L1_attn_gamma"]).then_inc(sem("vecs"), 16)
            sp.dma_start(vecs[5:7, :], a["L1_attn_beta"]).then_inc(sem("vecs"), 16)
            sp.dma_start(vecs[7:39, :], a["L1_ffn_b1"].rearrange("e (c n) -> (e c) n", n=P)).then_inc(sem("vecs"), 16)
            sp.dma_start(vecs[39:43, :], a["L1_ffn_ob1"].rearrange("(c n) -> c n", n=P)).then_inc(sem("vecs"), 16)
            sp.dma_start(emb[:, :], a["L1_attn_rel_emb"]).then_inc(sem("vecs"), 16)
            load_absorb(sp, "w0", a["L0_xattn_Wq"], a["L0_xattn_Wkv"][:, 0:1024], a["L0_xattn_Wkv"][:, 1024:2048],
                        a["L0_xattn_Wo"])
            sp.dma_start(mask8[:, :], a["mask_1x1xSxS2_bk0"].rearrange("a b s k -> (a b s) k")).then_inc(sem("mask"), 16)
            for b in range(B):
                if b >= NR:
                    sp.wait_ge(sem("ctx_nl"), b - NR + 1)
                    sp.wait_ge(sem("ctx_tp"), 4 * (b - NR + 1))
                src = a["ctx_768"][b]
                r = ring[:, b % NR, :, :]
                sp.dma_start(r[:, 0:NCH - 1, :], src[0:(NCH - 1) * P, :].rearrange("(c p) d -> p c d", p=P))\
                    .then_inc(sem(f"ctx{b % NR}"), 16)
                sp.dma_start(r[0:KEYS - (NCH - 1) * P, NCH - 1, :], src[(NCH - 1) * P:KEYS, :])\
                    .then_inc(sem(f"ctx{b % NR}"), 16)
            sp.dma_start(wqk1[:, 0, :], a["L1_attn_Wqk"]).then_inc(sem("small"), 16)
            sp.dma_start(wqk1[:, 1, :], a["L1_attn_Wv"]).then_inc(sem("small"), 16)
            sp.dma_start(rw[:, :], a["L1_ffn_router_w"]).then_inc(sem("small"), 16)
            sp.dma_start(rb[:, :], a["L1_ffn_router_b"].unsqueeze(0)).then_inc(sem("small"), 16)
            sp.dma_start(b2r[0:EXPERTS, :], a["L1_ffn_b2"]).then_inc(sem("small"), 16)
            sp.dma_start(b2r[EXPERTS:SELS, :], a["L1_ffn_ob2"].unsqueeze(0)).then_inc(sem("small"), 16)
            for i, n in enumerate(["L0_xattn_bo", "L0_attn_proj_bias", "L1_xattn_bo", "L1_attn_bv"]):
                sp.dma_start(rows1[:, i * D:(i + 1) * D], a[n].unsqueeze(0)).then_inc(sem("small"), 16)
            sp.wait_ge(sem("gp"), 1)
            sp.dma_start(scratch.unsqueeze(0), gp[:, :]).then_inc(sem("gp_out"), 16)
            sp.wait_ge(sem("gp_out"), 16)
            hs = bass.AP(scratch.tensor, 0, [[1, S], [1, S]])
            sp.dma_start(hank[:, :], hs).then_inc(sem("hank"), 16)
            sp.wait_ge(sem("a0_y"), 1)
            sp.dma_start(sraw[:, 0:3, :], a["L0_attn_qkv_weight"].rearrange("(g p) n -> p g n", p=P)).then_inc(sem("mid"), 16)
            sp.dma_start(sraw[:, 3, :], a["L0_attn_proj_weight"]).then_inc(sem("mid"), 16)
            sp.dma_start(ffraw[:, 0:3, :], a["L0_ffn_w_gate"].rearrange("(g p) n -> p g n", p=P)).then_inc(sem("mid"), 16)
            sp.dma_start(ffraw[:, 3:6, :], a["L0_ffn_w_up"].rearrange("(g p) n -> p g n", p=P)).then_inc(sem("mid"), 16)
            sp.dma_start(ffraw[:, 6:9, :], a["L0_ffn_w_down"].rearrange("p (g n) -> p g n", g=3)).then_inc(sem("mid"), 16)
            load_absorb(sp, "w1", a["L1_xattn_Wq"], a["L1_xattn_Wk"], a["L1_xattn_Wv"], a["L1_xattn_Wo"])
            sp.wait_ge(sem("a3_y"), 1)
            for e in range(EXPERTS):
                sp.dma_start(w1[:, e, :], a["L1_ffn_w1"][e]).then_inc(sem(f"ex{e}"), 16)
                sp.dma_start(w2[:, e, :, :], a["L1_ffn_w2"][e].rearrange("(c p) n -> p c n", p=P)).then_inc(sem(f"ex{e}"), 16)
            sp.dma_start(w1[:, EXPERTS, :], a["L1_ffn_ow1"]).then_inc(sem(f"ex{EXPERTS}"), 16)
            sp.dma_start(w2[:, EXPERTS, :, :], a["L1_ffn_ow2"].rearrange("(c p) n -> p c n", p=P)).then_inc(sem(f"ex{EXPERTS}"), 16)
            sp.wait_ge(sem("x_a5"), 1)
            sp.dma_start(out.rearrange("b s d -> (b s) d").rearrange("(t p) d -> p t d", p=P), xs[:, :, :])\
                .then_inc(sem("stored"), 16)
            sp.wait_ge(sem("stored"), 16)

        @block.gpsimd
        def _(pool):
            nc.gpsimd.memset(mhalf[:, :], -0.5).then_inc(sem("mhalf"), 1)
            pool.wait_ge(sem("mhalf"), 1)
            nc.gpsimd.memset(maskb[S:P, :], 0.0).then_inc(sem("maskz"), 1)
            pool.wait_ge(sem("maskz"), 1)
            nc.gpsimd.memset(ctxTh[CD:P, :], 1.0).then_inc(sem("ones_rows"), 1)
            pool.wait_ge(sem("ones_rows"), 1)
            n3 = ctxNh[:, :].rearrange("p (c f) -> p c f", f=CPAD)
            nc.gpsimd.memset(n3[:, :, CD:CPAD], 1.0).then_inc(sem("ones_col"), 1)
            n3 = ctxNl[:, :].rearrange("p (c f) -> p c f", f=CPAD)
            nc.gpsimd.memset(n3[:, :, CD:CPAD], 0.0).then_inc(sem("ones_col"), 1)
            pool_ln(pool, "l0a")
            pool_ln(pool, "l0b")
            for b in range(B):
                pool.wait_ge(sem(f"ctx{b % NR}"), 32 * (b // NR + 1))
                h3 = ctxNh[:, :].rearrange("p (b c f) -> p b c f", b=B, c=NCH)[:, b]
                l3 = ctxNl[:, :].rearrange("p (b c f) -> p b c f", b=B, c=NCH)[:, b]
                last = KEYS - (NCH - 1) * P
                nc.gpsimd.tensor_copy(h3[:, 0:NCH - 1, 0:CD], ring[:, b % NR, 0:NCH - 1, :]).then_inc(sem("ctx_nh"), 1)
                nc.gpsimd.tensor_copy(h3[0:last, NCH - 1, 0:CD], ring[0:last, b % NR, NCH - 1, :]).then_inc(sem("ctx_nh"), 1)
                pool.wait_ge(sem("ctx_nh"), 2 * b + 2)
                nc.gpsimd.tensor_tensor(l3[:, 0:NCH - 1, 0:CD], ring[:, b % NR, 0:NCH - 1, :],
                                        h3[:, 0:NCH - 1, 0:CD], ALU.subtract)
                nc.gpsimd.tensor_tensor(l3[0:last, NCH - 1, 0:CD], ring[0:last, b % NR, NCH - 1, :],
                                        h3[0:last, NCH - 1, 0:CD], ALU.subtract).then_inc(sem("ctx_nl"), 1)
            for tag in ("l1", "l2", "l3", "l4", "l5"):
                pool_ln(pool, tag)

        @block.scalar
        def _(act):
            act.wait_ge(sem("vT"), 1)
            nc.scalar.activation(vcol[:, 0:43], bank(7)[:, 0:43], ACT.Copy).then_inc(sem("vcol"), 1)
            act_absorb(act, "w0")
            for b in range(B):
                for k in range(4):
                    act.wait_ge(sem("ctx_tp"), 4 * b + k + 1)
                    k0, n = k * HALF, min(HALF, KEYS - k * HALF)
                    nc.scalar.activation(ctxTh[0:CD, b * KPAD + k0:b * KPAD + k0 + n], bank(k)[0:CD, 0:n],
                                         ACT.Copy).then_inc(sem("ctx_th"), 1)
            act.wait_ge(sem("ln_T"), nth("l0b") - 1)
            act.wait_ge(sem("vcol"), 1)
            nc.scalar.activation(yT[:, :], bank(6), ACT.Identity, bias=vcol[:, 1:2], scale=vcol[:, 0:1])\
                .then_inc(sem("yT0"), 1)
            act.wait_ge(sem("ctx_nl"), B)
            act_queries(act, "w0")
            either(act, act_attention)
            act.wait_ge(sem("ln_T"), nth("l1") - 1)
            nc.scalar.activation(yT[:, :], bank(0), ACT.Copy).then_inc(sem("yT1"), 1)
            act.wait_ge(sem("lq"), 1)
            nc.scalar.activation(tq[:, 0:TOK], bank(1), ACT.Relu).then_inc(sem("lqs"), 1)
            act.wait_ge(sem("gate_q"), 1)
            nc.scalar.activation(tl[:, 1536:3072], tl[:, 0:1536], ACT.Exp, scale=-1.0).then_inc(sem("fexp"), 1)
            act.wait_ge(sem("x_a2"), 1)
            act_absorb(act, "w1")
            act.wait_ge(sem("ln_T"), nth("l3") - 1)
            nc.scalar.activation(yT[:, :], bank(6), ACT.Copy).then_inc(sem("yT3"), 1)
            act_queries(act, "w1")
            act_attention(act, att1)
            act.wait_ge(sem("ln_T"), nth("l4") - 1)
            nc.scalar.activation(yT[:, :], bank(0), ACT.Copy).then_inc(sem("yT4"), 1)
            act.wait_ge(sem("sqk"), 1)
            nc.scalar.activation(tq[:, 0:512], bank(1), ACT.Identity, bias=vcol[:, 2:3]).then_inc(sem("sqk_s"), 1)
            act.wait_ge(sem("sqk_s"), 1)
            nc.scalar.activation(tq[:, 512:1024], tq[:, 0:512], ACT.Exp, scale=-1.0).then_inc(sem("sqk_e"), 1)
            act.wait_ge(sem("sv"), 1)
            nc.scalar.activation(tl[:, 0:512], bank(2), ACT.Exp, scale=-1.0).then_inc(sem("sv_e"), 1)
            act.wait_ge(sem("z2"), 1)
            nc.scalar.activation(tp[:, 0:512], tp[:, 512:1024], ACT.Exp, scale=-1.0).then_inc(sem("ze"), 1)
            act.wait_ge(sem("ln_T"), nth("l5") - 1)
            nc.scalar.activation(yT[:, :], bank(0), ACT.Copy).then_inc(sem("yT5"), 1)
            for e in range(SELS):
                for c in range(HC):
                    k = e * HC + c
                    if k % 2 == 0:
                        act.wait_ge(sem("hid"), k + 1)
                        if k >= 4:
                            act.wait_ge(sem("hid_used"), k - 3)
                        nc.scalar.activation(tl[:, (k % 4) * HALF:(k % 4 + 1) * HALF], bank(2 + k % 4), ACT.Relu,
                                             bias=vcol[:, 7 + k:8 + k]).then_inc(sem("hid_a"), 1)

        @block.vector
        def _(dve):
            dve_ln(dve, "l0a", xs, (sem("x_in"), 16))
            dve.wait_ge(sem("mask"), 16)
            nc.vector.tensor_scalar(maskb[0:S, 0:KEYS], mask8[:, :], -NEG, NEG, ALU.mult, ALU.add)\
                .then_inc(sem("maskb"), 1)
            nc.vector.tensor_reduce(flag_c[:, :], mask8[:, 0:TAIL0 * P], X, ALU.max).then_inc(sem("flag_c"), 1)
            dve.wait_ge(sem("gp_p"), 1)
            nc.vector.tensor_scalar(gp[:, :], bank(6)[0:1, 0:2 * S], D ** 0.5 * ERF_A, -MU * ERF_A,
                                    ALU.mult, ALU.add).then_inc(sem("gp"), 1)
            dve_ln(dve, "l0b", yn, (sem("ln_rows"), nth("l0a")))
            dve_absorb(dve, "w0")
            for b in range(B):
                for k in range(4):
                    dve.wait_ge(sem("ctx_th"), 4 * b + k + 1)
                    k0, n = k * HALF, min(HALF, KEYS - k * HALF)
                    at = slice(b * KPAD + k0, b * KPAD + k0 + n)
                    nc.vector.tensor_tensor(ctxTl[0:CD, at], bank(k)[0:CD, 0:n], ctxTh[0:CD, at], ALU.subtract)\
                        .then_inc(sem("ctx_tl"), 1)
            dve.wait_ge(sem("flag_T"), 1)
            nc.vector.tensor_reduce(flag_r[:, :], bank(7)[0:1, 256:256 + S], X, ALU.max).then_inc(sem("flag_r"), 1)
            dve.wait_ge(sem("flag_r"), 1)
            nc.vector.tensor_copy(flag_i[:, :], flag_r[:, :]).then_inc(sem("flag"), 1)
            dve_queries(dve, "w0")
            dve.wait_ge(sem("ctx_nl"), B)
            either(dve, dve_attention)
            nc.vector.drain().then_inc(sem("x0_done"), 1)
            dve_residual(dve, "a0", bank(6))
            dve.wait_ge(sem("sT"), 1)
            nc.vector.tensor_copy(qkvT[:, :], bank(2)[:, 0:3 * D]).then_inc(sem("sTs"), 1)
            nc.vector.tensor_copy(projT[:, :], bank(2)[:, 3 * D:4 * D]).then_inc(sem("sTs"), 1)
            dve_ln(dve, "l1", xs, (sem("x_a0"), 1))
            kk = tq[:, 512:1024].rearrange("p (t n) -> p t n", t=TILES)
            vv = tq[:, 1024:1536].rearrange("p (t n) -> p t n", t=TILES)
            for t in range(TILES):
                dve.wait_ge(sem("lkv"), t + 1)
                src = bank(2 + t)
                nc.vector.tensor_scalar(kk[:, t, :], src[:, 0:D], 0.0, None, ALU.max)
                nc.vector.tensor_scalar(vv[:, t, :], src[:, D:2 * D], 0.0, None, ALU.max).then_inc(sem("lkvs"), 1)
            blk = cf[:, C_BLK:C_BLK + P]
            kvm = tq[:, 2048:3072].rearrange("p (b n) -> p b n", b=B)
            ksm = tq[:, 3072:4096].rearrange("p (b n) -> p b n", b=B)
            for odd in range(2):
                dve.wait_ge(sem("kv"), odd + 1)
                src = bank(odd).rearrange("p (b n) -> p b n", b=4)
                nc.vector.tensor_tensor(kvm[:, odd:B:2, :], src, blk.unsqueeze(1).to_broadcast([P, 4, P]), ALU.mult)
                dve.wait_ge(sem("ks"), odd + 1)
                src = bank(2 + odd)[:, 0:4].unsqueeze(2).to_broadcast([P, 4, P])
                nc.vector.tensor_tensor(ksm[:, odd:B:2, :], src, blk.unsqueeze(1).to_broadcast([P, 4, P]), ALU.mult)\
                    .then_inc(sem("kvm"), 1)
            dve.wait_ge(sem("lden"), 1)
            den, rat = tl[:, 0:512], tl[:, 512:1024]
            nc.vector.tensor_scalar(den, bank(5), 1e-15, None, ALU.add).then_inc(sem("den"), 1)
            dve.wait_ge(sem("den"), 1)
            nc.vector.reciprocal(rat, den).then_inc(sem("den"), 1)
            dve.wait_ge(sem("den"), 2)
            nc.vector.tensor_tensor(rat, bank(4), rat, ALU.mult).then_inc(sem("rat"), 1)
            dve_residual(dve, "a1", bank(6))
            w36 = ffraw[:, :, :].rearrange("p g (k n) -> p (g k) n", n=WBLK)
            dve.wait_ge(sem("mid"), 16 * 5)
            nc.vector.tensor_reduce(fsc[:, :], w36, X, ALU.max, apply_absolute_value=True).then_inc(sem("fw"), 1)
            dve.wait_ge(sem("fw"), 1)
            nc.vector.tensor_scalar(fsc[:, :], fsc[:, :], 1.0 / 7.0, 1e-12, ALU.mult, ALU.max).then_inc(sem("fw"), 1)
            dve.wait_ge(sem("fw"), 2)
            nc.vector.reciprocal(fin[:, :], fsc[:, :]).then_inc(sem("fw"), 1)
            dve.wait_ge(sem("fw"), 3)
            nc.vector.tensor_tensor(w36, w36, fin[:, :].unsqueeze(2).to_broadcast([P, 36, WBLK]), ALU.mult)\
                .then_inc(sem("fw"), 1)
            dve.wait_ge(sem("fw"), 4)
            nc.vector.tensor_scalar(w36, w36, MAGIC, -MAGIC, ALU.add, ALU.add).then_inc(sem("fw"), 1)
            dve.wait_ge(sem("fw"), 5)
            nc.vector.tensor_tensor(w36, w36, fsc[:, :].unsqueeze(2).to_broadcast([P, 36, WBLK]), ALU.mult)\
                .then_inc(sem("fw"), 1)
            for k in range(3):
                dve.wait_ge(sem("fwT"), k + 1)
                nc.vector.tensor_copy(ffT[:, 3 * k:3 * k + 3, :],
                                      bank(k)[:, 0:3 * P].rearrange("p (g n) -> p g n", g=3)).then_inc(sem("fwTs"), 1)
            dve_ln(dve, "l2", xs, (sem("x_a1"), 1))
            dve.wait_ge(sem("ln_rows"), nth("l2"))
            y512 = yn[:, :, :].rearrange("p t n -> p (t n)")
            nc.vector.tensor_reduce(gq[:, 0:1], y512, X, ALU.max, apply_absolute_value=True).then_inc(sem("g0"), 1)
            dve_scales(dve, "x", 1, 1)
            dve.wait_ge(sem("ln_T"), nth("l2") - 1)
            nc.vector.tensor_scalar(yT[:, :], bank(6), gq[:, 4:5], MAGIC, ALU.mult, ALU.add).then_inc(sem("fy"), 1)
            dve.wait_ge(sem("fy"), 1)
            nc.vector.tensor_scalar(yT[:, :], yT[:, :], -MAGIC, gq[:, 2:3], ALU.add, ALU.mult).then_inc(sem("fy"), 1)
            gate, up = tl[:, 0:1536], tq[:, 0:1536]
            sg, gs = tq[:, 1536:3072], tl[:, 1536:3072]
            dve.wait_ge(sem("fg"), 3)
            nc.vector.tensor_reduce(gq[:, 0:1], PS[:, 0:1536], X, ALU.max, apply_absolute_value=True)
            dve.wait_ge(sem("fu"), 3)
            nc.vector.tensor_reduce(gq[:, 1:2], PS[:, 1536:3072], X, ALU.max, apply_absolute_value=True)\
                .then_inc(sem("g0"), 1)
            dve_scales(dve, "gu", 2, 2)
            nc.vector.tensor_scalar(gate, PS[:, 0:1536], gq[:, 4:5], MAGIC, ALU.mult, ALU.add).then_inc(sem("gate"), 1)
            dve.wait_ge(sem("gate"), 1)
            nc.vector.tensor_scalar(gate, gate, -MAGIC, gq[:, 2:3], ALU.add, ALU.mult).then_inc(sem("gate_q"), 1)
            nc.vector.tensor_scalar(up, PS[:, 1536:3072], gq[:, 5:6], MAGIC, ALU.mult, ALU.add).then_inc(sem("up"), 1)
            dve.wait_ge(sem("up"), 1)
            nc.vector.tensor_scalar(up, up, -MAGIC, gq[:, 3:4], ALU.add, ALU.mult).then_inc(sem("up_q"), 1)
            dve.wait_ge(sem("fexp"), 1)
            et = tl[:, 1536:3072]
            nc.vector.tensor_scalar(et, et, 1.0, None, ALU.add).then_inc(sem("sg"), 1)
            dve.wait_ge(sem("sg"), 1)
            nc.vector.reciprocal(sg, et).then_inc(sem("sg"), 1)
            dve.wait_ge(sem("sg"), 2)
            nc.vector.tensor_scalar(sg, sg, 65536.0, MAGIC, ALU.mult, ALU.add).then_inc(sem("sg"), 1)
            dve.wait_ge(sem("sg"), 3)
            nc.vector.tensor_scalar(sg, sg, -MAGIC, 65535.0, ALU.add, ALU.min).then_inc(sem("sg"), 1)
            dve.wait_ge(sem("sg"), 4)
            nc.vector.scalar_tensor_tensor(gs, sg, 2.0 ** -16, gate, ALU.mult, ALU.mult).then_inc(sem("sg"), 1)
            dve.wait_ge(sem("sg"), 5)
            nc.vector.tensor_reduce(gq[:, 0:1], gs, X, ALU.max, apply_absolute_value=True).then_inc(sem("g0"), 1)
            dve_scales(dve, "gs", 1, 3)
            nc.vector.tensor_scalar(gs, gs, gq[:, 4:5], MAGIC, ALU.mult, ALU.add).then_inc(sem("sg"), 1)
            dve.wait_ge(sem("sg"), 6)
            nc.vector.tensor_scalar(gs, gs, -MAGIC, gq[:, 2:3], ALU.add, ALU.mult).then_inc(sem("sg"), 1)
            dve.wait_ge(sem("sg"), 7)
            nc.vector.tensor_tensor(gs, gs, up, ALU.mult).then_inc(sem("sg"), 1)
            dve.wait_ge(sem("sg"), 8)
            nc.vector.tensor_reduce(gq[:, 0:1], gs, X, ALU.max, apply_absolute_value=True).then_inc(sem("g0"), 1)
            dve_scales(dve, "o", 1, 4)
            nc.vector.tensor_scalar(gs, gs, gq[:, 4:5], MAGIC, ALU.mult, ALU.add).then_inc(sem("sg"), 1)
            dve.wait_ge(sem("sg"), 9)
            nc.vector.tensor_scalar(gs, gs, -MAGIC, gq[:, 2:3], ALU.add, ALU.mult).then_inc(sem("fo"), 1)
            dve_residual(dve, "a2", bank(6))
            dve_ln(dve, "l3", xs, (sem("x_a2"), 1))
            dve_absorb(dve, "w1")
            dve_queries(dve, "w1")
            dve_attention(dve, att1)
            nc.vector.drain().then_inc(sem("x1_done"), 1)
            dve_residual(dve, "a3", bank(6))
            dve_ln(dve, "l4", xs, (sem("x_a3"), 1))
            dve.wait_ge(sem("biasT"), 1)
            for i in range(2):
                nc.vector.tensor_copy(biasz[:, i * S:(i + 1) * S], bank(7)[:, 0:S]).then_inc(sem("biasz"), 1)
            lin, ex = tq[:, 0:512], tq[:, 512:1024]
            dve.wait_ge(sem("sqk_e"), 1)
            nc.vector.tensor_scalar(ex, ex, 1.0, None, ALU.add).then_inc(sem("sw"), 1)
            dve.wait_ge(sem("sw"), 1)
            nc.vector.reciprocal(ex, ex).then_inc(sem("sw"), 1)
            dve.wait_ge(sem("sw"), 2)
            nc.vector.tensor_tensor(lin, lin, ex, ALU.mult).then_inc(sem("sw"), 1)
            dve.wait_ge(sem("sw"), 3)
            qT, kT = tq[:, 1024:1536], tq[:, 1536:2048]
            nc.vector.tensor_scalar(qT, lin, vcol[:, 3:4], vcol[:, 5:6], ALU.mult, ALU.add)
            nc.vector.tensor_scalar(kT, lin, vcol[:, 4:5], vcol[:, 6:7], ALU.mult, ALU.add).then_inc(sem("sqks"), 1)
            ev, vr = tl[:, 0:512], tl[:, 512:1024]
            dve.wait_ge(sem("sv_e"), 1)
            nc.vector.tensor_scalar(ev, ev, 1.0, None, ALU.add).then_inc(sem("sx"), 1)
            dve.wait_ge(sem("sx"), 1)
            nc.vector.reciprocal(ev, ev).then_inc(sem("sx"), 1)
            dve.wait_ge(sem("sx"), 2)
            nc.vector.tensor_tensor(vr, bank(2), ev, ALU.mult).then_inc(sem("svr"), 1)
            z, z2 = tl[:, 1024:1536], tp[:, 512:1024]
            az, tt, acc = tl[:, 1536:2048], tl[:, 2048:2560], tl[:, 2560:3072]
            dve.wait_ge(sem("sim"), 1)
            dve.wait_ge(sem("biasz"), 2)
            nc.vector.scalar_tensor_tensor(
                z.rearrange("p (t n) -> p t n", t=TILES), bank(3).rearrange("p (t n) -> p t n", t=TILES),
                ERF_A / S, biasz[:, :].unsqueeze(1).to_broadcast([P, TILES, P]), ALU.mult, ALU.add)\
                .then_inc(sem("z"), 1)
            dve.wait_ge(sem("z"), 1)
            nc.vector.tensor_tensor(z2, z, z, ALU.mult).then_inc(sem("z2"), 1)
            nc.vector.scalar_tensor_tensor(az, z, -1.0, z, ALU.mult, ALU.max).then_inc(sem("z"), 1)
            dve.wait_ge(sem("z"), 2)
            nc.vector.tensor_scalar(az, az, ERF_P, 1.0, ALU.mult, ALU.add).then_inc(sem("z"), 1)
            dve.wait_ge(sem("z"), 3)
            nc.vector.reciprocal(tt, az).then_inc(sem("z"), 1)
            dve.wait_ge(sem("z"), 4)
            nc.vector.tensor_scalar(acc, tt, ERF_C[4], None, ALU.mult).then_inc(sem("z"), 1)
            for i in range(4):
                dve.wait_ge(sem("z"), 5 + i)
                nc.vector.scalar_tensor_tensor(acc, acc, ERF_C[3 - i], tt, ALU.add, ALU.mult).then_inc(sem("z"), 1)
            dve.wait_ge(sem("z"), 9)
            dve.wait_ge(sem("ze"), 1)
            nc.vector.scalar_tensor_tensor(acc, acc, 0.5, tp[:, 0:512], ALU.mult, ALU.mult).then_inc(sem("z"), 1)
            nc.vector.tensor_scalar(az, z, 0.0, -2.0, ALU.is_ge, ALU.mult).then_inc(sem("z"), 1)
            dve.wait_ge(sem("z"), 11)
            nc.vector.scalar_tensor_tensor(acc, az, 1.0, acc, ALU.add, ALU.mult).then_inc(sem("z"), 1)
            dve.wait_ge(sem("z"), 12)
            nc.vector.scalar_tensor_tensor(acc, az, -0.5, acc, ALU.mult, ALU.add).then_inc(sem("z"), 1)
            dve.wait_ge(sem("z"), 13)
            acc3 = acc.rearrange("p (t n) -> p t n", t=TILES)
            nc.vector.tensor_tensor(acc3, acc3, cf[:, C_CAUSAL:C_CAUSAL + P].unsqueeze(1).to_broadcast([P, TILES, P]),
                                    ALU.mult).then_inc(sem("attn"), 1)
            dve_residual(dve, "a4", bank(6))
            dve_ln(dve, "l5", xs, (sem("x_a4"), 1))
            lg = tp[:, 0:32].rearrange("p (t e) -> p t e", e=EXPERTS)
            sc8 = tp[:, 32:64].rearrange("p (t e) -> p t e", e=EXPERTS)
            top = tp[:, 64:68]
            oh = tp[:, 68:100].rearrange("p (t e) -> p t e", e=EXPERTS)
            sel = tp[:, 100:136].rearrange("p (t e) -> p t e", e=SELS)
            oh16 = Pl[:, 0:32]
            sel16 = Pl[:, 32:32 + 4 * SELS]
            lp = bank(1)[:, 0:32].rearrange("p (t e) -> p t e", e=EXPERTS)
            dve.wait_ge(sem("rlog"), 1)
            nc.vector.tensor_reduce(top, lp, X, ALU.max).then_inc(sem("r"), 1)
            dve.wait_ge(sem("r"), 1)
            nc.vector.tensor_tensor(lg, lp, top.unsqueeze(2).to_broadcast([P, TILES, EXPERTS]), ALU.is_ge)\
                .then_inc(sem("r"), 1)
            dve.wait_ge(sem("r"), 2)
            nc.vector.tensor_tensor(sc8, lg, cf[:, C_FIRST:C_FIRST + EXPERTS].unsqueeze(1).to_broadcast(
                [P, TILES, EXPERTS]), ALU.mult).then_inc(sem("r"), 1)
            dve.wait_ge(sem("r"), 3)
            nc.vector.tensor_reduce(top, sc8, X, ALU.max).then_inc(sem("r"), 1)
            dve.wait_ge(sem("r"), 4)
            nc.vector.tensor_tensor(oh, sc8, top.unsqueeze(2).to_broadcast([P, TILES, EXPERTS]), ALU.is_equal)\
                .then_inc(sem("r"), 1)
            dve.wait_ge(sem("r"), 5)
            nc.vector.tensor_copy(oh16.rearrange("p (t e) -> p t e", e=EXPERTS), oh).then_inc(sem("oh"), 1)
            dve.wait_ge(sem("rank"), 1)
            rk = bank(2)[:, 0:32].rearrange("p (t e) -> p t e", e=EXPERTS)
            nc.vector.scalar_tensor_tensor(sel[:, :, 0:EXPERTS], rk, float(CAP), oh, ALU.is_le, ALU.mult)\
                .then_inc(sem("r"), 1)
            dve.wait_ge(sem("r"), 6)
            nc.vector.tensor_reduce(top, sel[:, :, 0:EXPERTS], X, ALU.add).then_inc(sem("r"), 1)
            dve.wait_ge(sem("r"), 7)
            nc.vector.tensor_scalar(sel[:, :, EXPERTS], top, -1.0, 1.0, ALU.mult, ALU.add).then_inc(sem("r"), 1)
            dve.wait_ge(sem("r"), 8)
            nc.vector.tensor_copy(sel16.rearrange("p (t e) -> p t e", e=SELS), sel).then_inc(sem("sel"), 1)
            dve.wait_ge(sem("selT"), 1)
            sT = bank(3).bitcast(F16)[0:SELS, 0:TOK]
            nc.vector.tensor_scalar(tq[0:SELS, 0:TOK], sT, 1.0, None, ALU.mult).then_inc(sem("selT_s"), 1)
            nc.vector.tensor_scalar(Ph[0:SELS, 2 * 512:2 * 512 + TOK], sT, -NEG, NEG, ALU.mult, ALU.add)\
                .then_inc(sem("selT_s"), 1)
            for k in range(SELS * HC):
                if k % 2 == 1:
                    dve.wait_ge(sem("hid"), k + 1)
                    if k >= 4:
                        dve.wait_ge(sem("hid_used"), k - 3)
                    nc.vector.tensor_scalar(tl[:, (k % 4) * HALF:(k % 4 + 1) * HALF], bank(2 + k % 4),
                                            vcol[:, 7 + k:8 + k], 0.0, ALU.add, ALU.max).then_inc(sem("hid_d"), 1)
            dve_residual(dve, "a5", bank(6))

        @block.tensor
        def _(pe):
            pe.wait_ge(sem("consts"), 32)
            pe.wait_ge(sem("vecs"), 8 * 16)
            nc.tensor.matmul(bank(6)[0:1, 0:2 * S], emb[:, :], cf[0:BUCKETS, C_ONEHOT:C_ONEHOT + 2 * S],
                             start=True, stop=True).then_inc(sem("gp_p"), 1)
            nc.tensor.transpose(bank(7)[:, 0:43], vecs[0:43, :], ident[0:43, 0:43]).then_inc(sem("vT"), 1)
            pe.wait_ge(sem("w0_w"), 64)
            pe.wait_ge(sem("vcol"), 1)
            pe.wait_ge(sem("gp"), 1)
            pe_absorb(pe, "w0")
            pe.wait_ge(sem("wTs"), 6 * 0 + 6)
            for b in range(B):
                pe.wait_ge(sem(f"ctx{b % NR}"), 32 * (b // NR + 1))
                for k in range(4):
                    if b:
                        pe.wait_ge(sem("ctx_tl"), 4 * (b - 1) + k + 1)
                    for c in range(4 * k, min(4 * k + 4, NCH)):
                        _, n = chunk(c)
                        o = (c - 4 * k) * P
                        ins = nc.tensor.transpose(bank(k)[0:CD, o:o + n], ring[0:n, b % NR, c, :], ident[0:n, 0:n])
                    ins.then_inc(sem("ctx_tp"), 1)
            pe.wait_ge(sem("abs"), 8 * 0 + 8)
            pe.wait_ge(sem("flag_c"), 1)
            nc.tensor.transpose(bank(7)[0:1, 256:256 + S], flag_c[:, :], ident[0:S, 0:S]).then_inc(sem("flag_T"), 1)
            pe.wait_ge(sem("ln_rows"), nth("l0b"))
            pe_rows_T(pe, yn, bank(6), sem("ln_T"))
            pe.wait_ge(sem("ctx_tl"), 4 * B)
            pe_queries(pe, "w0", (sem("yT0"), 1))
            pe.wait_ge(sem("ql"), 16 * 0 + HEADS)
            pe.wait_ge(sem("ctx_nl"), B)
            pe.wait_ge(sem("ones_col"), 2)
            pe.wait_ge(sem("ones_rows"), 1)
            pe.wait_ge(sem("maskz"), 1)
            pe.wait_ge(sem("maskb"), 1)
            pe.wait_ge(sem("flag"), 1)
            either(pe, pe_attention)
            pe.wait_ge(sem("x0_done"), 1)
            pe.wait_ge(sem("small"), 16 * 10)
            pe_heads_out(pe, "a0", att0, rows1[:, 0:D], bank(6))
            pe.wait_ge(sem("mid"), 16 * 5)
            pe_rows_T(pe, sraw, bank(2), sem("sT"))
            pe.wait_ge(sem("ln_rows"), nth("l1"))
            pe_rows_T(pe, yn, bank(0), sem("ln_T"))
            pe.wait_ge(sem("yT1"), 1)
            pe.wait_ge(sem("sTs"), 2)
            nc.tensor.matmul(bank(1), qkvT[:, 0:D], yT[:, :], start=True, stop=True).then_inc(sem("lq"), 1)
            for t in range(TILES):
                nc.tensor.matmul(bank(2 + t)[:, 0:2 * D], yT[:, t * P:(t + 1) * P], qkvT[:, D:3 * D],
                                 start=True, stop=True).then_inc(sem("lkv"), 1)
            kk = tq[:, 512:1024].rearrange("p (t n) -> p t n", t=TILES)
            vv = tq[:, 1024:1536].rearrange("p (t n) -> p t n", t=TILES)
            kvm = tq[:, 2048:3072].rearrange("p (b n) -> p b n", b=B)
            ksm = tq[:, 3072:4096].rearrange("p (b n) -> p b n", b=B)
            pe.wait_ge(sem("lkvs"), TILES)
            pe.wait_ge(sem("lqs"), 1)
            for odd in range(2):
                r = slice(S * odd, S * odd + S)
                for t in range(TILES):
                    ins = nc.tensor.matmul(bank(odd)[:, t * P:(t + 1) * P], kk[r, t, :], vv[r, t, :],
                                           start=True, stop=True)
                ins.then_inc(sem("kv"), 1)
                for t in range(TILES):
                    ins = nc.tensor.matmul(bank(2 + odd)[:, t:t + 1], kk[r, t, :], cf[r, C_ONE:C_ONE + 1],
                                           start=True, stop=True)
                ins.then_inc(sem("ks"), 1)
            pe.wait_ge(sem("kvm"), 2)
            for b in range(B):
                q = tq[:, b * S:(b + 1) * S]
                nc.tensor.matmul(bank(4)[:, b * S:(b + 1) * S], kvm[:, b, :], q, start=True, stop=True)
                ins = nc.tensor.matmul(bank(5)[:, b * S:(b + 1) * S], ksm[:, b, :], q, start=True, stop=True)
            ins.then_inc(sem("lden"), 1)
            pe.wait_ge(sem("rat"), 1)
            for t in range(TILES):
                o = bank(6)[:, t * P:(t + 1) * P]
                nc.tensor.matmul(o, tl[:, 512 + t * P:512 + (t + 1) * P], projT[:, :], start=True, stop=False)
                ins = nc.tensor.matmul(o, ones1, rows1[:, D:2 * D], start=False, stop=True)
            ins.then_inc(sem("a1_y"), 1)
            pe.wait_ge(sem("fw"), 6)
            for k in range(3):
                for g in range(3):
                    ins = nc.tensor.transpose(bank(k)[:, g * P:(g + 1) * P], ffraw[:, 3 * k + g, :], ident)
                ins.then_inc(sem("fwT"), 1)
            pe.wait_ge(sem("ln_rows"), nth("l2"))
            pe_rows_T(pe, yn, bank(6), sem("ln_T"))
            pe_scales(pe, 1, 1)
            pe.wait_ge(sem("fy"), 2)
            pe.wait_ge(sem("fwTs"), 3)
            for k in range(3):
                nc.tensor.matmul(bank(k), ffT[:, k, :], yT[:, :], start=True, stop=True).then_inc(sem("fg"), 1)
            for k in range(3):
                nc.tensor.matmul(bank(3 + k), ffT[:, 3 + k, :], yT[:, :], start=True, stop=True).then_inc(sem("fu"), 1)
            pe_scales(pe, 2, 2)
            pe_scales(pe, 1, 3)
            pe_scales(pe, 1, 4)
            pe.wait_ge(sem("fo"), 1)
            gs = tl[:, 1536:3072]
            for t in range(TILES):
                for k in range(FC):
                    ins = nc.tensor.matmul(bank(6)[:, t * P:(t + 1) * P], gs[:, k * TOK + t * P:k * TOK + (t + 1) * P],
                                           ffT[:, 6 + k, :], start=(k == 0), stop=(k == FC - 1))
            ins.then_inc(sem("a2_y"), 1)
            pe.wait_ge(sem("w1_w"), 64)
            pe.wait_ge(sem("x_a2"), 1)
            pe_absorb(pe, "w1")
            pe.wait_ge(sem("abs"), 8 * 1 + 8)
            pe.wait_ge(sem("ln_rows"), nth("l3"))
            pe_rows_T(pe, yn, bank(6), sem("ln_T"))
            pe_queries(pe, "w1", (sem("yT3"), 1))
            pe.wait_ge(sem("ql"), 16 * 1 + HEADS)
            pe_attention(pe, att1)
            pe.wait_ge(sem("x1_done"), 1)
            pe_heads_out(pe, "a3", att1, rows1[:, 2 * D:3 * D], bank(6))
            pe.wait_ge(sem("ln_rows"), nth("l4"))
            pe_rows_T(pe, yn, bank(0), sem("ln_T"))
            pe.wait_ge(sem("hank"), 16)
            nc.tensor.matmul(bank(7)[:, 0:S], cf[0:S, C_FLIP:C_FLIP + P], hank[:, :], start=True, stop=True)\
                .then_inc(sem("biasT"), 1)
            pe.wait_ge(sem("yT4"), 1)
            nc.tensor.matmul(bank(1), wqk1[:, 0, :], yT[:, :], start=True, stop=True).then_inc(sem("sqk"), 1)
            for t in range(TILES):
                o = bank(2)[:, t * P:(t + 1) * P]
                nc.tensor.matmul(o, yT[:, t * P:(t + 1) * P], wqk1[:, 1, :], start=True, stop=False)
                ins = nc.tensor.matmul(o, ones1, rows1[:, 3 * D:4 * D], start=False, stop=True)
            ins.then_inc(sem("sv"), 1)
            pe.wait_ge(sem("sqks"), 1)
            for t in range(TILES):
                c = slice(t * P, (t + 1) * P)
                ins = nc.tensor.matmul(bank(3)[:, c], tq[:, 1536 + t * P:1536 + (t + 1) * P],
                                       tq[:, 1024 + t * P:1024 + (t + 1) * P], start=True, stop=True)
            ins.then_inc(sem("sim"), 1)
            pe.wait_ge(sem("attn"), 1)
            pe.wait_ge(sem("svr"), 1)
            for t in range(TILES):
                ins = nc.tensor.matmul(bank(6)[:, t * P:(t + 1) * P], tl[:, 2560 + t * P:2560 + (t + 1) * P],
                                       tl[:, 512 + t * P:512 + (t + 1) * P], start=True, stop=True)
            ins.then_inc(sem("a4_y"), 1)
            pe.wait_ge(sem("ln_rows"), nth("l5"))
            pe_rows_T(pe, yn, bank(0), sem("ln_T"))
            pe.wait_ge(sem("yT5"), 1)
            for t in range(TILES):
                o = bank(1)[:, t * EXPERTS:(t + 1) * EXPERTS]
                nc.tensor.matmul(o, yT[:, t * P:(t + 1) * P], rw[:, :], start=True, stop=False)
                ins = nc.tensor.matmul(o, ones1, rb[:, :], start=False, stop=True)
            ins.then_inc(sem("rlog"), 1)
            pe.wait_ge(sem("oh"), 1)
            for t in range(TILES):
                o = bank(2)[:, t * EXPERTS:(t + 1) * EXPERTS]
                for u in range(t):
                    nc.tensor.matmul(o, ch[:, H_ONES:H_ONES + P], Pl[:, u * EXPERTS:(u + 1) * EXPERTS],
                                     start=(u == 0), stop=False)
                ins = nc.tensor.matmul(o, ch[:, H_TRI:H_TRI + P], Pl[:, t * EXPERTS:(t + 1) * EXPERTS],
                                       start=(t == 0), stop=True)
            ins.then_inc(sem("rank"), 1)
            pe.wait_ge(sem("sel"), 1)
            for t in range(TILES):
                ins = nc.tensor.transpose(bank(3).bitcast(F16)[0:SELS, t * P:(t + 1) * P],
                                          Pl[:, 32 + t * SELS:32 + (t + 1) * SELS], ident16)
            ins.then_inc(sem("selT"), 1)
            pe.wait_ge(sem("selT_s"), 2)
            pe.wait_ge(sem("x_a4"), 1)

            def expert_out(k):
                e, c = divmod(k, HC)
                if k % 2 == 0:
                    pe.wait_ge(sem("hid_a"), k // 2 + 1)
                else:
                    pe.wait_ge(sem("hid_d"), k // 2 + 1)
                for t in range(TILES):
                    at = (k % 4) * HALF + t * P
                    ins = nc.tensor.matmul(bank(6)[:, t * P:(t + 1) * P], tl[:, at:at + P], w2[:, e, c, :],
                                           start=False, stop=(k == SELS * HC - 1), skip_group_check=True)
                ins.then_inc(sem("hid_used"), 1)
                return ins

            for t in range(TILES):
                nc.tensor.matmul(bank(6)[:, t * P:(t + 1) * P], tq[0:SELS, t * P:(t + 1) * P], b2r[:, :],
                                 start=(t == 0), stop=False, skip_group_check=True)
            for k in range(SELS * HC):
                e, c = divmod(k, HC)
                if c == 0:
                    pe.wait_ge(sem(f"ex{e}"), 32)
                if k >= 4:
                    if k % 2 == 0:
                        pe.wait_ge(sem("hid_a"), (k - 4) // 2 + 1)
                    else:
                        pe.wait_ge(sem("hid_d"), (k - 4) // 2 + 1)
                o = bank(2 + k % 4)
                nc.tensor.matmul(o, ch[0:SELS, H_ROW + e * P:H_ROW + (e + 1) * P], Ph[0:SELS, 1024:1024 + TOK],
                                 start=True, stop=False)
                nc.tensor.matmul(o, w1[:, e, c * P:(c + 1) * P], yT[:, :], start=False, stop=True)\
                    .then_inc(sem("hid"), 1)
                if k >= 2:
                    expert_out(k - 2)
            expert_out(SELS * HC - 2)
            ins = expert_out(SELS * HC - 1)
            pe.wait_ge(sem("hid_used"), SELS * HC)
            nc.tensor.matmul(bank(7)[0:1, 0:1], ones1[:, 0:1], ones1[:, 0:1], start=True, stop=True)\
                .then_inc(sem("a5_y"), 1)


_INS = ['x', 'ctx_768', 'mask_1x1xSxS2_bk0', 'L0_xattn_ln_gamma', 'L0_xattn_ln_beta', 'L0_xattn_Wq',
        'L0_xattn_Wkv', 'L0_xattn_Wo', 'L0_xattn_bo', 'L0_attn_qkv_weight', 'L0_attn_proj_weight',
        'L0_attn_proj_bias', 'L0_ffn_w_gate', 'L0_ffn_w_up', 'L0_ffn_w_down', 'L1_xattn_Wq', 'L1_xattn_Wk',
        'L1_xattn_Wv', 'L1_xattn_Wo', 'L1_xattn_bo', 'L1_attn_Wqk', 'L1_attn_bqk', 'L1_attn_gamma',
        'L1_attn_beta', 'L1_attn_Wv', 'L1_attn_bv', 'L1_attn_rel_emb', 'L1_ffn_router_w', 'L1_ffn_router_b',
        'L1_ffn_w1', 'L1_ffn_b1', 'L1_ffn_w2', 'L1_ffn_b2', 'L1_ffn_ow1', 'L1_ffn_ob1', 'L1_ffn_ow2',
        'L1_ffn_ob2']


def kernel(**inputs):
    import numpy as _np
    import concourse.bacc as _bacc
    from concourse import mybir as _mybir
    from concourse.bass_utils import run_bass_kernel_spmd as _run

    nc = _bacc.Bacc("TRN2", target_bir_lowering=False, num_devices=1)
    arrays, args = {}, {}
    c, h = constants()
    given = {n: _np.ascontiguousarray(inputs[n]) for n in _INS} | {"cf": c, "ch": h}
    for name, v in given.items():
        arrays[f"in_{name}_dram"] = v
        args[name] = nc.dram_tensor(f"in_{name}_dram", v.shape, _mybir.dt.from_np(v.dtype),
                                    kind="ExternalInput").ap()
    o = nc.dram_tensor("out_0_dram", (B, S, D), F32, kind="ExternalOutput").ap()
    perceiver(nc, args, o)
    r = _run(nc, [arrays], core_ids=[0])
    return r.results[0]["out_0_dram"]
```

```python
from contextlib import ExitStack

import numpy as np

import concourse.bass as bass
from concourse import mybir

F32 = mybir.dt.float32
F16 = mybir.dt.float16
U8 = mybir.dt.uint8
I32 = mybir.dt.int32
ALU = mybir.AluOpType
ACT = mybir.ActivationFunctionType
X = mybir.AxisListType.X

P = 128
B, S, D = 8, 64, 128
TOK = B * S
TILES = TOK // P
KEYS, CD = 1601, 96
HEADS, DH = 16, 64
ROWS = HEADS * S
BLOCKS = ROWS // P
HALF = 512
KPAD = 1602
NCH = -(-KEYS // P)
CPAD = CD + 2
SHIFT = CD
NSH = BLOCKS
KS = CD + NSH
TAIL0 = 9
TAILS = NCH - TAIL0
GROUP = 3
GROUPS = TAIL0 // GROUP
LAST = KEYS - (NCH - 1) * P
FF = 384
FC = FF // P
WBLK = 32
EXPERTS, CAP, HID = 8, 160, 512
HC = HID // P
SELS = EXPERTS + 1
NEG = -60000.0
BIG = 32768.0
MAGIC = 12582912.0
LN_EPS = 1e-5
BUCKETS, MAXD = 32, 128
MU = float(np.sqrt(0.5))
ERF_A = 1.0 / float(np.sqrt(0.25 * np.pi) * np.sqrt(2.0))
ERF_P = 0.3275911
ERF_C = (0.254829592, -0.284496736, 1.421413741, -1.453152027, 1.061405429)

C_ID, C_BLK, C_CAUSAL, C_NDELTA, C_FIRST, C_ONE, C_ONEHOT, C_FLIP = np.cumsum(
    [0, 128, 128, 128, 8, 8, 128, 128]).tolist()
C_END = C_FLIP + 128
H_ID, H_ONES, H_TRI, H_IND, H_ROW = np.cumsum([0, 128, 128, 128, 512]).tolist()
H_END = H_ROW + SELS * 128


def constants():
    c = np.zeros((P, C_END), np.float32)
    h = np.zeros((P, H_END), np.float16)
    i = np.arange(P)
    c[:, C_ID:C_ID + P] = np.eye(P)
    c[:, C_BLK:C_BLK + P] = i[:, None] // 4 == i[None] // 4
    key, query = i[:, None], i[None]
    c[:, C_CAUSAL:C_CAUSAL + P] = (key // S == query // S) & (key <= query)
    c[SHIFT:SHIFT + NSH, C_NDELTA:C_NDELTA + NSH] = -np.eye(NSH)
    c[:, C_FIRST:C_FIRST + EXPERTS] = EXPERTS - np.arange(EXPERTS)
    c[:, C_ONE:C_ONE + P] = 1.0
    n = np.maximum(np.arange(2 * S) - (S - 1), 0)
    exact = BUCKETS // 2
    large = exact + (np.log(np.maximum(n, 1).astype(np.float32) / exact) / np.log(MAXD / exact)
                     * (BUCKETS - exact)).astype(np.int32)
    bucket = np.where(n < exact, n, np.minimum(large, BUCKETS - 1))
    c[:BUCKETS, C_ONEHOT:C_ONEHOT + 2 * S] = np.arange(BUCKETS)[:, None] == bucket[None]
    c[:S, C_FLIP:C_FLIP + P] = np.arange(S)[:, None] == S - 1 - i[None] % S
    h[:, H_ID:H_ID + P] = np.eye(P)
    h[:, H_ONES:H_ONES + P] = 1.0
    h[:, H_TRI:H_TRI + P] = i[:, None] <= i[None]
    h[:S, H_IND:H_IND + HALF] = (np.arange(HALF)[None] % S == np.arange(S)[:, None]) * BIG
    for e in range(SELS):
        h[e, H_ROW + e * P:H_ROW + (e + 1) * P] = BIG
    return c, h


def chunk(c):
    return c * P, min(P, KEYS - c * P)


def slices(lo, hi, most=HALF):
    n = -(-(hi - lo) // most)
    cuts = [lo + (hi - lo) * i // n for i in range(n + 1)]
    return [(a, b - a) for a, b in zip(cuts, cuts[1:])]


def perceiver(nc, a, out):
    ctx = ExitStack()
    with ctx:
        def sb(name, shape, dt=F32):
            return ctx.enter_context(nc.sbuf_tensor(name, shape, dt))

        sems = {}

        def sem(name):
            if name not in sems:
                sems[name] = ctx.enter_context(nc.semaphore(name))
            return sems[name]

        ctxTh = sb("ctxTh", [P, B * KPAD], F16)
        ctxTl = sb("ctxTl", [P, B * KPAD], F16)
        ctxNh = sb("ctxNh", [P, B * NCH * CPAD], F16)
        ctxNl = sb("ctxNl", [P, B * NCH * CPAD], F16)
        Qh = sb("Qh", [P, B * ROWS], F16)
        Ql = sb("Ql", [P, B * ROWS], F16)
        maskb = sb("maskb", [P, KPAD], F16)
        pool32 = sb("pool32", [P, 11 * 1024])
        P32 = pool32[:, 0:2048]
        rawO = pool32[:, 2048:3072]
        Ph = sb("Ph", [P, 2 * ROWS], F16)
        Pl = sb("Pl", [P, 2 * ROWS], F16)
        On = pool32[:, 3072:3072 + HEADS * TOK].rearrange("p (b h s) -> p b h s", b=B, h=HEADS)
        wraw = pool32[:, 3072:]
        Wq = wraw[:, 0:1024]
        Wk = wraw[:, 1024:2048]
        Wv = wraw[:, 2048:3072]
        Wo = wraw[:, 3072:4096].rearrange("p (g n) -> p g n", g=8)
        WqT = wraw[:, 4096:5120].rearrange("p (g n) -> p g n", g=8)
        WkT = wraw[:, 5120:5120 + 8 * CD].rearrange("p (g n) -> p g n", g=8)
        WvT = wraw[:, 6144:6144 + 8 * CD].rearrange("p (g n) -> p g n", g=8)
        tail_raw = pool32[:, 0:B * TAILS * CD].rearrange("p (b c d) -> p b c d", b=B, c=TAILS)
        head_raw = [pool32[:, 3072 + (B - 2 + r) * ROWS:3072 + (B - 2 + r) * ROWS + TAIL0 * CD]
                    .rearrange("p (c d) -> p c d", c=TAIL0) for r in range(2)]
        Ah = wraw[:, 0:HEADS * CD].rearrange("p (h n) -> p h n", h=HEADS)
        Bh = sb("Bh", [P, HEADS, D])
        xs = sb("xs", [P, TILES, D])
        rows = sb("rows", [P, 2 * TOK])
        yn = rows[:, 0:TOK].rearrange("p (t n) -> p t n", t=TILES)
        yT = rows[:, TOK:2 * TOK]
        cf = sb("cf", [P, C_END])
        ch = sb("ch", [P, H_END], F16)
        vecs = sb("vecs", [64, D])
        vcol = sb("vcol", [P, 64])
        ghalf = sb("ghalf", [P, 2])
        rows1 = sb("rows1", [1, 2 * D])
        mask8 = Pl[0:S, :].bitcast(U8)[:, 0:KEYS]
        st = sb("st", [P, TILES, 6])
        mv = sb("mv", [P, TILES, 2])
        ve = sb("ve", [P, TILES])
        mhalf = sb("mhalf", [P, TILES])
        rstd = sb("rstd", [P, TILES])
        mx = sb("mx", [P, BLOCKS * 4])
        m8 = sb("m8", [P, BLOCKS])
        rcol = sb("rcol", [P, BLOCKS])
        diag = rows
        m16 = sb("m16", [P, BLOCKS], F16)
        qkvT = P32[:, 1152:1536]
        projT = P32[:, 1536:1664]
        ffraw = wraw[:, 6912:8064].rearrange("p (g n) -> p g n", n=P)
        ffT = P32[:, 0:1152].rearrange("p (g n) -> p g n", n=P)
        fsc = sb("fsc", [P, 36])
        fin = sb("fin", [P, 36])
        sraw = rawO[:, 0:512].rearrange("p (g n) -> p g n", n=P)
        wqk1 = sb("wqk1", [P, 2, D])
        rw = sb("rw", [P, EXPERTS])
        rb = sb("rb", [1, EXPERTS])
        b2r = sb("b2r", [SELS, D])
        emb = sb("emb", [BUCKETS, 1])
        gp = sb("gp", [1, 2 * S])
        hank = sb("hank", [S, S])
        biasz = sb("biasz", [P, P])
        gq = sb("gq", [P, 8])
        gr = sb("gr", [2, 8])
        tq = Qh[:, :].bitcast(F32)
        tl = Ql[:, :].bitcast(F32)
        tp = Ph[:, :].bitcast(F32)
        w1 = ctxTh[:, 0:2 * SELS * HID].bitcast(F32).rearrange("p (e n) -> p e n", e=SELS)
        w2 = ctxTl[:, 0:2 * SELS * HID].bitcast(F32).rearrange("p (e c n) -> p e c n", e=SELS, c=HC)
        scratch = nc.dram_tensor("bias_row", (2 * S,), F32, kind="Internal").ap()

        PS = ctx.enter_context(nc.psum_tensor("PS", [P, 8 * HALF], F32))
        PO = PS[:, 2048:3072]

        def bank(k):
            return PS[:, k * HALF:(k + 1) * HALF]

        MISC = [bank(6), bank(7)]
        ident = cf[:, C_ID:C_ID + P]
        ident16 = ch[:, H_ID:H_ID + P]
        ones1 = cf[0:1, C_ONE:C_ONE + P]

        block = ctx.enter_context(nc.Block())

        class Att:

            def __init__(self, name, chunks, masked):
                self.name, self.chunks, self.masked = name, chunks, masked
                self.n = len(chunks)
                self.slices = slices(chunks[0] * P, KEYS)
                self.units = BLOCKS * len(self.slices)
                self.prep = GROUPS if self.n < NCH else 0
                if self.prep:
                    self.per = [self.units] + [0] * (self.n - 1)
                    self.recip_slot, self.norm_slot, self.shift_slot = 1, 2, 1
                else:
                    slots = self.n - 4
                    self.per = [self.units * (s + 1) // slots - self.units * s // slots if s < slots else 0
                                for s in range(self.n)]
                    self.recip_slot, self.norm_slot, self.shift_slot = 1, 3, self.n - 3

            def extras(self, i, last):
                before = sum(self.per[:i])
                most = [] if last else [("max", u) for u in range(before, before + self.per[i])]
                return most + ([("prep", i - 1)] if self.prep and i else [])

            def max_used(self, i, first):
                used = 0
                for k in range(i):
                    used += 0 if first else 2 * (k == self.recip_slot) + 2 * (k == self.norm_slot)
                    used += len(self.extras(k, False))
                return used

            def sem(self, what):
                return sem(f"{self.name}_{what}")

            def base(self, b):
                first = self.units + 1
                if isinstance(b, int) and b == 0:
                    return first
                return 2 * first + self.prep + (b - 1) * (first + 4 + self.prep)

        def pe_max_unit(pe, t, nb, u, full_wait, spare):
            j, s = divmod(u, len(t.slices))
            k0, n = t.slices[s]
            if full_wait is not None:
                pe.wait_ge(t.sem("spare_read"), full_wait)
            o = spare[:, 0:n]
            ins = nc.tensor.matmul(o, Qh[0:CD, bass.ds(nb * ROWS + j * P, P)],
                                   ctxTh[0:CD, bass.ds(nb * KPAD + k0, n)], start=True, stop=not t.masked)
            if t.masked:
                ins = nc.tensor.matmul(o, ch[:, H_IND:H_IND + P], maskb[:, k0:k0 + n], start=False, stop=True)
            ins.then_inc(t.sem("spare_written"), 1)

        def pe_shift(pe, t, nb, full_wait, spare):
            pe.wait_ge(t.sem("max_ready"), nb + 1)
            pe.wait_ge(t.sem("spare_read"), full_wait)
            nc.tensor.transpose(spare.bitcast(F16)[SHIFT:SHIFT + NSH, 0:P], m16[:, :], ident16)\
                .then_inc(t.sem("spare_written"), 1)

        def pe_scores(pe, t, nb, c, par, half):
            k0, n = chunk(c)
            o = PS[0:n, bass.ds(par * ROWS + half * HALF, HALF)]
            q = nb * ROWS + half * HALF
            hi = ctxTh[0:KS, bass.ds(nb * KPAD + k0, n)]
            nc.tensor.matmul(o, hi, Qh[0:KS, bass.ds(q, HALF)], start=True, stop=False)
            nc.tensor.matmul(o, ctxTh[0:CD, bass.ds(nb * KPAD + k0, n)], Ql[0:CD, bass.ds(q, HALF)],
                             start=False, stop=False)
            ins = nc.tensor.matmul(o, ctxTl[0:CD, bass.ds(nb * KPAD + k0, n)], Qh[0:CD, bass.ds(q, HALF)],
                                   start=False, stop=not t.masked)
            if t.masked:
                ins = nc.tensor.matmul(o, maskb[:, k0:k0 + n], ch[:, H_IND:H_IND + HALF], start=False, stop=True)
            ins.then_inc(t.sem("scores"), 1)

        def pe_out(pe, t, nb, c, par, half, first, last):
            _, n = chunk(c)
            o = PO[0:CD + 1, half * HALF:(half + 1) * HALF]
            at = nb * (NCH * CPAD) + c * CPAD
            hi = ctxNh[0:n, bass.ds(at, CD + 1)]
            ph = Ph[0:n, bass.ds(par * ROWS + half * HALF, HALF)]
            nc.tensor.matmul(o, hi, ph, start=first, stop=False)
            nc.tensor.matmul(o, ctxNl[0:n, bass.ds(at, CD + 1)], ph, start=False, stop=False)
            return nc.tensor.matmul(o, hi, Pl[0:n, bass.ds(par * ROWS + half * HALF, HALF)],
                                    start=False, stop=last)

        def pe_sums(pe, t, half, spare):
            for j in range(4):
                at = half * HALF + j * P
                ins = nc.tensor.matmul(spare[:, j:j + 1], rawO[CD:CD + 1, at:at + P],
                                       cf[CD:CD + 1, C_ONE:C_ONE + 1], start=True, stop=True)
            ins.then_inc(t.sem("spare_written"), 1)

        def pe_spread(pe, t, half, spare):
            nc.tensor.matmul(spare[0:CD, :], cf[:, C_ONE:C_ONE + CD], diag[:, half * HALF:(half + 1) * HALF],
                             start=True, stop=True).then_inc(t.sem("spare_written"), 1)

        def pe_sequence(pe, t, b, pars, first=False, last=False, odd=None):
            g0 = b * t.n
            used = 0

            def spare():
                nonlocal used
                pe.wait_ge(t.sem("spare_read"), t.base(b) + (used - 1 if used else 0))
                used += 1
                return MISC[(used - 1) % 2]

            for i, c in enumerate(t.chunks):
                pi = pars[i % 2]
                ahead = i + 2
                nb, ci = (b, ahead) if ahead < t.n else (b + 1, ahead - t.n)
                if i == t.recip_slot and not first:
                    pe.wait_ge(t.sem("out_copied"), b)
                    for half in range(2):
                        pe_sums(pe, t, half, spare())
                if i == t.norm_slot and not first:
                    pe.wait_ge(t.sem("diag"), b)
                    for half in range(2):
                        pe_spread(pe, t, half, spare())
                if i == t.shift_slot and not last:
                    pe_shift(pe, t, b + 1, t.base(b) + used, MISC[used % 2])
                    used += 1
                extras = t.extras(i, last)

                def some():
                    if extras:
                        what, k = extras.pop(0)
                        if what == "max":
                            pe_max_unit(pe, t, b + 1, k, None, spare())
                        else:
                            pe_head_T(pe, b, b % 2 if odd is None else odd, k, spare()).then_inc(t.sem("spare_written"), 1)

                some()
                if not (last and nb is not b):
                    if ahead == t.n:
                        pe.wait_ge(t.sem("shift"), b + 2)
                    pe.wait_ge(t.sem("exp"), 2 * (g0 + i) + 1)
                    pe_scores(pe, t, nb, t.chunks[ci], pi, 0)
                    some()
                    pe.wait_ge(t.sem("exp"), 2 * (g0 + i) + 2)
                    pe_scores(pe, t, nb, t.chunks[ci], pi, 1)
                while len(extras) > 1:
                    some()
                for half in range(2):
                    pe.wait_ge(t.sem("p_high"), 2 * (g0 + i) + half + 1)
                    pe.wait_ge(t.sem("p_low"), 2 * (g0 + i) + half + 1)
                    if i == 0 and not first:
                        pe.wait_ge(t.sem("out_copied"), b)
                    pe_out(pe, t, b, c, pi, half, i == 0, i == t.n - 1).then_inc(t.sem("out"), 1)
                    some()

        def pe_attention(pe, t):
            if not t.prep:
                pe_heads(pe, t)
            for u in range(t.units):
                pe_max_unit(pe, t, 0, u, u - 1 if u >= 2 else None, MISC[u % 2])
            pe_shift(pe, t, 0, t.units, MISC[0])
            pe.wait_ge(t.sem("shift"), 1)
            for i in range(2):
                for half in range(2):
                    pe_scores(pe, t, 0, t.chunks[i], i, half)
            pe_sequence(pe, t, 0, (0, 1), first=True)
            pe_sequence(pe, t, 1, parities(t, 1))
            with pe.Fori(0, (B - 4) // 2) as pair:
                b = pair * 2 + 2
                pe_sequence(pe, t, b, (0, 1), odd=0)
                pe_sequence(pe, t, b + 1, parities(t, 1), odd=1)
            pe_sequence(pe, t, B - 2, (0, 1))
            pe_sequence(pe, t, B - 1, parities(t, B - 1), last=True)
            base = t.base(B - 1) + 4 + t.prep
            pe.wait_ge(t.sem("out_copied"), B)
            for half in range(2):
                pe.wait_ge(t.sem("spare_read"), base + half)
                pe_sums(pe, t, half, MISC[half])
            pe.wait_ge(t.sem("diag"), B)
            for half in range(2):
                pe.wait_ge(t.sem("spare_read"), base + 1 + half)
                pe_spread(pe, t, half, MISC[half])

        def parities(t, b):
            return b * t.n % 2, (b * t.n + 1) % 2

        def act_sequence(act, t, b, pars, first=False):
            g0 = b * t.n
            for i, c in enumerate(t.chunks):
                pi = pars[i % 2]
                _, n = chunk(c)
                for half in range(2):
                    at = slice(pi * ROWS + half * HALF, pi * ROWS + (half + 1) * HALF)
                    done = 2 * (g0 + i) + half + 1
                    act.wait_ge(t.sem("scores"), done)
                    if not (first and i < 2):
                        act.wait_ge(t.sem("p_low"), done - 4)
                    nc.scalar.activation(P32[0:n, at], PS[0:n, at], ACT.Exp).then_inc(t.sem("exp"), 1)
                    act.wait_ge(t.sem("exp"), done)
                    if not (first and i < 2):
                        act.wait_ge(t.sem("out"), done - 4)
                    nc.scalar.activation(Ph[0:n, at], P32[0:n, at], ACT.Copy).then_inc(t.sem("p_high"), 1)
                if i == 0 and not first:
                    act_copy_out(act, t, b)

        def act_copy_out(act, t, b):
            act.wait_ge(t.sem("out"), 2 * b * t.n)
            if not (isinstance(b, int) and b == 1):
                act.wait_ge(t.sem("normed"), b - 1)
            nc.scalar.activation(rawO[0:CD + 1, :], PO[0:CD + 1, :], ACT.Copy).then_inc(t.sem("out_copied"), 1)

        def act_attention(act, t):
            act_sequence(act, t, 0, (0, 1), first=True)
            act_sequence(act, t, 1, parities(t, 1))
            with act.Fori(0, (B - 2) // 2) as pair:
                b = pair * 2 + 2
                act_sequence(act, t, b, (0, 1))
                act_sequence(act, t, b + 1, parities(t, 1))
            act_copy_out(act, t, B)

        def dve_max_unit(dve, t, u, count, spare):
            j, s = divmod(u, len(t.slices))
            dve.wait_ge(t.sem("spare_written"), count)
            nc.vector.tensor_reduce(mx[:, u:u + 1], spare[:, 0:t.slices[s][1]], X, ALU.max)\
                .then_inc(t.sem("spare_read"), 1)

        def dve_round(dve, t, nb, read):
            dve.wait_ge(t.sem("spare_read"), read)
            src = mx[:, 0:BLOCKS]
            if len(t.slices) > 1:
                nc.vector.tensor_reduce(m8[:, :], mx[:, 0:t.units].rearrange("p (j s) -> p j s", j=BLOCKS),
                                        X, ALU.max).then_inc(t.sem("max_whole"), 1)
                dve.wait_ge(t.sem("max_whole"), nb + 1)
                src = m8[:, :]
            nc.vector.tensor_scalar(m16[:, :], src, NEG, -NEG, ALU.max, ALU.min).then_inc(t.sem("max_ready"), 1)

        def dve_shift(dve, t, nb, count, spare):
            dve.wait_ge(t.sem("spare_written"), count)
            mt = spare.bitcast(F16)[SHIFT:SHIFT + NSH, 0:P]
            nc.vector.tensor_tensor(
                Qh[SHIFT:SHIFT + NSH, bass.ds(nb * ROWS, ROWS)].rearrange("p (j r) -> p j r", j=BLOCKS),
                mt.unsqueeze(1).to_broadcast([NSH, BLOCKS, P]),
                cf[SHIFT:SHIFT + NSH, C_NDELTA:C_NDELTA + NSH].unsqueeze(2).to_broadcast([NSH, BLOCKS, P]),
                ALU.mult).then_inc(t.sem("spare_read"), 1)
            dve.wait_ge(t.sem("spare_read"), count)
            nc.vector.tensor_copy(ve[0:1, 0:1], ve[0:1, 0:1]).then_inc(t.sem("shift"), 1)

        def dve_norm(dve, t, b, half, spare, count):
            dve.wait_ge(t.sem("spare_written"), count)
            nc.vector.tensor_tensor(
                On[0:CD, b - 1, half * 8:(half + 1) * 8, :] if isinstance(b, int) else
                pool32[0:CD, bass.ds((b - 1) * ROWS + 3072 + half * HALF, HALF)].rearrange("p (h s) -> p h s", h=8),
                spare[0:CD, :].rearrange("p (h s) -> p h s", h=8),
                rawO[0:CD, half * HALF:(half + 1) * HALF].rearrange("p (h s) -> p h s", h=8),
                ALU.mult).then_inc(t.sem("spare_read"), 1)

        def dve_recip(dve, t, half, spare, count):
            dve.wait_ge(t.sem("spare_written"), count)
            ins = nc.vector.reciprocal(rcol[:, 4 * half:4 * half + 4], spare[:, 0:4])
            ins.then_inc(t.sem("spare_read"), 1)
            if half:
                dve.wait_ge(t.sem("spare_read"), count)
                nc.vector.tensor_copy(ve[0:1, 0:1], ve[0:1, 0:1]).then_inc(t.sem("rden"), 1)

        def pool_diag(pool, t, b):
            pool.wait_ge(t.sem("rden"), b + 1)
            if b:
                pool.wait_ge(t.sem("normed"), b)
            nc.gpsimd.tensor_tensor(diag[:, :].rearrange("p (j r) -> p j r", j=BLOCKS),
                                    ident.unsqueeze(1).to_broadcast([P, BLOCKS, P]),
                                    rcol[:, :].unsqueeze(2).to_broadcast([P, BLOCKS, P]), ALU.mult)\
                .then_inc(t.sem("diag"), 1)

        def dve_sequence(dve, t, b, pars, first=False, last=False):
            g0 = b * t.n
            used = 0

            def spare():
                nonlocal used
                used += 1
                return MISC[(used - 1) % 2], t.base(b) + used

            for i, c in enumerate(t.chunks):
                pi = pars[i % 2]
                _, n = chunk(c)
                if i == t.shift_slot and not last:
                    dve_round(dve, t, b + 1, t.base(b) + t.max_used(i, first))
                for half in range(2):
                    at = slice(pi * ROWS + half * HALF, pi * ROWS + (half + 1) * HALF)
                    done = 2 * (g0 + i) + half + 1
                    dve.wait_ge(t.sem("p_high"), done)
                    if not (first and i < 2):
                        dve.wait_ge(t.sem("out"), done - 4)
                    nc.vector.tensor_tensor(Pl[0:n, at], P32[0:n, at], Ph[0:n, at], ALU.subtract)\
                        .then_inc(t.sem("p_low"), 1)
                if i == t.recip_slot and not first:
                    if not (isinstance(b, int) and b == 1):
                        dve.wait_ge(t.sem("diag"), b - 1)
                    for half in range(2):
                        dve_recip(dve, t, half, *spare())
                if i == t.norm_slot and not first:
                    for half in range(2):
                        dve_norm(dve, t, b, half, *spare())
                    dve.wait_ge(t.sem("spare_read"), t.base(b) + used)
                    nc.vector.tensor_copy(ve[0:1, 0:1], ve[0:1, 0:1]).then_inc(t.sem("normed"), 1)
                if i == t.shift_slot and not last:
                    bank_, count = spare()
                    dve_shift(dve, t, b + 1, count, bank_)
                for what, k in t.extras(i, last):
                    bank_, count = spare()
                    if what == "max":
                        dve_max_unit(dve, t, k, count, bank_)
                    else:
                        dve.wait_ge(t.sem("spare_written"), count)
                        dve_head_T(dve, b, k, bank_).then_inc(t.sem("spare_read"), 1)

        def dve_attention(dve, t):
            if not t.prep:
                dve_heads(dve, t)
            for u in range(t.units):
                dve_max_unit(dve, t, u, u + 1, MISC[u % 2])
            dve_round(dve, t, 0, t.units)
            dve_shift(dve, t, 0, t.units + 1, MISC[0])
            dve_sequence(dve, t, 0, (0, 1), first=True)
            dve_sequence(dve, t, 1, parities(t, 1))
            with dve.Fori(0, (B - 4) // 2) as pair:
                b = pair * 2 + 2
                dve_sequence(dve, t, b, (0, 1))
                dve_sequence(dve, t, b + 1, parities(t, 1))
            dve_sequence(dve, t, B - 2, (0, 1))
            dve_sequence(dve, t, B - 1, parities(t, B - 1), last=True)
            base = t.base(B - 1) + 4 + t.prep
            dve.wait_ge(t.sem("diag"), B - 1)
            for half in range(2):
                dve_recip(dve, t, half, MISC[half], base + 1 + half)
            for half in range(2):
                dve_norm(dve, t, B, half, MISC[half], base + 3 + half)

        def pe_head_T(pe, k, odd, g, o):
            if g == 0:
                pe.wait_ge(sem(f"head{odd}"), 8 * (k - odd) + 16)
            for c in range(GROUP):
                ins = nc.tensor.transpose(o[0:CD, c * P:(c + 1) * P], head_raw[odd][:, g * GROUP + c, :], ident)
            return ins

        def dve_head_T(dve, k, g, o):
            at = k * KPAD + g * GROUP * P
            at = slice(at, at + GROUP * P) if isinstance(k, int) else bass.ds(at, GROUP * P)
            nc.vector.tensor_copy(ctxTh[0:CD, at], o[0:CD, 0:GROUP * P]).then_inc(sem("head_th"), 1)
            dve.wait_ge(sem("head_th"), k * GROUPS + g + 1)
            return nc.vector.tensor_tensor(ctxTl[0:CD, at], o[0:CD, 0:GROUP * P], ctxTh[0:CD, at], ALU.subtract)

        def pe_heads(pe, t):
            if t is att1:
                return
            with pe.Fori(0, B // 2) as pair:
                for odd in range(2):
                    k = pair * 2 + odd
                    for g in range(GROUPS):
                        pe.wait_ge(sem("ctx_tl"), B + k * GROUPS + g - GROUPS + 1)
                        pe_head_T(pe, k, odd, g, bank(g)).then_inc(sem("head_tp"), 1)
            pe.wait_ge(sem("ctx_tl"), B + B * GROUPS)
            pe.wait_ge(sem("ctx_nl"), 2 * B)

        def dve_heads(dve, t):
            if t is att1:
                return
            with dve.Fori(0, B) as k:
                for g in range(GROUPS):
                    dve.wait_ge(sem("head_tp"), k * GROUPS + g + 1)
                    dve_head_T(dve, k, g, bank(g)).then_inc(sem("ctx_tl"), 1)

        def pool_by_keys(b, raw, c0, n, done):
            h3 = ctxNh[:, :].rearrange("p (b c f) -> p b c f", b=B, c=NCH)[:, b]
            l3 = ctxNl[:, :].rearrange("p (b c f) -> p b c f", b=B, c=NCH)[:, b]
            parts = [(P, slice(c0, c0 + n), slice(0, n))]
            if c0 >= TAIL0:
                parts.append((LAST, slice(c0 + n, c0 + n + 1), slice(n, n + 1)))
            for k, c, rc in parts:
                nc.gpsimd.tensor_copy(h3[0:k, c, 0:CD], raw[0:k, rc, :]).then_inc(sem("ctx_nh"), 1)
            nc.gpsimd.wait_ge(sem("ctx_nh"), done)
            for k, c, rc in parts:
                ins = nc.gpsimd.tensor_tensor(l3[0:k, c, 0:CD], raw[0:k, rc, :], h3[0:k, c, 0:CD], ALU.subtract)
            ins.then_inc(sem("ctx_nl"), 1)

        def pool_head(pool, b):
            pool.wait_ge(sem(f"head{b % 2}"), 16 * (b // 2 + 1))
            pool_by_keys(b, head_raw[b % 2], 0, TAIL0, 2 * B + b + 1)

        def pool_attention(pool, t):
            if t is att0:
                for b in range(B):
                    pool_head(pool, b)
            for b in range(B):
                if t is att0s:
                    pool_head(pool, b)
                pool_diag(pool, t, b)

        att0 = Att("x0", list(range(NCH)), True)
        att0s = Att("x0", list(range(TAIL0, NCH)), True)
        att1 = Att("x1", list(range(NCH)), False)

        def either(eng, run):
            eng.wait_ge(sem("flag"), 1)
            v = eng.value_load(flag_i[0:1, 0:1], min_val=0, max_val=1)
            with eng.If(v > 0):
                run(eng, att0)
            with eng.Else():
                run(eng, att0s)

        flag_i = sb("flag_i", [1, 1], I32)
        flag_c = sb("flag_c", [S, 1])
        flag_r = sb("flag_r", [1, 1])

        LNS = ["l0a", "l0b", "l1", "l2", "l3", "l4", "l5"]

        def nth(tag):
            return LNS.index(tag) + 1

        def dve_ln(dve, tag, src, ready):
            dve.wait_ge(*ready)
            for t in range(TILES):
                ins = nc.vector.bn_stats(st[:, t, :], src[:, t, :])
            ins.then_inc(sem("ln_stats"), 1)
            dve.wait_ge(sem("ln_stats"), 2 * nth(tag) - 1)
            for t in range(TILES):
                ins = nc.vector.bn_aggr(mv[:, t, :], st[:, t, :])
            ins.then_inc(sem("ln_stats"), 1)
            dve.wait_ge(sem("ln_stats"), 2 * nth(tag))
            nc.vector.tensor_scalar(ve[:, :], mv[:, :, 1], LN_EPS, None, ALU.add).then_inc(sem("ln_var"), 1)
            dve.wait_ge(sem("ln_rstd"), nth(tag))
            for t in range(TILES):
                ins = nc.vector.tensor_scalar(yn[:, t, :], src[:, t, :], mv[:, t, 0:1], rstd[:, t:t + 1],
                                              ALU.subtract, ALU.mult)
            ins.then_inc(sem("ln_rows"), 1)

        def pool_ln(pool, tag):
            pool.wait_ge(sem("ln_var"), nth(tag))
            nc.gpsimd.tensor_tensor(rstd[:, :], ve[:, :], mhalf[:, :], ALU.pow).then_inc(sem("ln_rstd"), 1)

        def pe_rows_T(pe, src, dst, done):
            for t in range(TILES):
                ins = nc.tensor.transpose(dst[:, t * P:(t + 1) * P], src[:, t, :], ident)
            ins.then_inc(done, 1)

        def dve_residual(dve, tag, o):
            dve.wait_ge(sem(tag + "_y"), 1)
            nc.vector.tensor_tensor(xs[:, :, :], xs[:, :, :], o.rearrange("p (t n) -> p t n", t=TILES), ALU.add)\
                .then_inc(sem("x_" + tag), 1)

        def pe_heads_out(pe, tag, k, o):
            for h in range(HEADS):
                ins = nc.tensor.matmul(o[0], Bh[0:CD, h, :], On[0:CD, :, h, :], start=(h == 0), stop=(h == HEADS - 1))
            ins.then_inc(sem("heads_p"), 1)
            pe.wait_ge(sem("heads_s"), k)
            for u in range(TILES):
                ins = nc.tensor.transpose(o[1][:, u * P:(u + 1) * P], yT[:, u * P:(u + 1) * P], ident)
            ins.then_inc(sem(tag + "_y"), 1)

        def act_heads_out(act, k, bias, o):
            act.wait_ge(sem("heads_p"), k)
            nc.scalar.activation(yT[:, :], o[0], ACT.Identity, bias=bias).then_inc(sem("heads_s"), 1)

        def layer(tag):
            return int(tag[1])

        def pe_absorb(pe, tag):
            for i in range(24):
                g, which = i % 8, i // 8
                src, rows = ((Wq, P), (Wk, CD), (Wv, CD))[which]
                k = i // 4
                nc.tensor.transpose(bank(k)[:, (i % 4) * P:(i % 4) * P + rows],
                                    src[0:rows, g * P:(g + 1) * P], ident[0:rows, 0:rows])\
                    .then_inc(sem("wT"), 1)
            for which in range(2):
                for k in range(4):
                    if k < 2:
                        pe.wait_ge(sem("wTs"), 6 * layer(tag) + 6)
                    else:
                        pe.wait_ge(sem("wTs"), 6 * layer(tag) + 6)
                    o = bank(6 + k % 2)
                    if which or k >= 2:
                        pe.wait_ge(sem("abs"), 8 * layer(tag) + 4 * which + k - 1)
                    for i in range(4):
                        h = 8 * (k // 2) + 2 * i + k % 2
                        r = slice(DH * (h % 2), DH * (h % 2) + DH)
                        if which == 0:
                            ins = nc.tensor.matmul(o[:, i * P:i * P + CD], WqT[r, h // 2, :], WkT[r, h // 2, :],
                                                   start=True, stop=True)
                        else:
                            ins = nc.tensor.matmul(o[0:CD, i * P:(i + 1) * P], WvT[r, h // 2, :], Wo[r, h // 2, :],
                                                   start=True, stop=True)
                    ins.then_inc(sem("absp"), 1)

        def act_absorb(act, tag):
            for i in range(6):
                act.wait_ge(sem("wT"), 24 * layer(tag) + 4 * (i + 1))
                dst, rows = ((WqT, P), (WkT, CD), (WvT, CD))[i // 2]
                src = bank(i).rearrange("p (g n) -> p g n", g=4)[:, :, 0:rows]
                nc.scalar.activation(dst[:, 4 * (i % 2):4 * (i % 2) + 4, :], src, ACT.Copy)\
                    .then_inc(sem("wTs"), 1)

        def dve_absorb(dve, tag):
            for k in range(8):
                dve.wait_ge(sem("absp"), 8 * layer(tag) + k + 1)
                h0 = 8 * (k % 4 // 2) + k % 2
                src = bank(6 + k % 2).rearrange("p (g n) -> p g n", g=4)
                if k < 4:
                    nc.vector.tensor_scalar(Ah[:, h0:h0 + 7:2, :], src[:, :, 0:CD], DH ** -0.5, None, ALU.mult)\
                        .then_inc(sem("abs"), 1)
                else:
                    nc.vector.tensor_copy(Bh[0:CD, h0:h0 + 7:2, :], src[0:CD, :, :]).then_inc(sem("abs"), 1)

        def pe_queries(pe, tag, rdy):
            pe.wait_ge(*rdy)
            pe.wait_ge(sem("abs"), 8 * layer(tag) + 8)
            for h in range(HEADS):
                if h >= 4:
                    pe.wait_ge(sem("ql"), 16 * layer(tag) + h - 3)
                nc.tensor.matmul(bank(h % 4)[0:CD, :], Ah[:, h, :], yT[:, :], start=True, stop=True)\
                    .then_inc(sem("q"), 1)

        def q_view(t, h):
            return t[0:CD, :].rearrange("p (b r) -> p b r", b=B)[:, :, h * S:(h + 1) * S]

        def act_queries(act, tag):
            for h in range(HEADS):
                act.wait_ge(sem("q"), 16 * layer(tag) + h + 1)
                nc.scalar.activation(q_view(Qh, h), bank(h % 4)[0:CD, :].rearrange("p (b s) -> p b s", b=B), ACT.Copy)\
                    .then_inc(sem("qh"), 1)

        def dve_queries(dve, tag):
            for h in range(HEADS):
                dve.wait_ge(sem("qh"), 16 * layer(tag) + h + 1)
                nc.vector.tensor_tensor(q_view(Ql, h), bank(h % 4)[0:CD, :].rearrange("p (b s) -> p b s", b=B),
                                        q_view(Qh, h), ALU.subtract).then_inc(sem("ql"), 1)

        def load_absorb(eng, tag, wq, wk, wv, wo):
            eng.dma_start(Wq, wq).then_inc(sem(tag + "_w"), 16)
            eng.dma_start(Wk[0:CD, :], wk).then_inc(sem(tag + "_w"), 16)
            eng.dma_start(Wv[0:CD, :], wv).then_inc(sem(tag + "_w"), 16)
            eng.dma_start(Wo, wo.rearrange("(g p) n -> p g n", p=P)).then_inc(sem(tag + "_w"), 16)

        def dve_scales(dve, tag, n, count):
            dve.wait_ge(sem("gT"), count)
            nc.vector.tensor_reduce(gr[0:n, 0:1], bank(7)[0:n, 0:P], X, ALU.max).then_inc(sem("g_step"), 1)
            dve.wait_ge(sem("g_step"), 3 * count - 2)
            nc.vector.tensor_scalar(gr[0:n, 1:1 + n], ident[0:n, 0:n], gr[0:n, 0:1], None, ALU.mult)\
                .then_inc(sem("g2"), 1)
            dve.wait_ge(sem("gB"), count)
            nc.vector.tensor_scalar(gq[:, 2:2 + n], bank(7)[:, 256:256 + n], 1.0 / 32767.0, 1e-12,
                                    ALU.mult, ALU.max).then_inc(sem("g_step"), 1)
            dve.wait_ge(sem("g_step"), 3 * count - 1)
            nc.vector.reciprocal(gq[:, 4:4 + n], gq[:, 2:2 + n]).then_inc(sem("g_step"), 1)
            dve.wait_ge(sem("g_step"), 3 * count)

        def pe_scales(pe, n, count):
            pe.wait_ge(sem("g0"), count)
            nc.tensor.transpose(bank(7)[0:n, 0:P], gq[:, 0:n], ident).then_inc(sem("gT"), 1)
            pe.wait_ge(sem("g2"), count)
            nc.tensor.matmul(bank(7)[:, 256:256 + n], cf[0:n, C_ONE:C_ONE + P], gr[0:n, 1:1 + n],
                             start=True, stop=True).then_inc(sem("gB"), 1)

        @block.sync
        def _(sp):
            sp.dma_start(xs[:, :, :], a["x"].rearrange("b s d -> (b s) d").rearrange("(t p) d -> p t d", p=P))\
                .then_inc(sem("x_in"), 16)
            sp.dma_start(cf[:, :], a["cf"]).then_inc(sem("consts"), 16)
            sp.dma_start(ch[:, :], a["ch"]).then_inc(sem("consts"), 16)
            v = [a["L0_xattn_ln_gamma"], a["L0_xattn_ln_beta"], a["L1_attn_bqk"]]
            for i, r in enumerate(v):
                sp.dma_start(vecs[i:i + 1, :], r.unsqueeze(0)).then_inc(sem("vecs"), 16)
            sp.dma_start(vecs[3:5, :], a["L1_attn_gamma"]).then_inc(sem("vecs"), 16)
            sp.dma_start(vecs[5:7, :], a["L1_attn_beta"]).then_inc(sem("vecs"), 16)
            sp.dma_start(vecs[7:39, :], a["L1_ffn_b1"].rearrange("e (c n) -> (e c) n", n=P)).then_inc(sem("vecs"), 16)
            sp.dma_start(vecs[39:43, :], a["L1_ffn_ob1"].rearrange("(c n) -> c n", n=P)).then_inc(sem("vecs"), 16)
            sp.dma_start(vecs[43:44, :], a["L0_xattn_bo"].unsqueeze(0)).then_inc(sem("vecs"), 16)
            sp.dma_start(vecs[44:45, :], a["L1_xattn_bo"].unsqueeze(0)).then_inc(sem("vecs"), 16)
            sp.dma_start(emb[:, :], a["L1_attn_rel_emb"]).then_inc(sem("vecs"), 16)
            load_absorb(sp, "w0", a["L0_xattn_Wq"], a["L0_xattn_Wkv"][:, 0:1024], a["L0_xattn_Wkv"][:, 1024:2048],
                        a["L0_xattn_Wo"])
            sp.dma_start(mask8[:, :], a["mask_1x1xSxS2_bk0"].rearrange("a b s k -> (a b s) k")).then_inc(sem("mask"), 16)
            for b in range(B):
                src = a["ctx_768"][b]
                sp.dma_start(tail_raw[:, b, 0:TAILS - 1, :],
                             src[TAIL0 * P:(NCH - 1) * P, :].rearrange("(c p) d -> p c d", p=P))\
                    .then_inc(sem(f"tail{b // 2}"), 16)
                sp.dma_start(tail_raw[0:LAST, b, TAILS - 1, :], src[(NCH - 1) * P:KEYS, :])\
                    .then_inc(sem(f"tail{b // 2}"), 16)
            sp.dma_start(wqk1[:, 0, :], a["L1_attn_Wqk"]).then_inc(sem("small"), 16)
            sp.dma_start(wqk1[:, 1, :], a["L1_attn_Wv"]).then_inc(sem("small"), 16)
            sp.dma_start(rw[:, :], a["L1_ffn_router_w"]).then_inc(sem("small"), 16)
            sp.dma_start(rb[:, :], a["L1_ffn_router_b"].unsqueeze(0)).then_inc(sem("small"), 16)
            sp.dma_start(b2r[0:EXPERTS, :], a["L1_ffn_b2"]).then_inc(sem("small"), 16)
            sp.dma_start(b2r[EXPERTS:SELS, :], a["L1_ffn_ob2"].unsqueeze(0)).then_inc(sem("small"), 16)
            for i, n in enumerate(["L0_attn_proj_bias", "L1_attn_bv"]):
                sp.dma_start(rows1[:, i * D:(i + 1) * D], a[n].unsqueeze(0)).then_inc(sem("small"), 16)
            sp.wait_ge(sem("gp"), 1)
            sp.dma_start(scratch.unsqueeze(0), gp[:, :]).then_inc(sem("gp_out"), 16)
            sp.wait_ge(sem("gp_out"), 16)
            hs = bass.AP(scratch.tensor, 0, [[1, S], [1, S]])
            sp.dma_start(hank[:, :], hs).then_inc(sem("hank"), 16)
            sp.wait_ge(sem("abs"), 8)
            for b in range(B):
                if b >= 2:
                    sp.wait_ge(sem("head_th"), GROUPS * (b - 1))
                    sp.wait_ge(sem("ctx_nl"), B + b - 1)
                sp.dma_start(head_raw[b % 2][:, :, :],
                             a["ctx_768"][b][0:TAIL0 * P, :].rearrange("(c p) d -> p c d", p=P))\
                    .then_inc(sem(f"head{b % 2}"), 16)
            sp.wait_ge(sem("a0_y"), 1)
            sp.dma_start(sraw[:, 0:3, :], a["L0_attn_qkv_weight"].rearrange("(g p) n -> p g n", p=P)).then_inc(sem("mid"), 16)
            sp.dma_start(sraw[:, 3, :], a["L0_attn_proj_weight"]).then_inc(sem("mid"), 16)
            sp.dma_start(ffraw[:, 0:3, :], a["L0_ffn_w_gate"].rearrange("(g p) n -> p g n", p=P)).then_inc(sem("mid"), 16)
            sp.dma_start(ffraw[:, 3:6, :], a["L0_ffn_w_up"].rearrange("(g p) n -> p g n", p=P)).then_inc(sem("mid"), 16)
            sp.dma_start(ffraw[:, 6:9, :], a["L0_ffn_w_down"].rearrange("p (g n) -> p g n", g=3)).then_inc(sem("mid"), 16)
            load_absorb(sp, "w1", a["L1_xattn_Wq"], a["L1_xattn_Wk"], a["L1_xattn_Wv"], a["L1_xattn_Wo"])
            sp.wait_ge(sem("a3_y"), 1)
            for e in range(EXPERTS):
                sp.dma_start(w1[:, e, :], a["L1_ffn_w1"][e]).then_inc(sem(f"ex{e}"), 16)
                sp.dma_start(w2[:, e, :, :], a["L1_ffn_w2"][e].rearrange("(c p) n -> p c n", p=P)).then_inc(sem(f"ex{e}"), 16)
            sp.dma_start(w1[:, EXPERTS, :], a["L1_ffn_ow1"]).then_inc(sem(f"ex{EXPERTS}"), 16)
            sp.dma_start(w2[:, EXPERTS, :, :], a["L1_ffn_ow2"].rearrange("(c p) n -> p c n", p=P)).then_inc(sem(f"ex{EXPERTS}"), 16)
            sp.wait_ge(sem("x_a5"), 1)
            sp.dma_start(out.rearrange("b s d -> (b s) d").rearrange("(t p) d -> p t d", p=P), xs[:, :, :])\
                .then_inc(sem("stored"), 16)
            sp.wait_ge(sem("stored"), 16)

        @block.gpsimd
        def _(pool):
            nc.gpsimd.memset(mhalf[:, :], -0.5).then_inc(sem("fills"), 1)
            pool.wait_ge(sem("fills"), 1)
            nc.gpsimd.memset(maskb[S:P, :], 0.0).then_inc(sem("fills"), 1)
            pool.wait_ge(sem("fills"), 2)
            nc.gpsimd.memset(ctxTh[CD:P, :], 1.0).then_inc(sem("fills"), 1)
            pool.wait_ge(sem("fills"), 3)
            n3 = ctxNh[:, :].rearrange("p (c f) -> p c f", f=CPAD)
            nc.gpsimd.memset(n3[:, :, CD:CPAD], 1.0).then_inc(sem("fills"), 1)
            n3 = ctxNl[:, :].rearrange("p (c f) -> p c f", f=CPAD)
            nc.gpsimd.memset(n3[:, :, CD:CPAD], 0.0).then_inc(sem("fills"), 1)
            pool_ln(pool, "l0a")
            pool_ln(pool, "l0b")
            for b in range(B):
                pool.wait_ge(sem(f"tail{b // 2}"), 64)
                pool_by_keys(b, tail_raw[:, b], TAIL0, TAILS - 1, 2 * b + 2)
            either(pool, pool_attention)
            for tag in ("l1", "l2", "l3"):
                pool_ln(pool, tag)
            for b in range(B):
                pool_diag(pool, att1, b)
            for tag in ("l4", "l5"):
                pool_ln(pool, tag)

        @block.scalar
        def _(act):
            act.wait_ge(sem("vT"), 1)
            nc.scalar.activation(vcol[:, 0:45], bank(7)[:, 0:45], ACT.Copy).then_inc(sem("vcol"), 1)
            act_absorb(act, "w0")
            for b in range(B):
                act.wait_ge(sem("ctx_tp"), b + 1)
                at = slice(b * KPAD + TAIL0 * P, b * KPAD + KEYS)
                nc.scalar.activation(ctxTh[0:CD, at], bank(b % 4)[0:CD, 0:KEYS - TAIL0 * P], ACT.Copy)\
                    .then_inc(sem("ctx_th"), 1)
            act.wait_ge(sem("ln_T"), nth("l0b") - 1)
            act.wait_ge(sem("vcol"), 1)
            nc.scalar.activation(yT[:, :], bank(6), ACT.Identity, bias=vcol[:, 1:2], scale=vcol[:, 0:1])\
                .then_inc(sem("yT0"), 1)
            act_queries(act, "w0")
            act.wait_ge(sem("ctx_nl"), B)
            either(act, act_attention)
            act_heads_out(act, 1, vcol[:, 43:44], (bank(0), bank(6)))
            act.wait_ge(sem("ln_T"), nth("l1") - 1)
            nc.scalar.activation(yT[:, :], bank(0), ACT.Copy).then_inc(sem("yT1"), 1)
            act.wait_ge(sem("lq"), 1)
            nc.scalar.activation(tq[:, 0:TOK], bank(1), ACT.Relu).then_inc(sem("lqs"), 1)
            act.wait_ge(sem("gate_q"), 1)
            nc.scalar.activation(tl[:, 1536:3072], tl[:, 0:1536], ACT.Tanh, scale=0.5).then_inc(sem("fexp"), 1)
            act.wait_ge(sem("x_a2"), 1)
            act_absorb(act, "w1")
            act.wait_ge(sem("ln_T"), nth("l3") - 1)
            nc.scalar.activation(yT[:, :], bank(6), ACT.Copy).then_inc(sem("yT3"), 1)
            act_queries(act, "w1")
            act_attention(act, att1)
            act_heads_out(act, 2, vcol[:, 44:45], (bank(0), bank(6)))
            act.wait_ge(sem("ln_T"), nth("l4") - 1)
            nc.scalar.activation(yT[:, :], bank(0), ACT.Copy).then_inc(sem("yT4"), 1)
            act.wait_ge(sem("sqk"), 1)
            nc.scalar.activation(tq[:, 0:512], bank(1), ACT.Identity, bias=vcol[:, 2:3]).then_inc(sem("sqk_s"), 1)
            act.wait_ge(sem("sqk_s"), 1)
            nc.scalar.activation(tq[:, 512:1024], tq[:, 0:512], ACT.Tanh, scale=0.5).then_inc(sem("sqk_e"), 1)
            act.wait_ge(sem("sv"), 1)
            nc.scalar.activation(tl[:, 0:512], bank(2), ACT.Tanh, scale=0.5).then_inc(sem("sv_e"), 1)
            act.wait_ge(sem("z2"), 1)
            nc.scalar.activation(tp[:, 0:512], tp[:, 512:1024], ACT.Exp, scale=-1.0).then_inc(sem("ze"), 1)
            act.wait_ge(sem("ln_T"), nth("l5") - 1)
            nc.scalar.activation(yT[:, :], bank(0), ACT.Copy).then_inc(sem("yT5"), 1)
            for e in range(SELS):
                for c in range(HC):
                    k = e * HC + c
                    if k % 2 == 0:
                        act.wait_ge(sem("hid"), k + 1)
                        if k >= 4:
                            act.wait_ge(sem("hid_used"), k - 3)
                        nc.scalar.activation(tl[:, (k % 4) * HALF:(k % 4 + 1) * HALF], bank(2 + k % 4), ACT.Relu,
                                             bias=vcol[:, 7 + k:8 + k]).then_inc(sem("hid_a"), 1)

        @block.vector
        def _(dve):
            dve_ln(dve, "l0a", xs, (sem("x_in"), 16))
            dve.wait_ge(sem("mask"), 16)
            nc.vector.tensor_scalar(maskb[0:S, 0:KEYS], mask8[:, :], -NEG, NEG, ALU.mult, ALU.add)\
                .then_inc(sem("maskb"), 1)
            nc.vector.tensor_reduce(flag_c[:, :], mask8[:, 0:TAIL0 * P], X, ALU.max).then_inc(sem("flag_c"), 1)
            dve.wait_ge(sem("gp_p"), 1)
            nc.vector.tensor_scalar(gp[:, :], bank(6)[0:1, 0:2 * S], D ** 0.5 * ERF_A, -MU * ERF_A,
                                    ALU.mult, ALU.add).then_inc(sem("gp"), 1)
            dve.wait_ge(sem("vcol"), 1)
            nc.vector.tensor_scalar(ghalf[:, :], vcol[:, 3:5], 0.5, None, ALU.mult)
            dve_ln(dve, "l0b", yn, (sem("ln_rows"), nth("l0a")))
            dve_absorb(dve, "w0")
            for b in range(B):
                dve.wait_ge(sem("ctx_th"), b + 1)
                at = slice(b * KPAD + TAIL0 * P, b * KPAD + KEYS)
                nc.vector.tensor_tensor(ctxTl[0:CD, at], bank(b % 4)[0:CD, 0:KEYS - TAIL0 * P], ctxTh[0:CD, at],
                                        ALU.subtract).then_inc(sem("ctx_tl"), 1)
            dve.wait_ge(sem("flag_T"), 1)
            nc.vector.tensor_reduce(flag_r[:, :], bank(7)[0:1, 256:256 + S], X, ALU.max).then_inc(sem("flag_c"), 1)
            dve.wait_ge(sem("flag_c"), 2)
            nc.vector.tensor_copy(flag_i[:, :], flag_r[:, :]).then_inc(sem("flag"), 1)
            dve_queries(dve, "w0")
            dve.wait_ge(sem("ctx_nl"), B)
            either(dve, dve_attention)
            nc.vector.drain().then_inc(sem("x0_done"), 1)
            dve_residual(dve, "a0", bank(6))
            dve.wait_ge(sem("sT"), 1)
            nc.vector.tensor_copy(qkvT[:, :], bank(2)[:, 0:3 * D]).then_inc(sem("sTs"), 1)
            nc.vector.tensor_copy(projT[:, :], bank(2)[:, 3 * D:4 * D]).then_inc(sem("sTs"), 1)
            dve_ln(dve, "l1", xs, (sem("x_a0"), 1))
            kk = tq[:, 512:1024].rearrange("p (t n) -> p t n", t=TILES)
            vv = tq[:, 1024:1536].rearrange("p (t n) -> p t n", t=TILES)
            for t in range(TILES):
                dve.wait_ge(sem("lkv"), t + 1)
                src = bank(2 + t)
                nc.vector.tensor_scalar(kk[:, t, :], src[:, 0:D], 0.0, None, ALU.max)
                nc.vector.tensor_scalar(vv[:, t, :], src[:, D:2 * D], 0.0, None, ALU.max).then_inc(sem("lkvs"), 1)
            blk = cf[:, C_BLK:C_BLK + P]
            kvm = tq[:, 2048:3072].rearrange("p (b n) -> p b n", b=B)
            ksm = tq[:, 3072:4096].rearrange("p (b n) -> p b n", b=B)
            for odd in range(2):
                dve.wait_ge(sem("kv"), odd + 1)
                src = bank(odd).rearrange("p (b n) -> p b n", b=4)
                nc.vector.tensor_tensor(kvm[:, odd:B:2, :], src, blk.unsqueeze(1).to_broadcast([P, 4, P]), ALU.mult)
                dve.wait_ge(sem("ks"), odd + 1)
                src = bank(2 + odd)[:, 0:4].unsqueeze(2).to_broadcast([P, 4, P])
                nc.vector.tensor_tensor(ksm[:, odd:B:2, :], src, blk.unsqueeze(1).to_broadcast([P, 4, P]), ALU.mult)\
                    .then_inc(sem("kvm"), 1)
            dve.wait_ge(sem("lden"), 1)
            den, rat = tl[:, 0:512], tl[:, 512:1024]
            nc.vector.tensor_scalar(den, bank(5), 1e-15, None, ALU.add).then_inc(sem("den"), 1)
            dve.wait_ge(sem("den"), 1)
            nc.vector.reciprocal(rat, den).then_inc(sem("den"), 1)
            dve.wait_ge(sem("den"), 2)
            nc.vector.tensor_tensor(rat, bank(4), rat, ALU.mult).then_inc(sem("rat"), 1)
            dve_residual(dve, "a1", bank(6))
            w36 = ffraw[:, :, :].rearrange("p g (k n) -> p (g k) n", n=WBLK)
            dve.wait_ge(sem("mid"), 16 * 5)
            nc.vector.tensor_reduce(fsc[:, :], w36, X, ALU.max, apply_absolute_value=True).then_inc(sem("fw"), 1)
            dve.wait_ge(sem("fw"), 1)
            nc.vector.tensor_scalar(fsc[:, :], fsc[:, :], 1.0 / 7.0, 1e-12, ALU.mult, ALU.max).then_inc(sem("fw"), 1)
            dve.wait_ge(sem("fw"), 2)
            nc.vector.reciprocal(fin[:, :], fsc[:, :]).then_inc(sem("fw"), 1)
            dve.wait_ge(sem("fw"), 3)
            nc.vector.tensor_tensor(w36, w36, fin[:, :].unsqueeze(2).to_broadcast([P, 36, WBLK]), ALU.mult)\
                .then_inc(sem("fw"), 1)
            dve.wait_ge(sem("fw"), 4)
            nc.vector.tensor_scalar(w36, w36, MAGIC, -MAGIC, ALU.add, ALU.add).then_inc(sem("fw"), 1)
            dve.wait_ge(sem("fw"), 5)
            nc.vector.tensor_tensor(w36, w36, fsc[:, :].unsqueeze(2).to_broadcast([P, 36, WBLK]), ALU.mult)\
                .then_inc(sem("fw"), 1)
            for k in range(3):
                dve.wait_ge(sem("fwT"), k + 1)
                nc.vector.tensor_copy(ffT[:, 3 * k:3 * k + 3, :],
                                      bank(k)[:, 0:3 * P].rearrange("p (g n) -> p g n", g=3)).then_inc(sem("fwTs"), 1)
            dve_ln(dve, "l2", xs, (sem("x_a1"), 1))
            dve.wait_ge(sem("ln_rows"), nth("l2"))
            y512 = yn[:, :, :].rearrange("p t n -> p (t n)")
            nc.vector.tensor_reduce(gq[:, 0:1], y512, X, ALU.max, apply_absolute_value=True).then_inc(sem("g0"), 1)
            dve_scales(dve, "x", 1, 1)
            dve.wait_ge(sem("ln_T"), nth("l2") - 1)
            nc.vector.tensor_scalar(yT[:, :], bank(6), gq[:, 4:5], MAGIC, ALU.mult, ALU.add).then_inc(sem("fy"), 1)
            dve.wait_ge(sem("fy"), 1)
            nc.vector.tensor_scalar(yT[:, :], yT[:, :], -MAGIC, gq[:, 2:3], ALU.add, ALU.mult).then_inc(sem("fy"), 1)
            gate, up = tl[:, 0:1536], tq[:, 0:1536]
            sg, gs = tq[:, 1536:3072], tl[:, 1536:3072]
            dve.wait_ge(sem("fg"), 3)
            nc.vector.tensor_reduce(gq[:, 0:1], PS[:, 0:1536], X, ALU.max, apply_absolute_value=True)
            dve.wait_ge(sem("fu"), 3)
            nc.vector.tensor_reduce(gq[:, 1:2], PS[:, 1536:3072], X, ALU.max, apply_absolute_value=True)\
                .then_inc(sem("g0"), 1)
            dve_scales(dve, "gu", 2, 2)
            nc.vector.tensor_scalar(gate, PS[:, 0:1536], gq[:, 4:5], MAGIC, ALU.mult, ALU.add).then_inc(sem("gate"), 1)
            dve.wait_ge(sem("gate"), 1)
            nc.vector.tensor_scalar(gate, gate, -MAGIC, gq[:, 2:3], ALU.add, ALU.mult).then_inc(sem("gate_q"), 1)
            nc.vector.tensor_scalar(up, PS[:, 1536:3072], gq[:, 5:6], MAGIC, ALU.mult, ALU.add).then_inc(sem("gate"), 1)
            dve.wait_ge(sem("gate"), 2)
            nc.vector.tensor_scalar(up, up, -MAGIC, gq[:, 3:4], ALU.add, ALU.mult)
            dve.wait_ge(sem("fexp"), 1)
            et = tl[:, 1536:3072]
            nc.vector.tensor_scalar(et, et, 32768.0, 32768.0, ALU.mult, ALU.add).then_inc(sem("sg"), 2)
            dve.wait_ge(sem("sg"), 2)
            nc.vector.tensor_scalar(sg, et, MAGIC, None, ALU.add).then_inc(sem("sg"), 1)
            dve.wait_ge(sem("sg"), 3)
            nc.vector.tensor_scalar(sg, sg, -MAGIC, 65535.0, ALU.add, ALU.min).then_inc(sem("sg"), 1)
            dve.wait_ge(sem("sg"), 4)
            nc.vector.scalar_tensor_tensor(gs, sg, 2.0 ** -16, gate, ALU.mult, ALU.mult).then_inc(sem("sg"), 1)
            dve.wait_ge(sem("sg"), 5)
            nc.vector.tensor_reduce(gq[:, 0:1], gs, X, ALU.max, apply_absolute_value=True).then_inc(sem("g0"), 1)
            dve_scales(dve, "gs", 1, 3)
            nc.vector.tensor_scalar(gs, gs, gq[:, 4:5], MAGIC, ALU.mult, ALU.add).then_inc(sem("sg"), 1)
            dve.wait_ge(sem("sg"), 6)
            nc.vector.tensor_scalar(gs, gs, -MAGIC, gq[:, 2:3], ALU.add, ALU.mult).then_inc(sem("sg"), 1)
            dve.wait_ge(sem("sg"), 7)
            nc.vector.tensor_tensor(gs, gs, up, ALU.mult).then_inc(sem("sg"), 1)
            dve.wait_ge(sem("sg"), 8)
            nc.vector.tensor_reduce(gq[:, 0:1], gs, X, ALU.max, apply_absolute_value=True).then_inc(sem("g0"), 1)
            dve_scales(dve, "o", 1, 4)
            nc.vector.tensor_scalar(gs, gs, gq[:, 4:5], MAGIC, ALU.mult, ALU.add).then_inc(sem("sg"), 1)
            dve.wait_ge(sem("sg"), 9)
            nc.vector.tensor_scalar(gs, gs, -MAGIC, gq[:, 2:3], ALU.add, ALU.mult).then_inc(sem("fo"), 1)
            dve_residual(dve, "a2", bank(6))
            dve_ln(dve, "l3", xs, (sem("x_a2"), 1))
            dve_absorb(dve, "w1")
            dve_queries(dve, "w1")
            dve_attention(dve, att1)
            nc.vector.drain().then_inc(sem("x1_done"), 1)
            dve_residual(dve, "a3", bank(6))
            dve_ln(dve, "l4", xs, (sem("x_a3"), 1))
            dve.wait_ge(sem("biasT"), 1)
            for i in range(2):
                nc.vector.tensor_copy(biasz[:, i * S:(i + 1) * S], bank(7)[:, 0:S]).then_inc(sem("biasz"), 1)
            lin, ex = tq[:, 0:512], tq[:, 512:1024]
            dve.wait_ge(sem("sqk_e"), 1)
            nc.vector.scalar_tensor_tensor(lin, ex, 1.0, lin, ALU.add, ALU.mult).then_inc(sem("sw"), 1)
            dve.wait_ge(sem("sw"), 1)
            qT, kT = tq[:, 1024:1536], tq[:, 1536:2048]
            nc.vector.tensor_scalar(qT, lin, ghalf[:, 0:1], vcol[:, 5:6], ALU.mult, ALU.add)
            nc.vector.tensor_scalar(kT, lin, ghalf[:, 1:2], vcol[:, 6:7], ALU.mult, ALU.add).then_inc(sem("sqks"), 1)
            ev, vr = tl[:, 0:512], tl[:, 512:1024]
            dve.wait_ge(sem("sv_e"), 1)
            nc.vector.tensor_scalar(ev, ev, 0.5, 0.5, ALU.mult, ALU.add).then_inc(sem("sw"), 1)
            dve.wait_ge(sem("sw"), 2)
            nc.vector.tensor_tensor(vr, bank(2), ev, ALU.mult).then_inc(sem("svr"), 1)
            z, z2 = tl[:, 1024:1536], tp[:, 512:1024]
            az, tt, acc = tl[:, 1536:2048], tl[:, 2048:2560], tl[:, 2560:3072]
            dve.wait_ge(sem("sim"), 1)
            dve.wait_ge(sem("biasz"), 2)
            nc.vector.scalar_tensor_tensor(
                z.rearrange("p (t n) -> p t n", t=TILES), bank(3).rearrange("p (t n) -> p t n", t=TILES),
                ERF_A / S, biasz[:, :].unsqueeze(1).to_broadcast([P, TILES, P]), ALU.mult, ALU.add)\
                .then_inc(sem("z"), 1)
            dve.wait_ge(sem("z"), 1)
            nc.vector.tensor_tensor(z2, z, z, ALU.mult).then_inc(sem("z2"), 1)
            nc.vector.scalar_tensor_tensor(az, z, -1.0, z, ALU.mult, ALU.max).then_inc(sem("z"), 1)
            dve.wait_ge(sem("z"), 2)
            nc.vector.tensor_scalar(az, az, ERF_P, 1.0, ALU.mult, ALU.add).then_inc(sem("z"), 1)
            dve.wait_ge(sem("z"), 3)
            nc.vector.reciprocal(tt, az).then_inc(sem("z"), 1)
            dve.wait_ge(sem("z"), 4)
            nc.vector.tensor_scalar(acc, tt, ERF_C[4], None, ALU.mult).then_inc(sem("z"), 1)
            for i in range(4):
                dve.wait_ge(sem("z"), 5 + i)
                nc.vector.scalar_tensor_tensor(acc, acc, ERF_C[3 - i], tt, ALU.add, ALU.mult).then_inc(sem("z"), 1)
            dve.wait_ge(sem("z"), 9)
            dve.wait_ge(sem("ze"), 1)
            nc.vector.scalar_tensor_tensor(acc, acc, 0.5, tp[:, 0:512], ALU.mult, ALU.mult).then_inc(sem("z"), 1)
            nc.vector.tensor_scalar(az, z, 0.0, -2.0, ALU.is_ge, ALU.mult).then_inc(sem("z"), 1)
            dve.wait_ge(sem("z"), 11)
            nc.vector.scalar_tensor_tensor(acc, az, 1.0, acc, ALU.add, ALU.mult).then_inc(sem("z"), 1)
            dve.wait_ge(sem("z"), 12)
            nc.vector.scalar_tensor_tensor(acc, az, -0.5, acc, ALU.mult, ALU.add).then_inc(sem("z"), 1)
            dve.wait_ge(sem("z"), 13)
            acc3 = acc.rearrange("p (t n) -> p t n", t=TILES)
            nc.vector.tensor_tensor(acc3, acc3, cf[:, C_CAUSAL:C_CAUSAL + P].unsqueeze(1).to_broadcast([P, TILES, P]),
                                    ALU.mult).then_inc(sem("attn"), 1)
            dve_residual(dve, "a4", bank(6))
            dve_ln(dve, "l5", xs, (sem("x_a4"), 1))
            lg = tp[:, 0:32].rearrange("p (t e) -> p t e", e=EXPERTS)
            sc8 = tp[:, 32:64].rearrange("p (t e) -> p t e", e=EXPERTS)
            top = tp[:, 64:68]
            oh = tp[:, 68:100].rearrange("p (t e) -> p t e", e=EXPERTS)
            sel = tp[:, 100:136].rearrange("p (t e) -> p t e", e=SELS)
            oh16 = Pl[:, 0:32]
            sel16 = Pl[:, 32:32 + 4 * SELS]
            lp = bank(1)[:, 0:32].rearrange("p (t e) -> p t e", e=EXPERTS)
            dve.wait_ge(sem("rlog"), 1)
            nc.vector.tensor_reduce(top, lp, X, ALU.max).then_inc(sem("r"), 1)
            dve.wait_ge(sem("r"), 1)
            nc.vector.tensor_tensor(lg, lp, top.unsqueeze(2).to_broadcast([P, TILES, EXPERTS]), ALU.is_ge)\
                .then_inc(sem("r"), 1)
            dve.wait_ge(sem("r"), 2)
            nc.vector.tensor_tensor(sc8, lg, cf[:, C_FIRST:C_FIRST + EXPERTS].unsqueeze(1).to_broadcast(
                [P, TILES, EXPERTS]), ALU.mult).then_inc(sem("r"), 1)
            dve.wait_ge(sem("r"), 3)
            nc.vector.tensor_reduce(top, sc8, X, ALU.max).then_inc(sem("r"), 1)
            dve.wait_ge(sem("r"), 4)
            nc.vector.tensor_tensor(oh, sc8, top.unsqueeze(2).to_broadcast([P, TILES, EXPERTS]), ALU.is_equal)\
                .then_inc(sem("r"), 1)
            dve.wait_ge(sem("r"), 5)
            nc.vector.tensor_copy(oh16.rearrange("p (t e) -> p t e", e=EXPERTS), oh).then_inc(sem("oh"), 1)
            dve.wait_ge(sem("rank"), 1)
            rk = bank(2)[:, 0:32].rearrange("p (t e) -> p t e", e=EXPERTS)
            nc.vector.scalar_tensor_tensor(sel[:, :, 0:EXPERTS], rk, float(CAP), oh, ALU.is_le, ALU.mult)\
                .then_inc(sem("r"), 1)
            dve.wait_ge(sem("r"), 6)
            nc.vector.tensor_reduce(top, sel[:, :, 0:EXPERTS], X, ALU.add).then_inc(sem("r"), 1)
            dve.wait_ge(sem("r"), 7)
            nc.vector.tensor_scalar(sel[:, :, EXPERTS], top, -1.0, 1.0, ALU.mult, ALU.add).then_inc(sem("r"), 1)
            dve.wait_ge(sem("r"), 8)
            nc.vector.tensor_copy(sel16.rearrange("p (t e) -> p t e", e=SELS), sel).then_inc(sem("sel"), 1)
            dve.wait_ge(sem("selT"), 1)
            sT = bank(3).bitcast(F16)[0:SELS, 0:TOK]
            nc.vector.tensor_scalar(tq[0:SELS, 0:TOK], sT, 1.0, None, ALU.mult).then_inc(sem("selT_s"), 1)
            nc.vector.tensor_scalar(Ph[0:SELS, 2 * 512:2 * 512 + TOK], sT, -NEG, NEG, ALU.mult, ALU.add)\
                .then_inc(sem("selT_s"), 1)
            for k in range(SELS * HC):
                if k % 2 == 1:
                    dve.wait_ge(sem("hid"), k + 1)
                    if k >= 4:
                        dve.wait_ge(sem("hid_used"), k - 3)
                    nc.vector.tensor_scalar(tl[:, (k % 4) * HALF:(k % 4 + 1) * HALF], bank(2 + k % 4),
                                            vcol[:, 7 + k:8 + k], 0.0, ALU.add, ALU.max).then_inc(sem("hid_d"), 1)
            dve_residual(dve, "a5", bank(6))

        @block.tensor
        def _(pe):
            pe.wait_ge(sem("consts"), 32)
            pe.wait_ge(sem("vecs"), 10 * 16)
            nc.tensor.matmul(bank(6)[0:1, 0:2 * S], emb[:, :], cf[0:BUCKETS, C_ONEHOT:C_ONEHOT + 2 * S],
                             start=True, stop=True).then_inc(sem("gp_p"), 1)
            nc.tensor.transpose(bank(7)[:, 0:45], vecs[0:45, :], ident[0:45, 0:45]).then_inc(sem("vT"), 1)
            pe.wait_ge(sem("w0_w"), 64)
            pe.wait_ge(sem("vcol"), 1)
            pe.wait_ge(sem("gp"), 1)
            pe_absorb(pe, "w0")
            pe.wait_ge(sem("wTs"), 6 * 0 + 6)
            for b in range(B):
                pe.wait_ge(sem(f"tail{b // 2}"), 64)
                if b >= 4:
                    pe.wait_ge(sem("ctx_tl"), b - 3)
                for c in range(TAILS):
                    _, n = chunk(TAIL0 + c)
                    ins = nc.tensor.transpose(bank(b % 4)[0:CD, c * P:c * P + n], tail_raw[0:n, b, c, :],
                                              ident[0:n, 0:n])
                ins.then_inc(sem("ctx_tp"), 1)
            pe.wait_ge(sem("abs"), 8 * 0 + 8)
            pe.wait_ge(sem("flag_c"), 1)
            nc.tensor.transpose(bank(7)[0:1, 256:256 + S], flag_c[:, :], ident[0:S, 0:S]).then_inc(sem("flag_T"), 1)
            pe.wait_ge(sem("ln_rows"), nth("l0b"))
            pe_rows_T(pe, yn, bank(6), sem("ln_T"))
            pe.wait_ge(sem("ctx_tl"), B)
            pe_queries(pe, "w0", (sem("yT0"), 1))
            pe.wait_ge(sem("ql"), 16 * 0 + HEADS)
            pe.wait_ge(sem("ctx_nl"), B)
            pe.wait_ge(sem("fills"), 5)
            pe.wait_ge(sem("maskb"), 1)
            pe.wait_ge(sem("flag"), 1)
            either(pe, pe_attention)
            pe.wait_ge(sem("x0_done"), 1)
            pe.wait_ge(sem("small"), 16 * 8)
            pe_heads_out(pe, "a0", 1, (bank(0), bank(6)))
            pe.wait_ge(sem("mid"), 16 * 5)
            pe_rows_T(pe, sraw, bank(2), sem("sT"))
            pe.wait_ge(sem("ln_rows"), nth("l1"))
            pe_rows_T(pe, yn, bank(0), sem("ln_T"))
            pe.wait_ge(sem("yT1"), 1)
            pe.wait_ge(sem("sTs"), 2)
            nc.tensor.matmul(bank(1), qkvT[:, 0:D], yT[:, :], start=True, stop=True).then_inc(sem("lq"), 1)
            for t in range(TILES):
                nc.tensor.matmul(bank(2 + t)[:, 0:2 * D], yT[:, t * P:(t + 1) * P], qkvT[:, D:3 * D],
                                 start=True, stop=True).then_inc(sem("lkv"), 1)
            kk = tq[:, 512:1024].rearrange("p (t n) -> p t n", t=TILES)
            vv = tq[:, 1024:1536].rearrange("p (t n) -> p t n", t=TILES)
            kvm = tq[:, 2048:3072].rearrange("p (b n) -> p b n", b=B)
            ksm = tq[:, 3072:4096].rearrange("p (b n) -> p b n", b=B)
            pe.wait_ge(sem("lkvs"), TILES)
            pe.wait_ge(sem("lqs"), 1)
            for odd in range(2):
                r = slice(S * odd, S * odd + S)
                for t in range(TILES):
                    ins = nc.tensor.matmul(bank(odd)[:, t * P:(t + 1) * P], kk[r, t, :], vv[r, t, :],
                                           start=True, stop=True)
                ins.then_inc(sem("kv"), 1)
                for t in range(TILES):
                    ins = nc.tensor.matmul(bank(2 + odd)[:, t:t + 1], kk[r, t, :], cf[r, C_ONE:C_ONE + 1],
                                           start=True, stop=True)
                ins.then_inc(sem("ks"), 1)
            pe.wait_ge(sem("kvm"), 2)
            for b in range(B):
                q = tq[:, b * S:(b + 1) * S]
                nc.tensor.matmul(bank(4)[:, b * S:(b + 1) * S], kvm[:, b, :], q, start=True, stop=True)
                ins = nc.tensor.matmul(bank(5)[:, b * S:(b + 1) * S], ksm[:, b, :], q, start=True, stop=True)
            ins.then_inc(sem("lden"), 1)
            pe.wait_ge(sem("rat"), 1)
            for t in range(TILES):
                o = bank(6)[:, t * P:(t + 1) * P]
                nc.tensor.matmul(o, tl[:, 512 + t * P:512 + (t + 1) * P], projT[:, :], start=True, stop=False)
                ins = nc.tensor.matmul(o, ones1, rows1[:, 0:D], start=False, stop=True)
            ins.then_inc(sem("a1_y"), 1)
            pe.wait_ge(sem("fw"), 6)
            for k in range(3):
                for g in range(3):
                    ins = nc.tensor.transpose(bank(k)[:, g * P:(g + 1) * P], ffraw[:, 3 * k + g, :], ident)
                ins.then_inc(sem("fwT"), 1)
            pe.wait_ge(sem("ln_rows"), nth("l2"))
            pe_rows_T(pe, yn, bank(6), sem("ln_T"))
            pe_scales(pe, 1, 1)
            pe.wait_ge(sem("fy"), 2)
            pe.wait_ge(sem("fwTs"), 3)
            for k in range(3):
                nc.tensor.matmul(bank(k), ffT[:, k, :], yT[:, :], start=True, stop=True).then_inc(sem("fg"), 1)
            for k in range(3):
                nc.tensor.matmul(bank(3 + k), ffT[:, 3 + k, :], yT[:, :], start=True, stop=True).then_inc(sem("fu"), 1)
            pe_scales(pe, 2, 2)
            pe_scales(pe, 1, 3)
            pe_scales(pe, 1, 4)
            pe.wait_ge(sem("fo"), 1)
            gs = tl[:, 1536:3072]
            for t in range(TILES):
                for k in range(FC):
                    ins = nc.tensor.matmul(bank(6)[:, t * P:(t + 1) * P], gs[:, k * TOK + t * P:k * TOK + (t + 1) * P],
                                           ffT[:, 6 + k, :], start=(k == 0), stop=(k == FC - 1))
            ins.then_inc(sem("a2_y"), 1)
            pe.wait_ge(sem("w1_w"), 64)
            pe.wait_ge(sem("x_a2"), 1)
            pe_absorb(pe, "w1")
            pe.wait_ge(sem("abs"), 8 * 1 + 8)
            pe.wait_ge(sem("ln_rows"), nth("l3"))
            pe_rows_T(pe, yn, bank(6), sem("ln_T"))
            pe_queries(pe, "w1", (sem("yT3"), 1))
            pe.wait_ge(sem("ql"), 16 * 1 + HEADS)
            pe_attention(pe, att1)
            pe.wait_ge(sem("x1_done"), 1)
            pe_heads_out(pe, "a3", 2, (bank(0), bank(6)))
            pe.wait_ge(sem("ln_rows"), nth("l4"))
            pe_rows_T(pe, yn, bank(0), sem("ln_T"))
            pe.wait_ge(sem("hank"), 16)
            nc.tensor.matmul(bank(7)[:, 0:S], cf[0:S, C_FLIP:C_FLIP + P], hank[:, :], start=True, stop=True)\
                .then_inc(sem("biasT"), 1)
            pe.wait_ge(sem("yT4"), 1)
            nc.tensor.matmul(bank(1), wqk1[:, 0, :], yT[:, :], start=True, stop=True).then_inc(sem("sqk"), 1)
            for t in range(TILES):
                o = bank(2)[:, t * P:(t + 1) * P]
                nc.tensor.matmul(o, yT[:, t * P:(t + 1) * P], wqk1[:, 1, :], start=True, stop=False)
                ins = nc.tensor.matmul(o, ones1, rows1[:, D:2 * D], start=False, stop=True)
            ins.then_inc(sem("sv"), 1)
            pe.wait_ge(sem("sqks"), 1)
            for t in range(TILES):
                c = slice(t * P, (t + 1) * P)
                ins = nc.tensor.matmul(bank(3)[:, c], tq[:, 1536 + t * P:1536 + (t + 1) * P],
                                       tq[:, 1024 + t * P:1024 + (t + 1) * P], start=True, stop=True)
            ins.then_inc(sem("sim"), 1)
            pe.wait_ge(sem("attn"), 1)
            pe.wait_ge(sem("svr"), 1)
            for t in range(TILES):
                ins = nc.tensor.matmul(bank(6)[:, t * P:(t + 1) * P], tl[:, 2560 + t * P:2560 + (t + 1) * P],
                                       tl[:, 512 + t * P:512 + (t + 1) * P], start=True, stop=True)
            ins.then_inc(sem("a4_y"), 1)
            pe.wait_ge(sem("ln_rows"), nth("l5"))
            pe_rows_T(pe, yn, bank(0), sem("ln_T"))
            pe.wait_ge(sem("yT5"), 1)
            for t in range(TILES):
                o = bank(1)[:, t * EXPERTS:(t + 1) * EXPERTS]
                nc.tensor.matmul(o, yT[:, t * P:(t + 1) * P], rw[:, :], start=True, stop=False)
                ins = nc.tensor.matmul(o, ones1, rb[:, :], start=False, stop=True)
            ins.then_inc(sem("rlog"), 1)
            pe.wait_ge(sem("oh"), 1)
            for t in range(TILES):
                o = bank(2)[:, t * EXPERTS:(t + 1) * EXPERTS]
                for u in range(t):
                    nc.tensor.matmul(o, ch[:, H_ONES:H_ONES + P], Pl[:, u * EXPERTS:(u + 1) * EXPERTS],
                                     start=(u == 0), stop=False)
                ins = nc.tensor.matmul(o, ch[:, H_TRI:H_TRI + P], Pl[:, t * EXPERTS:(t + 1) * EXPERTS],
                                       start=(t == 0), stop=True)
            ins.then_inc(sem("rank"), 1)
            pe.wait_ge(sem("sel"), 1)
            for t in range(TILES):
                ins = nc.tensor.transpose(bank(3).bitcast(F16)[0:SELS, t * P:(t + 1) * P],
                                          Pl[:, 32 + t * SELS:32 + (t + 1) * SELS], ident16)
            ins.then_inc(sem("selT"), 1)
            pe.wait_ge(sem("selT_s"), 2)
            pe.wait_ge(sem("x_a4"), 1)

            def expert_out(k):
                e, c = divmod(k, HC)
                if k % 2 == 0:
                    pe.wait_ge(sem("hid_a"), k // 2 + 1)
                else:
                    pe.wait_ge(sem("hid_d"), k // 2 + 1)
                for t in range(TILES):
                    at = (k % 4) * HALF + t * P
                    ins = nc.tensor.matmul(bank(6)[:, t * P:(t + 1) * P], tl[:, at:at + P], w2[:, e, c, :],
                                           start=False, stop=(k == SELS * HC - 1), skip_group_check=True)
                ins.then_inc(sem("hid_used"), 1)
                return ins

            for t in range(TILES):
                nc.tensor.matmul(bank(6)[:, t * P:(t + 1) * P], tq[0:SELS, t * P:(t + 1) * P], b2r[:, :],
                                 start=(t == 0), stop=False, skip_group_check=True)
            for k in range(SELS * HC):
                e, c = divmod(k, HC)
                if c == 0:
                    pe.wait_ge(sem(f"ex{e}"), 32)
                if k >= 4:
                    if k % 2 == 0:
                        pe.wait_ge(sem("hid_a"), (k - 4) // 2 + 1)
                    else:
                        pe.wait_ge(sem("hid_d"), (k - 4) // 2 + 1)
                o = bank(2 + k % 4)
                nc.tensor.matmul(o, ch[0:SELS, H_ROW + e * P:H_ROW + (e + 1) * P], Ph[0:SELS, 1024:1024 + TOK],
                                 start=True, stop=False)
                nc.tensor.matmul(o, w1[:, e, c * P:(c + 1) * P], yT[:, :], start=False, stop=True)\
                    .then_inc(sem("hid"), 1)
                if k >= 2:
                    expert_out(k - 2)
            expert_out(SELS * HC - 2)
            ins = expert_out(SELS * HC - 1)
            pe.wait_ge(sem("hid_used"), SELS * HC)
            nc.tensor.matmul(bank(7)[0:1, 0:1], ones1[:, 0:1], ones1[:, 0:1], start=True, stop=True)\
                .then_inc(sem("a5_y"), 1)


_INS = ['x', 'ctx_768', 'mask_1x1xSxS2_bk0', 'L0_xattn_ln_gamma', 'L0_xattn_ln_beta', 'L0_xattn_Wq',
        'L0_xattn_Wkv', 'L0_xattn_Wo', 'L0_xattn_bo', 'L0_attn_qkv_weight', 'L0_attn_proj_weight',
        'L0_attn_proj_bias', 'L0_ffn_w_gate', 'L0_ffn_w_up', 'L0_ffn_w_down', 'L1_xattn_Wq', 'L1_xattn_Wk',
        'L1_xattn_Wv', 'L1_xattn_Wo', 'L1_xattn_bo', 'L1_attn_Wqk', 'L1_attn_bqk', 'L1_attn_gamma',
        'L1_attn_beta', 'L1_attn_Wv', 'L1_attn_bv', 'L1_attn_rel_emb', 'L1_ffn_router_w', 'L1_ffn_router_b',
        'L1_ffn_w1', 'L1_ffn_b1', 'L1_ffn_w2', 'L1_ffn_b2', 'L1_ffn_ow1', 'L1_ffn_ob1', 'L1_ffn_ow2',
        'L1_ffn_ob2']


def kernel(**inputs):
    import numpy as _np
    import concourse.bacc as _bacc
    from concourse import mybir as _mybir
    from concourse.bass_utils import run_bass_kernel_spmd as _run

    nc = _bacc.Bacc("TRN2", target_bir_lowering=False, num_devices=1)
    arrays, args = {}, {}
    c, h = constants()
    given = {n: _np.ascontiguousarray(inputs[n]) for n in _INS} | {"cf": c, "ch": h}
    for name, v in given.items():
        arrays[f"in_{name}_dram"] = v
        args[name] = nc.dram_tensor(f"in_{name}_dram", v.shape, _mybir.dt.from_np(v.dtype),
                                    kind="ExternalInput").ap()
    o = nc.dram_tensor("out_0_dram", (B, S, D), F32, kind="ExternalOutput").ap()
    perceiver(nc, args, o)
    r = _run(nc, [arrays], core_ids=[0])
    return r.results[0]["out_0_dram"]
```

```python
from contextlib import ExitStack

import numpy as np

import concourse.bass as bass
from concourse import mybir

F32 = mybir.dt.float32
F16 = mybir.dt.float16
U8 = mybir.dt.uint8
I32 = mybir.dt.int32
ALU = mybir.AluOpType
ACT = mybir.ActivationFunctionType
X = mybir.AxisListType.X

P = 128
B, S, D = 8, 64, 128
TOK = B * S
TILES = TOK // P
KEYS, CD = 1601, 96
HEADS, DH = 16, 64
ROWS = HEADS * S
BLOCKS = ROWS // P
HALF = 512
KPAD = 1602
NCH = -(-KEYS // P)
CPAD = CD + 2
SHIFT = CD
NSH = BLOCKS
KS = CD + NSH
TAIL0 = 9
TAILS = NCH - TAIL0
GROUP = 3
GROUPS = TAIL0 // GROUP
LAST = KEYS - (NCH - 1) * P
FF = 384
FC = FF // P
WBLK = 32
EXPERTS, CAP, HID = 8, 160, 512
HC = HID // P
V_B1 = 7
V_BO = V_B1 + (EXPERTS + 1) * HC
V_B2 = V_BO + 2
VECS = V_B2 + EXPERTS + 1
SELS = EXPERTS + 1
NEG = -60000.0
BIG = 32768.0
MAGIC = 12582912.0
LN_EPS = 1e-5
RSCALE = 256.0
BUCKETS, MAXD = 32, 128
MU = float(np.sqrt(0.5))
ERF_A = 1.0 / float(np.sqrt(0.25 * np.pi) * np.sqrt(2.0))
ERF_P = 0.3275911
ERF_C = (0.254829592, -0.284496736, 1.421413741, -1.453152027, 1.061405429)

C_ID, C_BLK, C_CAUSAL, C_NDELTA, C_DELTA, C_FIRST, C_ONE, C_ONEHOT, C_FLIP = np.cumsum(
    [0, 128, 128, 128, 8, 9, 8, 128, 128]).tolist()
C_END = C_FLIP + 128
H_ID, H_ONES, H_TRI, H_INV, H_NEG, H_IND, H_ROW = np.cumsum([0, 128, 128, 128, CD, CD, 512]).tolist()
H_END = H_ROW + SELS * 128


def constants():
    c = np.zeros((P, C_END), np.float32)
    h = np.zeros((P, H_END), np.float16)
    i = np.arange(P)
    c[:, C_ID:C_ID + P] = np.eye(P)
    c[:, C_BLK:C_BLK + P] = i[:, None] // 4 == i[None] // 4
    key, query = i[:, None], i[None]
    c[:, C_CAUSAL:C_CAUSAL + P] = (key // S == query // S) & (key <= query)
    c[SHIFT:SHIFT + NSH, C_NDELTA:C_NDELTA + NSH] = -np.eye(NSH)
    c[:2 * NSH, C_DELTA:C_DELTA + NSH] = np.concatenate([-np.eye(NSH), np.eye(NSH)])
    c[NSH:2 * NSH, C_DELTA + NSH] = RSCALE
    c[:, C_FIRST:C_FIRST + EXPERTS] = EXPERTS - np.arange(EXPERTS)
    c[:, C_ONE:C_ONE + P] = 1.0
    n = np.maximum(np.arange(2 * S) - (S - 1), 0)
    exact = BUCKETS // 2
    large = exact + (np.log(np.maximum(n, 1).astype(np.float32) / exact) / np.log(MAXD / exact)
                     * (BUCKETS - exact)).astype(np.int32)
    bucket = np.where(n < exact, n, np.minimum(large, BUCKETS - 1))
    c[:BUCKETS, C_ONEHOT:C_ONEHOT + 2 * S] = np.arange(BUCKETS)[:, None] == bucket[None]
    c[:S, C_FLIP:C_FLIP + P] = np.arange(S)[:, None] == S - 1 - i[None] % S
    h[:, H_ID:H_ID + P] = np.eye(P)
    h[:, H_ONES:H_ONES + P] = 1.0
    h[:CD, H_NEG:H_NEG + CD] = -np.eye(CD)
    h[:, H_INV:H_INV + CD] = 1 / RSCALE
    h[:, H_TRI:H_TRI + P] = i[:, None] <= i[None]
    h[:S, H_IND:H_IND + HALF] = (np.arange(HALF)[None] % S == np.arange(S)[:, None]) * BIG
    for e in range(SELS):
        h[e, H_ROW + e * P:H_ROW + (e + 1) * P] = 1.0
    return c, h


def chunk(c):
    return c * P, min(P, KEYS - c * P)


def slices(lo, hi, most=HALF):
    n = -(-(hi - lo) // most)
    w = -(-(hi - lo) // n)
    return [(min(lo + w * i, hi - w), w) for i in range(n)]


def perceiver(nc, a, out):
    ctx = ExitStack()
    with ctx:
        def sb(name, shape, dt=F32):
            return ctx.enter_context(nc.sbuf_tensor(name, shape, dt))

        sems = {}

        def sem(name):
            if name not in sems:
                sems[name] = ctx.enter_context(nc.semaphore(name))
            return sems[name]

        ctxTh = sb("ctxTh", [P, B * KPAD], F16)
        ctxTl = sb("ctxTl", [P, B * KPAD], F16)
        ctxNh = sb("ctxNh", [P, B * NCH * CPAD], F16)
        ctxNl = sb("ctxNl", [P, B * NCH * CPAD], F16)
        Qh = sb("Qh", [P, B * ROWS], F16)
        Ql = sb("Ql", [P, B * ROWS], F16)
        maskb = sb("maskb", [P, KPAD], F16)
        pool32 = sb("pool32", [P, 11 * 1024])
        P32 = pool32[:, 0:2048]
        rawO = pool32[:, 2048:3072]
        Ph = sb("Ph", [P, 2 * ROWS], F16)
        Pl = sb("Pl", [P, 2 * ROWS], F16)
        On = pool32[:, 3072:3072 + HEADS * TOK].rearrange("p (b h s) -> p b h s", b=B, h=HEADS)
        wraw = pool32[:, 3072:]
        Wq = wraw[:, 0:1024]
        Wk = wraw[:, 1024:2048]
        Wv = wraw[:, 2048:3072]
        Wo = wraw[:, 3072:4096].rearrange("p (g n) -> p g n", g=8)
        WqT = wraw[:, 4096:5120].rearrange("p (g n) -> p g n", g=8)
        WkT = wraw[:, 5120:5120 + 8 * CD].rearrange("p (g n) -> p g n", g=8)
        WvT = wraw[:, 6144:6144 + 8 * CD].rearrange("p (g n) -> p g n", g=8)
        tail_raw = pool32[:, 0:B * TAILS * CD].rearrange("p (b c d) -> p b c d", b=B, c=TAILS)
        head_raw = [pool32[:, 3072 + (B - 2 + r) * ROWS:3072 + (B - 2 + r) * ROWS + TAIL0 * CD]
                    .rearrange("p (c d) -> p c d", c=TAIL0) for r in range(2)]
        Ah = wraw[:, 0:HEADS * CD].rearrange("p (h n) -> p h n", h=HEADS)
        Bh = sb("Bh", [P, HEADS, D])
        xs = sb("xs", [P, TILES, D])
        rows = sb("rows", [P, 2 * TOK])
        yn = rows[:, 0:TOK].rearrange("p (t n) -> p t n", t=TILES)
        yT = rows[:, TOK:2 * TOK]
        cf = sb("cf", [P, C_END])
        ch = sb("ch", [P, H_END], F16)
        vecs = sb("vecs", [64, D])
        vcol = sb("vcol", [P, 64])
        ghalf = sb("ghalf", [P, 2])
        rows1 = sb("rows1", [1, 2 * D + EXPERTS])
        mask8 = Pl[0:S, :].bitcast(U8)[:, 0:KEYS]
        st = sb("st", [P, TILES, 6])
        mv = sb("mv", [P, TILES, 2])
        ve = sb("ve", [P, TILES])
        mhalf = sb("mhalf", [P, TILES])
        rstd = sb("rstd", [P, TILES])
        mx = sb("mx", [P, BLOCKS * 4])
        m8 = sb("m8", [P, BLOCKS])
        rsum = sb("rsum", [2 * BLOCKS, P])
        rhigh = sb("rhigh", [2 * BLOCKS, P], F16)
        rpart = sb("rpart", [2 * BLOCKS, P], F16)
        rsel = rows[0:2 * BLOCKS, 0:HALF].bitcast(F16)
        m16 = sb("m16", [P, BLOCKS], F16)
        tq = Qh[:, :].bitcast(F32)
        tl = Ql[:, :].bitcast(F32)
        tp = Ph[:, :].bitcast(F32)
        qkvT = P32[:, 1152:1536]
        projT = P32[:, 1536:1664]
        ffraw = tl[:, 2944:4096].rearrange("p (g n) -> p g n", n=P)
        ffT = P32[:, 0:1152].rearrange("p (g n) -> p g n", n=P)
        fsc = sb("fsc", [P, 36])
        fin = sb("fin", [P, 36])
        sraw = tl[:, 2432:2944].rearrange("p (g n) -> p g n", n=P)
        wqk1 = sb("wqk1", [P, 2, D])
        rw = sb("rw", [P, EXPERTS])
        emb = sb("emb", [BUCKETS, 1])
        gp = sb("gp", [1, 2 * S])
        hank = sb("hank", [S, S])
        biasz = sb("biasz", [P, S])
        gq = sb("gq", [P, 8])
        gr = sb("gr", [2, 8])
        gu = sb("gu", [P, 4])
        magic = sb("magic", [P, 2])
        EW = HID + HC * D
        wraw32 = [(ctxTh if e < 6 else ctxTl)[:, 2 * EW * (e % 6):2 * EW * (e % 6 + 1)].bitcast(F32) for e in range(SELS)]
        whigh = [ctxNh[:, EW * e:EW * (e + 1)] for e in range(SELS)]
        wlow = [ctxNl[:, EW * e:EW * (e + 1)] for e in range(SELS)]
        hid32 = tl[:, 0:2 * TOK].rearrange("p (k t) -> p k t", k=2)
        hid_hi = tl[:, 1024:2048].bitcast(F16).rearrange("p (k t) -> p k t", k=4)
        hid_lo = tl[:, 2048:3072].bitcast(F16).rearrange("p (k t) -> p k t", k=4)
        yTh = tl[:, 3072:3328].bitcast(F16)
        yTl = tl[:, 3328:3584].bitcast(F16)
        selT16 = Ph[0:SELS, 2 * TOK:3 * TOK]
        total = tq[:, 0:TOK]
        prod = [tq[:, TOK:2 * TOK], tq[:, 2 * TOK:3 * TOK]]
        sel_b = [tq[:, 3 * TOK:4 * TOK].bitcast(F16)[:, k * TOK:(k + 1) * TOK] for k in range(2)]
        scratch = nc.dram_tensor("bias_row", (2 * S,), F32, kind="Internal").ap()

        PS = ctx.enter_context(nc.psum_tensor("PS", [P, 8 * HALF], F32))
        PO = PS[:, 2048:3072]

        def bank(k):
            return PS[:, k * HALF:(k + 1) * HALF]

        MISC = [bank(6), bank(7)]
        seq_q = [tq[:, at:at + TOK].rearrange("p (t o s) -> p t o s", t=TILES, o=2) for at in (0, 1536)]
        BVO = [6, 8, 10, 12]
        FB = [4, 5, 7]
        HB = [4, 5, 2, 3]
        ident = cf[:, C_ID:C_ID + P]
        ident16 = ch[:, H_ID:H_ID + P]
        ones1 = cf[0:1, C_ONE:C_ONE + P]

        block = ctx.enter_context(nc.Block())

        class Att:

            def __init__(self, name, chunks, masked):
                self.name, self.chunks, self.masked = name, chunks, masked
                self.layer = int(name[1])
                self.n = len(chunks)
                self.slices = slices(chunks[0] * P, KEYS)
                self.units = BLOCKS * len(self.slices)
                self.parts, self.width = (2, 2) if len(self.slices) == 4 else (1, 1)
                self.prep = GROUPS if self.n < NCH else 0
                if self.prep:
                    self.per = [self.units] + [0] * (self.n - 1)
                    self.inverse_slot, self.norm_slot, self.shift_slot = 1, 3, 1
                else:
                    slots = self.n - 4
                    self.per = [self.units * (s + 1) // slots - self.units * s // slots if s < slots else 0
                                for s in range(self.n)]
                    self.inverse_slot, self.norm_slot, self.shift_slot = 9, 12, self.n - 3

            def extras(self, i, last):
                before = sum(self.per[:i])
                most = [] if last else [("max", u) for u in range(before, before + self.per[i])]
                return most + ([("prep", i - 1)] if self.prep and i else [])

            def max_used(self, i, first):
                used = 0
                for k in range(i):
                    used += 0 if first else 2 * (k == self.norm_slot)
                    used += len(self.extras(k, False))
                return used

            def sem(self, what):
                return sem(f"{self.name}_{what}")

            def base(self, b):
                first = BLOCKS * self.parts + 1
                if isinstance(b, int) and b == 0:
                    return first
                return first + self.units + 1 + self.prep + (b - 1) * (self.units + 3 + self.prep)

        def pe_max_unit(pe, t, nb, u, full_wait, spare):
            j, s = divmod(u, len(t.slices))
            k0, n = t.slices[s]
            if full_wait is not None:
                pe.wait_ge(t.sem("spare_read"), full_wait)
            o = spare[:, 0:n]
            ins = nc.tensor.matmul(o, Qh[0:CD, bass.ds(nb * ROWS + j * P, P)],
                                   ctxTh[0:CD, bass.ds(nb * KPAD + k0, n)], start=True, stop=not t.masked)
            if t.masked:
                ins = nc.tensor.matmul(o, ch[:, H_IND:H_IND + P], maskb[:, k0:k0 + n], start=False, stop=True)
            ins.then_inc(t.sem("spare_written"), 1)

        def pe_shift(pe, t, nb, full_wait, spare):
            pe.wait_ge(t.sem("max_ready"), nb + 1)
            pe.wait_ge(t.sem("spare_read"), full_wait)
            nc.tensor.transpose(spare.bitcast(F16)[SHIFT:SHIFT + NSH, 0:P], m16[:, :], ident16)\
                .then_inc(t.sem("spare_written"), 1)

        def pe_scores(pe, t, nb, c, par, half):
            k0, n = chunk(c)
            o = PS[0:n, bass.ds(par * ROWS + half * HALF, HALF)]
            q = nb * ROWS + half * HALF
            hi = ctxTh[0:KS, bass.ds(nb * KPAD + k0, n)]
            nc.tensor.matmul(o, hi, Qh[0:KS, bass.ds(q, HALF)], start=True, stop=False)
            nc.tensor.matmul(o, ctxTh[0:CD, bass.ds(nb * KPAD + k0, n)], Ql[0:CD, bass.ds(q, HALF)],
                             start=False, stop=False)
            ins = nc.tensor.matmul(o, ctxTl[0:CD, bass.ds(nb * KPAD + k0, n)], Qh[0:CD, bass.ds(q, HALF)],
                                   start=False, stop=not t.masked)
            if t.masked:
                ins = nc.tensor.matmul(o, maskb[:, k0:k0 + n], ch[:, H_IND:H_IND + HALF], start=False, stop=True)
            ins.then_inc(t.sem("scores"), 1)

        def pe_out(pe, t, nb, c, par, half, first, last):
            _, n = chunk(c)
            o = PO[0:CD + 1, half * HALF:(half + 1) * HALF]
            at = nb * (NCH * CPAD) + c * CPAD
            hi = ctxNh[0:n, bass.ds(at, CD + 1)]
            ph = Ph[0:n, bass.ds(par * ROWS + half * HALF, HALF)]
            nc.tensor.matmul(o, hi, ph, start=first, stop=False)
            nc.tensor.matmul(o, ctxNl[0:n, bass.ds(at, CD + 1)], ph, start=False, stop=False)
            return nc.tensor.matmul(o, hi, Pl[0:n, bass.ds(par * ROWS + half * HALF, HALF)],
                                    start=False, stop=last)

        def pe_spread(pe, t, half, spare):
            nc.tensor.matmul(spare[0:CD, :], ch[0:2 * BLOCKS, H_INV:H_INV + CD], rsel[:, half * HALF:(half + 1) * HALF],
                             start=True, stop=True).then_inc(t.sem("spare_written"), 1)

        def pe_sequence(pe, t, b, pars, first=False, last=False):
            g0 = b * t.n
            used = 0

            def spare():
                nonlocal used
                pe.wait_ge(t.sem("spare_read"), t.base(b) + (used - 1 if used else 0))
                used += 1
                return MISC[(used - 1) % 2]

            for i, c in enumerate(t.chunks):
                pi = pars[i % 2]
                ahead = i + 2
                nb, ci = (b, ahead) if ahead < t.n else (b + 1, ahead - t.n)
                if i == t.norm_slot and not first:
                    pe.wait_ge(t.sem("spread"), b)
                    for half in range(2):
                        pe_spread(pe, t, half, spare())
                if i == t.shift_slot and not last:
                    pe_shift(pe, t, b + 1, t.base(b) + used, MISC[used % 2])
                    used += 1
                extras = t.extras(i, last)

                def some():
                    if extras:
                        what, k = extras.pop(0)
                        if what == "max":
                            pe_max_unit(pe, t, b + 1, k, None, spare())
                        else:
                            pe_head_T(pe, b, k, spare()).then_inc(t.sem("spare_written"), 1)

                some()
                if not (last and nb is not b):
                    if ahead == t.n:
                        pe.wait_ge(t.sem("shift"), b + 2)
                    pe.wait_ge(t.sem("exp"), 2 * (g0 + i) + 1)
                    pe_scores(pe, t, nb, t.chunks[ci], pi, 0)
                    some()
                    pe.wait_ge(t.sem("exp"), 2 * (g0 + i) + 2)
                    pe_scores(pe, t, nb, t.chunks[ci], pi, 1)
                while len(extras) > 1:
                    some()
                for half in range(2):
                    pe.wait_ge(t.sem("p_high"), 2 * (g0 + i) + half + 1)
                    pe.wait_ge(t.sem("p_low"), 2 * (g0 + i) + half + 1)
                    if i == 0 and not first:
                        pe.wait_ge(t.sem("out_copied"), b)
                    pe_out(pe, t, b, c, pi, half, i == 0, i == t.n - 1).then_inc(t.sem("out"), 1)
                    some()

        def pe_heads_out(t, seqs, heads):
            o = bank(0)[:, seqs.start * S:seqs.stop * S]
            for h in heads:
                ins = nc.tensor.matmul(o, Bh[0:CD, h, :], On[0:CD, seqs, h, :], start=(h == 0), stop=(h == HEADS - 1))
            return ins

        def pe_block_maxima(pe, t, j):
            pe.wait_ge(sem("qh"), 16 * t.layer + 2 * j + 2)
            for u in range(j * t.parts, (j + 1) * t.parts):
                if u >= 2:
                    pe.wait_ge(t.sem("spare_read"), u - 1)
                for s in range(t.width):
                    k0, n = t.slices[u % t.parts * t.width + s]
                    o = bank(4 + u % 2 * t.width + s)[:, 0:n]
                    ins = nc.tensor.matmul(o, Qh[0:CD, j * P:(j + 1) * P], ctxTh[0:CD, k0:k0 + n],
                                           start=True, stop=not t.masked)
                    if t.masked:
                        ins = nc.tensor.matmul(o, ch[:, H_IND:H_IND + P], maskb[:, k0:k0 + n], start=False, stop=True)
                ins.then_inc(t.sem("spare_written"), 1)

        def dve_block_maxima(dve, t, j):
            for u in range(j * t.parts, (j + 1) * t.parts):
                dve.wait_ge(t.sem("spare_written"), u + 1)
                at = 4 + u % 2 * t.width
                src = PS[:, at * HALF:(at + t.width) * HALF].rearrange("p (s k) -> p s k", s=t.width)
                nc.vector.tensor_reduce(mx[:, t.width * u:t.width * (u + 1)], src[:, :, 0:t.slices[0][1]], X, ALU.max)\
                    .then_inc(t.sem("spare_read"), 1)

        def pe_attention(pe, t):
            if t is att0:
                pe_absorb(pe, "w0", 1, (bank(2), bank(3)))
                pe.wait_ge(sem("abs"), 8)
                pe_heads(pe, t)
            pe_queries(pe, t)
            pe_shift(pe, t, 0, BLOCKS * t.parts, MISC[0])
            pe.wait_ge(sem("ql"), HEADS + (HEADS // 2 if t is att1 else 0))
            if t is att1:
                pe.wait_ge(sem("ql_act"), HEADS // 2)
            pe.wait_ge(t.sem("shift"), 1)
            for i in range(2):
                for half in range(2):
                    pe_scores(pe, t, 0, t.chunks[i], i, half)
            if t is not att1:
                pe.wait_ge(sem("ctx_nl"), B)
            pe_sequence(pe, t, 0, (0, 1), first=True)
            pe_sequence(pe, t, 1, parities(t, 1))
            with pe.Fori(0, (B - 4) // 2) as pair:
                b = pair * 2 + 2
                pe_sequence(pe, t, b, (0, 1))
                pe_sequence(pe, t, b + 1, parities(t, 1))
            pe_sequence(pe, t, B - 2, (0, 1))
            pe_sequence(pe, t, B - 1, parities(t, B - 1), last=True)
            ready = [slice(0, B - 2), slice(B - 2, B)]
            pe_heads_out(t, ready[0], range(0, 2))
            base = t.base(B - 1) + 2 + t.prep
            pe_heads_out(t, ready[0], range(2, 6))
            pe.wait_ge(t.sem("spread"), B)
            pe.wait_ge(t.sem("spare_read"), base)
            for half in range(2):
                pe_spread(pe, t, half, MISC[half])
            pe_heads_out(t, ready[0], range(6, HEADS))
            pe.wait_ge(t.sem("spare_read"), base + 2)
            pe_heads_out(t, ready[1], range(HEADS)).then_inc(sem("heads_p"), 1)

        def parities(t, b):
            return b * t.n % 2, (b * t.n + 1) % 2

        def act_sequence(act, t, b, pars, first=False):
            g0 = b * t.n
            for i, c in enumerate(t.chunks):
                pi = pars[i % 2]
                _, n = chunk(c)
                for half in range(2):
                    at = slice(pi * ROWS + half * HALF, pi * ROWS + (half + 1) * HALF)
                    done = 2 * (g0 + i) + half + 1
                    act.wait_ge(t.sem("scores"), done)
                    if not (first and i < 2):
                        act.wait_ge(t.sem("p_low"), done - 4)
                    nc.scalar.activation(P32[0:n, at], PS[0:n, at], ACT.Exp).then_inc(t.sem("exp"), 1)
                    act.wait_ge(t.sem("exp"), done)
                    if not (first and i < 2):
                        act.wait_ge(t.sem("out"), done - 4)
                    nc.scalar.activation(Ph[0:n, at], P32[0:n, at], ACT.Copy).then_inc(t.sem("p_high"), 1)
                if i == 0 and not first:
                    act_copy_out(act, t, b)

        def act_copy_out(act, t, b):
            act.wait_ge(t.sem("out"), 2 * b * t.n)
            if not (isinstance(b, int) and b == 1):
                act.wait_ge(t.sem("normed"), b - 1)
            nc.scalar.activation(rawO[0:CD + 1, :], PO[0:CD + 1, :], ACT.Copy).then_inc(t.sem("out_copied"), 1)

        def act_attention(act, t):
            if t is att0:
                act_products(act, "w0", range(4, 8), (bank(2), bank(3)))
            act_queries(act, t)
            if t is not att1:
                act.wait_ge(sem("ctx_nl"), B)
            act_sequence(act, t, 0, (0, 1), first=True)
            act_sequence(act, t, 1, parities(t, 1))
            with act.Fori(0, (B - 2) // 2) as pair:
                b = pair * 2 + 2
                act_sequence(act, t, b, (0, 1))
                act_sequence(act, t, b + 1, parities(t, 1))
            act_copy_out(act, t, B)

        def dve_max_unit(dve, t, u, count, spare):
            j, s = divmod(u, len(t.slices))
            dve.wait_ge(t.sem("spare_written"), count)
            nc.vector.tensor_reduce(mx[:, u:u + 1], spare[:, 0:t.slices[s][1]], X, ALU.max)\
                .then_inc(t.sem("spare_read"), 1)

        def dve_round(dve, t, nb, read):
            dve.wait_ge(t.sem("spare_read"), read)
            src = mx[:, 0:BLOCKS]
            if len(t.slices) > 1:
                nc.vector.tensor_reduce(m8[:, :], mx[:, 0:t.units].rearrange("p (j s) -> p j s", j=BLOCKS),
                                        X, ALU.max).then_inc(t.sem("max_whole"), 1)
                dve.wait_ge(t.sem("max_whole"), nb + 1)
                src = m8[:, :]
            nc.vector.tensor_scalar(m16[:, :], src, NEG, -NEG, ALU.max, ALU.min).then_inc(t.sem("max_ready"), 1)

        def dve_shift(dve, t, nb, count, spare):
            dve.wait_ge(t.sem("spare_written"), count)
            mt = spare.bitcast(F16)[SHIFT:SHIFT + NSH, 0:P]
            nc.vector.tensor_tensor(
                Qh[SHIFT:SHIFT + NSH, bass.ds(nb * ROWS, ROWS)].rearrange("p (j r) -> p j r", j=BLOCKS),
                mt.unsqueeze(1).to_broadcast([NSH, BLOCKS, P]),
                cf[SHIFT:SHIFT + NSH, C_NDELTA:C_NDELTA + NSH].unsqueeze(2).to_broadcast([NSH, BLOCKS, P]),
                ALU.mult).then_inc(t.sem("spare_read"), 1)
            dve.wait_ge(t.sem("spare_read"), count)
            nc.vector.tensor_copy(ve[0:1, 0:1], ve[0:1, 0:1]).then_inc(t.sem("shift"), 1)

        def dve_norm(dve, t, b, half, spare, count):
            dve.wait_ge(t.sem("spare_written"), count)
            nc.vector.tensor_tensor(
                On[0:CD, b - 1, half * 8:(half + 1) * 8, :] if isinstance(b, int) else
                pool32[0:CD, bass.ds((b - 1) * ROWS + 3072 + half * HALF, HALF)].rearrange("p (h s) -> p h s", h=8),
                spare[0:CD, :].rearrange("p (h s) -> p h s", h=8),
                rawO[0:CD, half * HALF:(half + 1) * HALF].rearrange("p (h s) -> p h s", h=8),
                ALU.mult).then_inc(t.sem("spare_read"), 1)

        def dve_inverse(dve, t, b):
            dve.wait_ge(t.sem("sums"), 32 * b)
            nc.vector.reciprocal(rsum[:, :], rsum[:, :]).then_inc(t.sem("inverse"), 1)
            dve.wait_ge(t.sem("inverse"), 3 * b - 2)
            nc.vector.tensor_scalar(rhigh[:, :], rsum[:, :], RSCALE, None, ALU.mult).then_inc(t.sem("inverse"), 1)
            dve.wait_ge(t.sem("inverse"), 3 * b - 1)
            nc.vector.scalar_tensor_tensor(rpart[:, :], rsum[:, :], cf[0:2 * BLOCKS, C_DELTA + NSH:C_DELTA + NSH + 1],
                                           rhigh[:, :], ALU.mult, ALU.subtract).then_inc(t.sem("inverse"), 1)

        def pool_place(pool, t, b):
            pool.wait_ge(t.sem("inverse"), 3 * (b + 1))
            nc.gpsimd.tensor_tensor(
                rsel[:, :].rearrange("p (j r) -> p j r", j=BLOCKS),
                rpart[:, :].unsqueeze(1).to_broadcast([2 * BLOCKS, BLOCKS, P]),
                cf[0:2 * BLOCKS, C_DELTA:C_DELTA + BLOCKS].unsqueeze(2).to_broadcast([2 * BLOCKS, BLOCKS, P]),
                ALU.mult).then_inc(t.sem("spread"), 1)

        def sp_sums(sp, t, b):
            sp.wait_ge(t.sem("out_copied"), b + 1)
            for k in range(2):
                sp.dma_start(rsum[k * BLOCKS:(k + 1) * BLOCKS, :],
                             rawO[CD:CD + 1, :].rearrange("o (j r) -> o j r", j=BLOCKS)).then_inc(t.sem("sums"), 16)

        def dve_sequence(dve, t, b, pars, first=False, last=False):
            g0 = b * t.n
            used = 0

            def spare():
                nonlocal used
                used += 1
                return MISC[(used - 1) % 2], t.base(b) + used

            for i, c in enumerate(t.chunks):
                pi = pars[i % 2]
                _, n = chunk(c)
                if i == t.shift_slot and not last:
                    dve_round(dve, t, b + 1, t.base(b) + t.max_used(i, first))
                for half in range(2):
                    at = slice(pi * ROWS + half * HALF, pi * ROWS + (half + 1) * HALF)
                    done = 2 * (g0 + i) + half + 1
                    dve.wait_ge(t.sem("p_high"), done)
                    if not (first and i < 2):
                        dve.wait_ge(t.sem("out"), done - 4)
                    nc.vector.tensor_tensor(Pl[0:n, at], P32[0:n, at], Ph[0:n, at], ALU.subtract)\
                        .then_inc(t.sem("p_low"), 1)
                if i == t.inverse_slot and not first:
                    dve_inverse(dve, t, b)
                if i == t.norm_slot and not first:
                    for half in range(2):
                        dve_norm(dve, t, b, half, *spare())
                    dve.wait_ge(t.sem("spare_read"), t.base(b) + used)
                    nc.vector.tensor_copy(ve[0:1, 0:1], ve[0:1, 0:1]).then_inc(t.sem("normed"), 1)
                if i == t.shift_slot and not last:
                    bank_, count = spare()
                    dve_shift(dve, t, b + 1, count, bank_)
                for what, k in t.extras(i, last):
                    bank_, count = spare()
                    if what == "max":
                        dve_max_unit(dve, t, k, count, bank_)
                    else:
                        dve.wait_ge(t.sem("spare_written"), count)
                        dve_head_T(dve, b, k, bank_).then_inc(t.sem("spare_read"), 1)

        def dve_attention(dve, t):
            if t is att0:
                dve_heads(dve, t)
            dve_queries(dve, t)
            dve_round(dve, t, 0, BLOCKS * t.parts)
            dve_shift(dve, t, 0, BLOCKS * t.parts + 1, MISC[0])
            dve_sequence(dve, t, 0, (0, 1), first=True)
            dve_sequence(dve, t, 1, parities(t, 1))
            with dve.Fori(0, (B - 4) // 2) as pair:
                b = pair * 2 + 2
                dve_sequence(dve, t, b, (0, 1))
                dve_sequence(dve, t, b + 1, parities(t, 1))
            dve_sequence(dve, t, B - 2, (0, 1))
            if t is not att1:
                dve.wait_ge(sem("ctx_nl"), 2 * B - 1)
            dve_sequence(dve, t, B - 1, parities(t, B - 1), last=True)
            if t is not att1:
                dve.wait_ge(sem("ctx_nl"), 2 * B)
            base = t.base(B - 1) + 2 + t.prep
            dve_inverse(dve, t, B)
            for half in range(2):
                dve_norm(dve, t, B, half, MISC[half], base + 1 + half)

        def pe_head_T(pe, k, g, o):
            if g == 0:
                pe.wait_ge(sem("ctx_nl"), k + B + 1)
            for part, src in enumerate((ctxNh, ctxNl)):
                for c in range(GROUP):
                    ins = nc.tensor.transpose(o.bitcast(F16)[0:CD, (part * GROUP + c) * P:(part * GROUP + c + 1) * P],
                                              src[:, bass.ds(k * (NCH * CPAD) + (g * GROUP + c) * CPAD, CD)], ident16)
            return ins

        def dve_head_T(dve, k, g, o):
            at = bass.ds(k * KPAD + g * GROUP * P, GROUP * P)
            o16 = o.bitcast(F16)[0:CD, 0:2 * GROUP * P]
            nc.vector.tensor_copy(ctxTh[0:CD, at], o16[:, 0:GROUP * P])
            return nc.vector.tensor_copy(ctxTl[0:CD, at], o16[:, GROUP * P:2 * GROUP * P])

        def pe_heads(pe, t):
            with pe.Fori(0, B) as k:
                for g in range(GROUPS):
                    pe.wait_ge(sem("ctx_tl"), k * GROUPS + g + B - GROUPS + 1)
                    pe_head_T(pe, k, g, bank(g)).then_inc(sem("head_tp"), 1)
            pe.wait_ge(sem("ctx_tl"), B + B * GROUPS)
        def dve_heads(dve, t):
            with dve.Fori(0, B) as k:
                for g in range(GROUPS):
                    dve.wait_ge(sem("head_tp"), k * GROUPS + g + 1)
                    dve_head_T(dve, k, g, bank(g)).then_inc(sem("ctx_tl"), 1)

        def pool_by_keys(b, raw, c0, n, done):
            h3 = ctxNh[:, :].rearrange("p (b c f) -> p b c f", b=B, c=NCH)[:, b]
            l3 = ctxNl[:, :].rearrange("p (b c f) -> p b c f", b=B, c=NCH)[:, b]
            parts = [(P, slice(c0, c0 + n), slice(0, n))]
            if c0 >= TAIL0:
                parts.append((LAST, slice(c0 + n, c0 + n + 1), slice(n, n + 1)))
            for k, c, rc in parts:
                nc.gpsimd.tensor_copy(h3[0:k, c, 0:CD], raw[0:k, rc, :]).then_inc(sem("ctx_nh"), 1)
            nc.gpsimd.wait_ge(sem("ctx_nh"), done)
            for k, c, rc in parts:
                ins = nc.gpsimd.tensor_tensor(l3[0:k, c, 0:CD], raw[0:k, rc, :], h3[0:k, c, 0:CD], ALU.subtract)
            ins.then_inc(sem("ctx_nl"), 1)

        def pool_head(pool, b):
            pool.wait_ge(sem(f"head{b % 2}"), 16 * (b // 2 + 1))
            pool_by_keys(b, head_raw[b % 2], 0, TAIL0, 2 * B + b + 1)

        def pool_attention(pool, t):
            ahead = {id(att0): B, id(att0s): 3, id(att1): 0}[id(t)]
            for b in range(ahead):
                pool_head(pool, b)
            for b in range(B):
                pool_place(pool, t, b)
                if t is att0s and b + ahead < B:
                    pool_head(pool, b + ahead)

        def sp_attention(sp, t):
            for b in range(2 if t is att0s else B):
                if t is not att1:
                    sp_head(sp, b)
            for b in range(B):
                if t is att0s and b + 2 < B:
                    sp_head(sp, b + 2)
                sp_sums(sp, t, b)

        def sp_head(sp, b):
            if b >= 2:
                sp.wait_ge(sem("ctx_nl"), B + b - 1)
            sp.dma_start(head_raw[b % 2][:, :, :],
                         a["ctx_768"][b][0:TAIL0 * P, :].rearrange("(c p) d -> p c d", p=P))\
                .then_inc(sem(f"head{b % 2}"), 16)

        att0 = Att("x0", list(range(NCH)), True)
        att0s = Att("x0", list(range(TAIL0, NCH)), True)
        att1 = Att("x1", list(range(NCH)), False)

        def either(eng, run):
            eng.wait_ge(sem("flag"), 1)
            v = eng.value_load(flag_i[0:1, 0:1], min_val=0, max_val=1)
            with eng.If(v > 0):
                run(eng, att0)
            with eng.Else():
                run(eng, att0s)

        flag_i = sb("flag_i", [1, 1], I32)
        flag_c = sb("flag_c", [S, 1])
        flag_r = sb("flag_r", [1, 1])

        LNS = ["l0a", "l0b", "l1", "l2", "l3", "l4", "l5"]

        def nth(tag):
            return LNS.index(tag) + 1

        def dve_ln(dve, tag, src, ready):
            dve.wait_ge(*ready)
            for t in range(TILES):
                ins = nc.vector.bn_stats(st[:, t, :], src[:, t, :])
            ins.then_inc(sem("ln_stats"), 1)
            dve.wait_ge(sem("ln_stats"), 2 * nth(tag) - 1)
            for t in range(TILES):
                ins = nc.vector.bn_aggr(mv[:, t, :], st[:, t, :])
            ins.then_inc(sem("ln_stats"), 1)
            dve.wait_ge(sem("ln_stats"), 2 * nth(tag))
            nc.vector.tensor_scalar(ve[:, :], mv[:, :, 1], LN_EPS, None, ALU.add).then_inc(sem("ln_var"), 1)
            dve.wait_ge(sem("ln_rstd"), nth(tag))
            for t in range(TILES):
                ins = nc.vector.tensor_scalar(yn[:, t, :], src[:, t, :], mv[:, t, 0:1], rstd[:, t:t + 1],
                                              ALU.subtract, ALU.mult)
            ins.then_inc(sem("ln_rows"), 1)

        def pool_ln(pool, tag):
            pool.wait_ge(sem("ln_var"), nth(tag))
            nc.gpsimd.tensor_tensor(rstd[:, :], ve[:, :], mhalf[:, :], ALU.pow).then_inc(sem("ln_rstd"), 1)

        def pe_rows_T(pe, src, dst, done):
            for t in range(TILES):
                ins = nc.tensor.transpose(dst[:, t * P:(t + 1) * P], src[:, t, :], ident)
            ins.then_inc(done, 1)

        def dve_residual(dve, tag, o):
            dve.wait_ge(sem("y"), int(tag[1]) + 1)
            nc.vector.tensor_tensor(xs[:, :, :], xs[:, :, :], o.rearrange("p (t n) -> p t n", t=TILES), ALU.add)\
                .then_inc(sem("x_sum"), 1)

        def pe_rows_out(pe, tag, k):
            pe.wait_ge(sem("heads_s"), k)
            for u in range(TILES):
                ins = nc.tensor.transpose(bank(6)[:, u * P:(u + 1) * P], yT[:, u * P:(u + 1) * P], ident)
            ins.then_inc(sem("y"), 1)

        def act_heads_out(act, k, bias):
            act.wait_ge(sem("heads_p"), k)
            nc.scalar.activation(yT[:, :], bank(0), ACT.Identity, bias=bias).then_inc(sem("heads_s"), 1)

        def act_experts(act, e0, e1):
            for e in range(e0, e1):
                act.wait_ge(sem(f"ex{e}"), 32)
                nc.scalar.activation(whigh[e], wraw32[e], ACT.Copy).then_inc(sem("w_high"), 1)

        def pool_experts(pool, e0, e1):
            for e in range(e0, e1):
                pool.wait_ge(sem("w_high"), e + 1)
                nc.gpsimd.tensor_tensor(wlow[e], wraw32[e], whigh[e], ALU.subtract).then_inc(sem("w_low"), 1)

        def layer(tag):
            return int(tag[1])

        def pe_weights_T(pe, tag, banks, first=0):
            for i in range(4 * first, 4 * (first + len(banks))):
                g, which = i % 8, i // 8
                src, rows = ((Wq, P), (Wk, CD), (Wv, CD))[which]
                nc.tensor.transpose(bank(banks[i // 4 - first])[:, (i % 4) * P:(i % 4) * P + rows],
                                    src[0:rows, g * P:(g + 1) * P], ident[0:rows, 0:rows])\
                    .then_inc(sem("wT"), 1)

        def pe_absorb(pe, tag, which, banks, parts=range(4)):
            pe.wait_ge(sem("wTs"), 6 * layer(tag) + (6 if which else 4))
            for k in parts:
                o = banks[k % len(banks)]
                if len(banks) == 2 and (which or k >= 2):
                    pe.wait_ge(sem("abs"), 8 * layer(tag) + 4 * which + max(k - 1, 0))
                for i in range(4):
                    h = 8 * (k // 2) + 2 * i + k % 2
                    r = slice(DH * (h % 2), DH * (h % 2) + DH)
                    if which == 0:
                        ins = nc.tensor.matmul(o[:, i * P:i * P + CD], WqT[r, h // 2, :], WkT[r, h // 2, :],
                                               start=True, stop=True)
                    else:
                        ins = nc.tensor.matmul(o[0:CD, i * P:(i + 1) * P], WvT[r, h // 2, :], Wo[r, h // 2, :],
                                               start=True, stop=True)
                ins.then_inc(sem("absp"), 1)

        def act_absorb(act, tag, banks, parts=range(6)):
            for i in parts:
                act.wait_ge(sem("wT"), 24 * layer(tag) + 4 * (i + 1))
                dst, rows = ((WqT, P), (WkT, CD), (WvT, CD))[i // 2]
                src = bank(banks[i]).rearrange("p (g n) -> p g n", g=4)[:, :, 0:rows]
                nc.scalar.activation(dst[:, 4 * (i % 2):4 * (i % 2) + 4, :], src, ACT.Copy)\
                    .then_inc(sem("wTs"), 1)

        def copy_absorb(eng, parts, copy, tag, banks):
            for k in parts:
                eng.wait_ge(sem("absp"), 8 * layer(tag) + k + 1)
                h0 = 8 * (k % 4 // 2) + k % 2
                src = banks[k % len(banks)].rearrange("p (g n) -> p g n", g=4)
                if k < 4:
                    copy(Ah[:, h0:h0 + 7:2, :], src[:, :, 0:CD], DH ** -0.5).then_inc(sem("abs"), 1)
                else:
                    copy(Bh[0:CD, h0:h0 + 7:2, :], src[0:CD, :, :], 1.0).then_inc(sem("abs"), 1)

        def dve_absorb(dve):
            copy_absorb(dve, range(4), lambda o, i, f: nc.vector.tensor_scalar(o, i, f, None, ALU.mult), "w0", [bank(k) for k in range(4, 8)])

        def act_products(act, tag, parts, banks):
            copy_absorb(act, parts, lambda o, i, f: nc.scalar.activation(o, i, ACT.Copy, scale=f), tag, banks)

        def pe_queries(pe, t):
            def rest(h):
                pe.wait_ge(sem("qh"), 16 * t.layer + h + 1)
                nc.tensor.matmul(bank(h % 4)[0:CD, :], ch[0:CD, H_NEG:H_NEG + CD], q_view(Qh, h), start=False,
                                 stop=True, skip_group_check=True).then_inc(sem("q_rest"), 1)

            for h in range(HEADS):
                if h >= 4:
                    if t is not att1:
                        pe.wait_ge(sem("ql"), h - 3)
                    elif h % 2 == 0:
                        pe.wait_ge(sem("ql"), 16 + h // 2 - 1)
                    else:
                        pe.wait_ge(sem("ql_act"), h // 2 - 1)
                nc.tensor.matmul(bank(h % 4)[0:CD, :], Ah[:, h, :], yT[:, :], start=True, stop=True)\
                    .then_inc(sem("q"), 1)
                if t is att1 and h % 2 == 0 and h:
                    rest(h - 1)
                if h % 2 and h > 1:
                    pe_block_maxima(pe, t, h // 2 - 1)
                if t is att0s and h in BVO:
                    pe_absorb(pe, "w0", 1, MISC, [BVO.index(h)])
            if t is att1:
                rest(HEADS - 1)
            pe_block_maxima(pe, t, BLOCKS - 1)

        def q_view(t, h):
            return t[0:CD, :].rearrange("p (b r) -> p b r", b=B)[:, :, h * S:(h + 1) * S]

        def act_queries(act, t):
            def low(h):
                act.wait_ge(sem("q_rest"), h // 2 + 1)
                nc.scalar.activation(q_view(Ql, h), bank(h % 4)[0:CD, :].rearrange("p (b s) -> p b s", b=B), ACT.Copy)\
                    .then_inc(sem("ql_act"), 1)

            for h in range(HEADS):
                act.wait_ge(sem("q"), 16 * t.layer + h + 1)
                nc.scalar.activation(q_view(Qh, h), bank(h % 4)[0:CD, :].rearrange("p (b s) -> p b s", b=B), ACT.Copy)\
                    .then_inc(sem("qh"), 1)
                if t is att1 and h % 2 == 0 and h:
                    low(h - 1)
                if t is att0s and h in BVO:
                    act_products(act, "w0", [4 + BVO.index(h)], MISC)
            if t is att1:
                low(HEADS - 1)

        def dve_queries(dve, t):
            for h in range(HEADS):
                if t is not att1 or h % 2 == 0:
                    dve.wait_ge(sem("qh"), 16 * t.layer + h + 1)
                    nc.vector.tensor_tensor(q_view(Ql, h), bank(h % 4)[0:CD, :].rearrange("p (b s) -> p b s", b=B),
                                            q_view(Qh, h), ALU.subtract).then_inc(sem("ql"), 1)
                if h % 2 and h > 1:
                    dve_block_maxima(dve, t, h // 2 - 1)
            dve_block_maxima(dve, t, BLOCKS - 1)

        def load_absorb(eng, tag, wq, wk, wv, wo):
            eng.dma_start(Wq, wq).then_inc(sem(tag + "_wqk"), 16)
            eng.dma_start(Wk[0:CD, :], wk).then_inc(sem(tag + "_wqk"), 16)
            eng.dma_start(Wv[0:CD, :], wv).then_inc(sem(tag + "_wvo"), 16)
            eng.dma_start(Wo, wo.rearrange("(g p) n -> p g n", p=P)).then_inc(sem(tag + "_wvo"), 16)

        def dve_scales(dve, tag, n, count):
            dve.wait_ge(sem("gT"), count)
            nc.vector.tensor_reduce(gr[0:n, 0:1], bank(7)[0:n, 0:P], X, ALU.max).then_inc(sem("g_step"), 1)
            dve.wait_ge(sem("g_step"), 3 * count - 2)
            nc.vector.tensor_scalar(gr[0:n, 1:1 + n], ident[0:n, 0:n], gr[0:n, 0:1], None, ALU.mult)\
                .then_inc(sem("g2"), 1)
            dve.wait_ge(sem("gB"), count)
            nc.vector.tensor_scalar(gq[:, 2:2 + n], bank(7)[:, 256:256 + n], 1.0 / 32767.0, 1e-12,
                                    ALU.mult, ALU.max).then_inc(sem("g_step"), 1)
            dve.wait_ge(sem("g_step"), 3 * count - 1)
            nc.vector.reciprocal(gq[:, 4:4 + n], gq[:, 2:2 + n]).then_inc(sem("g_step"), 1)
            dve.wait_ge(sem("g_step"), 3 * count)

        def pe_scales(pe, n, count):
            pe.wait_ge(sem("g0"), count)
            nc.tensor.transpose(bank(7)[0:n, 0:P], gq[:, 0:n], ident).then_inc(sem("gT"), 1)
            pe.wait_ge(sem("g2"), count)
            nc.tensor.matmul(bank(7)[:, 256:256 + n], cf[0:n, C_ONE:C_ONE + P], gr[0:n, 1:1 + n],
                             start=True, stop=True).then_inc(sem("gB"), 1)

        @block.sync
        def _(sp):
            sp.dma_start(xs[:, :, :], a["x"].rearrange("b s d -> (b s) d").rearrange("(t p) d -> p t d", p=P))\
                .then_inc(sem("x_in"), 16)
            sp.dma_start(cf[:, :], a["cf"]).then_inc(sem("cf"), 16)
            load_absorb(sp, "w0", a["L0_xattn_Wq"], a["L0_xattn_Wkv"][:, 0:1024], a["L0_xattn_Wkv"][:, 1024:2048],
                        a["L0_xattn_Wo"])
            sp.dma_start(vecs[0:VECS, :], a["columns"]).then_inc(sem("vecs"), 16)
            sp.dma_start(emb[:, :], a["L1_attn_rel_emb"]).then_inc(sem("vecs"), 16)
            sp.dma_start(mask8[:, :], a["mask_1x1xSxS2_bk0"].rearrange("a b s k -> (a b s) k")).then_inc(sem("mask"), 16)
            for b in range(B):
                src = a["ctx_768"][b]
                sp.dma_start(tail_raw[:, b, 0:TAILS - 1, :],
                             src[TAIL0 * P:(NCH - 1) * P, :].rearrange("(c p) d -> p c d", p=P))\
                    .then_inc(sem(f"tail{b // 2}"), 16)
                sp.dma_start(tail_raw[0:LAST, b, TAILS - 1, :], src[(NCH - 1) * P:KEYS, :])\
                    .then_inc(sem(f"tail{b // 2}"), 16)
                if b == 0:
                    sp.dma_start(ch[:, :], a["ch"]).then_inc(sem("ch"), 16)
            sp.dma_start(ctxTh[CD:KS, :], a["ones"]).then_inc(sem("ones_rows"), 16)
            sp.dma_start(wqk1[:, 0, :], a["L1_attn_Wqk"]).then_inc(sem("small"), 16)
            sp.dma_start(wqk1[:, 1, :], a["L1_attn_Wv"]).then_inc(sem("small"), 16)
            sp.dma_start(rw[:, :], a["L1_ffn_router_w"]).then_inc(sem("small"), 16)
            sp.dma_start(rows1[:, :], a["rows"]).then_inc(sem("small"), 16)
            sp.wait_ge(sem("gp"), 1)
            sp.dma_start(scratch.unsqueeze(0), gp[:, :]).then_inc(sem("gp_out"), 16)
            sp.wait_ge(sem("gp_out"), 16)
            hs = bass.AP(scratch.tensor, 0, [[1, S], [1, S]])
            sp.dma_start(hank[:, :], hs).then_inc(sem("hank"), 16)
            sp.wait_ge(sem("abs"), 8)
            either(sp, sp_attention)
            sp.wait_ge(sem("x0_out_copied"), B)
            sp.dma_start(sraw[:, 0:3, :], a["L0_attn_qkv_weight"].rearrange("(g p) n -> p g n", p=P)).then_inc(sem("mid"), 16)
            sp.dma_start(sraw[:, 3, :], a["L0_attn_proj_weight"]).then_inc(sem("mid"), 16)
            sp.dma_start(ffraw[:, 0:3, :], a["L0_ffn_w_gate"].rearrange("(g p) n -> p g n", p=P)).then_inc(sem("mid"), 16)
            sp.dma_start(ffraw[:, 3:6, :], a["L0_ffn_w_up"].rearrange("(g p) n -> p g n", p=P)).then_inc(sem("mid"), 16)
            sp.dma_start(ffraw[:, 6:9, :], a["L0_ffn_w_down"].rearrange("p (g n) -> p g n", g=3)).then_inc(sem("mid"), 16)
            sp.wait_ge(sem("heads_p"), 1)
            load_absorb(sp, "w1", a["L1_xattn_Wq"], a["L1_xattn_Wk"], a["L1_xattn_Wv"], a["L1_xattn_Wo"])
            sp_attention(sp, att1)
            sp.wait_ge(sem("x1_out_copied"), B)
            for e in range(SELS):
                f1, f2 = ("L1_ffn_w1", "L1_ffn_w2") if e < EXPERTS else ("L1_ffn_ow1", "L1_ffn_ow2")
                f1, f2 = (a[f1][e], a[f2][e]) if e < EXPERTS else (a[f1], a[f2])
                sp.dma_start(wraw32[e][:, 0:HID], f1).then_inc(sem(f"ex{e}"), 16)
                sp.dma_start(wraw32[e][:, HID:EW].rearrange("p (c n) -> p c n", c=HC),
                             f2.rearrange("(c p) n -> p c n", p=P)).then_inc(sem(f"ex{e}"), 16)
            sp.wait_ge(sem("x_sum"), 7)
            sp.dma_start(out.rearrange("b s d -> (b s) d").rearrange("(t p) d -> p t d", p=P), xs[:, :, :])\
                .then_inc(sem("stored"), 16)
            sp.wait_ge(sem("stored"), 16)

        @block.gpsimd
        def _(pool):
            nc.gpsimd.memset(mhalf[:, :], -0.5).then_inc(sem("fills"), 1)
            nc.gpsimd.memset(magic[:, 0:1], MAGIC)
            nc.gpsimd.memset(magic[:, 1:2], -MAGIC)
            pool.wait_ge(sem("fills"), 1)
            pool_ln(pool, "l0a")
            pool_ln(pool, "l0b")
            pool.wait_ge(sem("ln_rstd"), 2)
            nc.gpsimd.memset(maskb[S:P, :], 0.0).then_inc(sem("fills"), 1)
            pool.wait_ge(sem("fills"), 2)
            n3 = ctxNh[:, :].rearrange("p (c f) -> p c f", f=CPAD)
            nc.gpsimd.memset(n3[:, :, CD:CPAD], 1.0).then_inc(sem("fills"), 1)
            n3 = ctxNl[:, :].rearrange("p (c f) -> p c f", f=CPAD)
            nc.gpsimd.memset(n3[:, :, CD:CPAD], 0.0).then_inc(sem("fills"), 1)
            for b in range(B):
                pool.wait_ge(sem(f"tail{b // 2}"), 64)
                pool_by_keys(b, tail_raw[:, b], TAIL0, TAILS - 1, 2 * b + 2)
            either(pool, pool_attention)
            pool.wait_ge(sem("x0_out_copied"), B)
            for at in (0, 1536):
                nc.gpsimd.memset(tq[:, at:at + TOK], 0.0).then_inc(sem("fills"), 1)
            for tag in ("l1", "l2", "l3"):
                pool_ln(pool, tag)
            pool_attention(pool, att1)
            pool.wait_ge(sem("w_high"), 1)
            nc.gpsimd.memset(tl[:, 2560:3072], 0.0).then_inc(sem("fills"), 1)
            pool_experts(pool, 0, 4)
            pool_ln(pool, "l4")
            pool_experts(pool, 4, SELS)
            pool_ln(pool, "l5")
            for e in range(1, EXPERTS):
                pool.wait_ge(sem("chosen"), e + 1)
                if e >= 2:
                    pool.wait_ge(sem("acc"), e - 1)
                nc.gpsimd.tensor_tensor(total, total, prod[e % 2], ALU.add).then_inc(sem("acc"), 1)

        @block.scalar
        def _(act):
            act_absorb(act, "w0", range(6), range(4))
            for b in range(B):
                act.wait_ge(sem("ctx_tp"), b + 1)
                at = slice(b * KPAD + TAIL0 * P, b * KPAD + KEYS)
                nc.scalar.activation(ctxTh[0:CD, at], bank(b % 4)[0:CD, 0:KEYS - TAIL0 * P], ACT.Copy)\
                    .then_inc(sem("ctx_th"), 1)
            act.wait_ge(sem("vT"), 1)
            nc.scalar.activation(vcol[:, 0:VECS], bank(7)[:, 0:VECS], ACT.Copy).then_inc(sem("vcol"), 1)
            act_absorb(act, "w0", range(6), range(4, 6))
            act.wait_ge(sem("ln_T"), nth("l0b") - 1)
            act.wait_ge(sem("vcol"), 1)
            nc.scalar.activation(yT[:, :], bank(6), ACT.Identity, bias=vcol[:, 1:2], scale=vcol[:, 0:1])\
                .then_inc(sem("yT0"), 1)
            either(act, act_attention)
            act_heads_out(act, 1, vcol[:, V_BO:V_BO + 1])
            act.wait_ge(sem("sT"), 1)
            nc.scalar.activation(qkvT[:, :], bank(2)[:, 0:3 * D], ACT.Copy).then_inc(sem("sTs"), 1)
            nc.scalar.activation(projT[:, :], bank(2)[:, 3 * D:4 * D], ACT.Copy).then_inc(sem("sTs"), 1)
            act.wait_ge(sem("ln_T"), nth("l1") - 1)
            nc.scalar.activation(yT[:, :], bank(0), ACT.Copy).then_inc(sem("yT1"), 1)
            act.wait_ge(sem("lq"), 1)
            act.wait_ge(sem("fills"), 6)
            for odd in range(2):
                nc.scalar.activation(seq_q[odd][:, :, odd, :],
                                     bank(1).rearrange("p (t o s) -> p t o s", t=TILES, o=2)[:, :, odd, :], ACT.Relu)\
                    .then_inc(sem("lqs"), 1)
            act_absorb(act, "w1", (0, 1, 2, 3, 2, 3))
            for k in range(3):
                act.wait_ge(sem("fwT"), k + 1)
                nc.scalar.activation(ffT[:, 3 * k:3 * k + 3, :],
                                     bank(FB[k])[:, 0:3 * P].rearrange("p (g n) -> p g n", g=3), ACT.Copy)\
                    .then_inc(sem("fwTs"), 1)
            act_products(act, "w1", range(4), (bank(0), bank(1)))
            act_products(act, "w1", range(4, 5), MISC)
            act.wait_ge(sem("gate"), 2)
            nc.scalar.activation(tl[:, 1536:3072], tl[:, 0:1536], ACT.Tanh, scale=0.5).then_inc(sem("up"), 1)
            act_products(act, "w1", range(5, 8), MISC)
            up = tq[:, 0:1536]
            nc.scalar.activation(up, PS[:, 1536:3072], ACT.Identity, bias=magic[:, 0:1], scale=gu[:, 3:4])\
                .then_inc(sem("up"), 1)
            act.wait_ge(sem("up"), 2)
            nc.scalar.activation(up, up, ACT.Identity, bias=magic[:, 1:2]).then_inc(sem("up"), 1)
            act.wait_ge(sem("up"), 3)
            nc.scalar.activation(up, up, ACT.Copy, scale=gu[:, 1:2]).then_inc(sem("up"), 1)
            act.wait_ge(sem("ln_T"), nth("l3") - 1)
            nc.scalar.activation(yT[:, :], bank(6), ACT.Copy).then_inc(sem("yT3"), 1)
            act_attention(act, att1)
            act_experts(act, 0, 4)
            act_heads_out(act, 2, vcol[:, V_BO + 1:V_BO + 2])
            act_experts(act, 4, SELS)
            act.wait_ge(sem("ln_T"), nth("l4") - 1)
            nc.scalar.activation(yT[:, :], bank(0), ACT.Copy).then_inc(sem("yT4"), 1)
            act.wait_ge(sem("sqk"), 1)
            nc.scalar.activation(tq[:, 0:512], bank(1), ACT.Identity, bias=vcol[:, 2:3]).then_inc(sem("s_act"), 1)
            act.wait_ge(sem("s_act"), 1)
            nc.scalar.activation(tq[:, 512:1024], tq[:, 0:512], ACT.Tanh, scale=0.5).then_inc(sem("s_act"), 1)
            act.wait_ge(sem("sv"), 1)
            nc.scalar.activation(tl[:, 0:512], bank(2), ACT.Tanh, scale=0.5).then_inc(sem("s_act"), 1)
            act.wait_ge(sem("z2"), 1)
            nc.scalar.activation(tp[:, 0:256], tp[:, 256:512], ACT.Exp, scale=-1.0).then_inc(sem("ze"), 1)
            act.wait_ge(sem("ln_T"), nth("l5") - 1)
            nc.scalar.activation(yT[:, :], bank(0), ACT.Copy).then_inc(sem("yT5"), 1)
            nc.scalar.activation(yTh, bank(0), ACT.Copy).then_inc(sem("yT5"), 1)
            for k in range(SELS * HC):
                act.wait_ge(sem("hid"), k + 1)
                if k >= 2:
                    act.wait_ge(sem("hid_low"), k - 1)
                nc.scalar.activation(hid32[:, k % 2, :], bank(HB[k % 4]), ACT.Relu,
                                     bias=vcol[:, V_B1 + k:V_B1 + k + 1]).then_inc(sem("hid_a"), 1)
                if k > HC and k % HC == 1 or k == SELS * HC - 1:
                    e = k // HC - (k < SELS * HC - 1)
                    act.wait_ge(sem("sel_p"), e + 1)
                    if e >= 2:
                        act.wait_ge(sem("chosen"), e - 1)
                    nc.scalar.activation(sel_b[e % 2], bank(e % 2), ACT.Copy).then_inc(sem("sel_s"), 1)

        @block.vector
        def _(dve):
            dve_ln(dve, "l0a", xs, (sem("x_in"), 16))
            dve_ln(dve, "l0b", yn, (sem("ln_rows"), nth("l0a")))
            dve_absorb(dve)
            dve.wait_ge(sem("mask"), 16)
            nc.vector.tensor_reduce(flag_c[:, :], mask8[:, 0:TAIL0 * P], X, ALU.max).then_inc(sem("flag_c"), 1)
            nc.vector.tensor_scalar(maskb[0:S, 0:KEYS], mask8[:, :], -NEG, NEG, ALU.mult, ALU.add)\
                .then_inc(sem("maskb"), 1)
            for b in range(B):
                dve.wait_ge(sem("ctx_th"), b + 1)
                at = slice(b * KPAD + TAIL0 * P, b * KPAD + KEYS)
                nc.vector.tensor_tensor(ctxTl[0:CD, at], bank(b % 4)[0:CD, 0:KEYS - TAIL0 * P], ctxTh[0:CD, at],
                                        ALU.subtract).then_inc(sem("ctx_tl"), 1)
            dve.wait_ge(sem("gp_p"), 1)
            nc.vector.tensor_scalar(gp[:, :], bank(6)[0:1, 0:2 * S], D ** 0.5 * ERF_A, -MU * ERF_A,
                                    ALU.mult, ALU.add).then_inc(sem("gp"), 1)
            dve.wait_ge(sem("vcol"), 1)
            nc.vector.tensor_scalar(ghalf[:, :], vcol[:, 3:5], 0.5, None, ALU.mult)
            dve.wait_ge(sem("flag_T"), 1)
            nc.vector.tensor_reduce(flag_r[:, :], bank(7)[0:1, 256:256 + S], X, ALU.max).then_inc(sem("flag_c"), 1)
            dve.wait_ge(sem("flag_c"), 2)
            nc.vector.tensor_copy(flag_i[:, :], flag_r[:, :]).then_inc(sem("flag"), 1)
            either(dve, dve_attention)
            w36 = ffraw[:, :, :].rearrange("p g (k n) -> p (g k) n", n=WBLK)
            dve.wait_ge(sem("mid"), 16 * 5)
            nc.vector.tensor_reduce(fsc[:, :], w36, X, ALU.max, apply_absolute_value=True).then_inc(sem("fw"), 1)
            dve.wait_ge(sem("fw"), 1)
            nc.vector.tensor_scalar(fsc[:, :], fsc[:, :], 1.0 / 7.0, 1e-12, ALU.mult, ALU.max).then_inc(sem("fw"), 1)
            dve.wait_ge(sem("fw"), 2)
            nc.vector.reciprocal(fin[:, :], fsc[:, :]).then_inc(sem("fw"), 1)
            dve.wait_ge(sem("fw"), 3)
            nc.vector.tensor_tensor(w36, w36, fin[:, :].unsqueeze(2).to_broadcast([P, 36, WBLK]), ALU.mult)\
                .then_inc(sem("fw"), 1)
            dve.wait_ge(sem("fw"), 4)
            nc.vector.tensor_scalar(w36, w36, MAGIC, -MAGIC, ALU.add, ALU.add).then_inc(sem("fw"), 1)
            dve.wait_ge(sem("fw"), 5)
            nc.vector.tensor_tensor(w36, w36, fsc[:, :].unsqueeze(2).to_broadcast([P, 36, WBLK]), ALU.mult)\
                .then_inc(sem("fw"), 1)
            dve_residual(dve, "a0", bank(6))
            dve_ln(dve, "l1", xs, (sem("x_sum"), 1))
            kk = tq[:, 512:1024].rearrange("p (t n) -> p t n", t=TILES)
            vv = tq[:, 1024:1536].rearrange("p (t n) -> p t n", t=TILES)
            for t in range(TILES):
                dve.wait_ge(sem("lkv"), t + 1)
                src = bank(2 + t)
                nc.vector.tensor_scalar(kk[:, t, :], src[:, 0:D], 0.0, None, ALU.max)
                nc.vector.tensor_scalar(vv[:, t, :], src[:, D:2 * D], 0.0, None, ALU.max).then_inc(sem("lkvs"), 1)
            blk = cf[:, C_BLK:C_BLK + P]
            kvm = tq[:, 2048:3072].rearrange("p (b n) -> p b n", b=B)
            ksm = tq[:, 3072:4096].rearrange("p (b n) -> p b n", b=B)
            for odd in range(2):
                dve.wait_ge(sem("kv"), odd + 1)
                src = bank(odd).rearrange("p (b n) -> p b n", b=4)
                nc.vector.tensor_tensor(kvm[:, odd:B:2, :], src, blk.unsqueeze(1).to_broadcast([P, 4, P]), ALU.mult)
                dve.wait_ge(sem("ks"), odd + 1)
                src = bank(2 + odd)[:, 0:4].unsqueeze(2).to_broadcast([P, 4, P])
                nc.vector.tensor_tensor(ksm[:, odd:B:2, :], src, blk.unsqueeze(1).to_broadcast([P, 4, P]), ALU.mult)\
                    .then_inc(sem("kvm"), 1)
            dve.wait_ge(sem("lden"), 1)
            den, rat = tl[:, 0:512], tl[:, 512:1024]
            nc.vector.tensor_scalar(den, bank(5), 1e-15, None, ALU.add).then_inc(sem("den"), 1)
            dve.wait_ge(sem("den"), 1)
            nc.vector.reciprocal(rat, den).then_inc(sem("den"), 1)
            dve.wait_ge(sem("den"), 2)
            nc.vector.tensor_tensor(rat, bank(4), rat, ALU.mult).then_inc(sem("rat"), 1)
            dve_residual(dve, "a1", bank(6))
            dve_ln(dve, "l2", xs, (sem("x_sum"), 2))
            dve.wait_ge(sem("ln_rows"), nth("l2"))
            y512 = yn[:, :, :].rearrange("p t n -> p (t n)")
            nc.vector.tensor_reduce(gq[:, 0:1], y512, X, ALU.max, apply_absolute_value=True).then_inc(sem("g0"), 1)
            dve_scales(dve, "x", 1, 1)
            dve.wait_ge(sem("ln_T"), nth("l2") - 1)
            nc.vector.tensor_scalar(yT[:, :], bank(6), gq[:, 4:5], MAGIC, ALU.mult, ALU.add).then_inc(sem("fy"), 1)
            dve.wait_ge(sem("fy"), 1)
            nc.vector.tensor_scalar(yT[:, :], yT[:, :], -MAGIC, gq[:, 2:3], ALU.add, ALU.mult).then_inc(sem("fy"), 1)
            gate, up = tl[:, 0:1536], tq[:, 0:1536]
            sg, gs = tq[:, 1536:3072], tl[:, 1536:3072]
            dve.wait_ge(sem("fg"), 3)
            nc.vector.tensor_reduce(gq[:, 0:1], PS[:, 0:1536], X, ALU.max, apply_absolute_value=True)
            dve.wait_ge(sem("fu"), 3)
            nc.vector.tensor_reduce(gq[:, 1:2], PS[:, 1536:3072], X, ALU.max, apply_absolute_value=True)\
                .then_inc(sem("g0"), 1)
            dve_scales(dve, "gu", 2, 2)
            nc.vector.tensor_copy(gu[:, :], gq[:, 2:6])
            nc.vector.tensor_scalar(gate, PS[:, 0:1536], gq[:, 4:5], MAGIC, ALU.mult, ALU.add).then_inc(sem("gate"), 1)
            dve.wait_ge(sem("gate"), 1)
            nc.vector.tensor_scalar(gate, gate, -MAGIC, gq[:, 2:3], ALU.add, ALU.mult).then_inc(sem("gate"), 1)
            dve.wait_ge(sem("up"), 1)
            nc.vector.tensor_scalar(sg, tl[:, 1536:3072], 32768.0, MAGIC + 32768.0, ALU.mult, ALU.add)\
                .then_inc(sem("sg"), 3)
            dve.wait_ge(sem("sg"), 3)
            nc.vector.tensor_scalar(sg, sg, -MAGIC, 65535.0, ALU.add, ALU.min).then_inc(sem("sg"), 1)
            dve.wait_ge(sem("sg"), 4)
            nc.vector.scalar_tensor_tensor(gs, sg, 2.0 ** -16, gate, ALU.mult, ALU.mult).then_inc(sem("sg"), 1)
            dve.wait_ge(sem("sg"), 5)
            nc.vector.tensor_reduce(gq[:, 0:1], gs, X, ALU.max, apply_absolute_value=True).then_inc(sem("g0"), 1)
            dve_scales(dve, "gs", 1, 3)
            nc.vector.tensor_scalar(gs, gs, gq[:, 4:5], MAGIC, ALU.mult, ALU.add).then_inc(sem("sg"), 1)
            dve.wait_ge(sem("sg"), 6)
            nc.vector.tensor_scalar(gs, gs, -MAGIC, gq[:, 2:3], ALU.add, ALU.mult).then_inc(sem("sg"), 1)
            dve.wait_ge(sem("sg"), 7)
            dve.wait_ge(sem("up"), 4)
            nc.vector.tensor_tensor(gs, gs, up, ALU.mult).then_inc(sem("sg"), 1)
            dve.wait_ge(sem("sg"), 8)
            nc.vector.tensor_reduce(gq[:, 0:1], gs, X, ALU.max, apply_absolute_value=True).then_inc(sem("g0"), 1)
            dve_scales(dve, "o", 1, 4)
            nc.vector.tensor_scalar(gs, gs, gq[:, 4:5], MAGIC, ALU.mult, ALU.add).then_inc(sem("sg"), 1)
            dve.wait_ge(sem("sg"), 9)
            nc.vector.tensor_scalar(gs, gs, -MAGIC, gq[:, 2:3], ALU.add, ALU.mult).then_inc(sem("fo"), 1)
            dve_residual(dve, "a2", bank(6))
            dve_ln(dve, "l3", xs, (sem("x_sum"), 3))
            dve_attention(dve, att1)
            dve_residual(dve, "a3", bank(6))
            dve_ln(dve, "l4", xs, (sem("x_sum"), 4))
            dve.wait_ge(sem("biasT"), 1)
            nc.vector.tensor_copy(biasz[:, :], bank(7)[:, 0:S]).then_inc(sem("biasz"), 1)
            lin, ex = tq[:, 0:512], tq[:, 512:1024]
            dve.wait_ge(sem("s_act"), 2)
            nc.vector.scalar_tensor_tensor(lin, ex, 1.0, lin, ALU.add, ALU.mult).then_inc(sem("sw"), 1)
            dve.wait_ge(sem("sw"), 1)
            qT, kT = tq[:, 1024:1536], tq[:, 1536:2048]
            nc.vector.tensor_scalar(qT, lin, ghalf[:, 0:1], vcol[:, 5:6], ALU.mult, ALU.add)
            nc.vector.tensor_scalar(kT, lin, ghalf[:, 1:2], vcol[:, 6:7], ALU.mult, ALU.add).then_inc(sem("sqks"), 1)
            ev, vr = tl[:, 0:512], tl[:, 512:1024]
            dve.wait_ge(sem("s_act"), 3)
            nc.vector.tensor_scalar(ev, ev, 0.5, 0.5, ALU.mult, ALU.add).then_inc(sem("sw"), 1)
            dve.wait_ge(sem("sw"), 2)
            nc.vector.tensor_tensor(vr, bank(2), ev, ALU.mult).then_inc(sem("svr"), 1)
            z, z2 = tl[:, 1024:1280], tp[:, 256:512]
            az, tt, acc = tl[:, 1280:1536], tl[:, 1536:1792], tl[:, 1792:2048]
            dve.wait_ge(sem("sim"), 1)
            dve.wait_ge(sem("biasz"), 1)
            for odd in range(2):
                r = slice(odd * S, odd * S + S)
                ins = nc.vector.scalar_tensor_tensor(
                    z[r, :].rearrange("p (t n) -> p t n", t=TILES),
                    bank(3)[r, :].rearrange("p (t n) -> p t n", t=TILES)[:, :, r],
                    ERF_A / S, biasz[r, :].unsqueeze(1).to_broadcast([S, TILES, S]), ALU.mult, ALU.add)
            ins.then_inc(sem("z"), 1)
            dve.wait_ge(sem("z"), 1)
            nc.vector.tensor_tensor(z2, z, z, ALU.mult).then_inc(sem("z2"), 1)
            nc.vector.scalar_tensor_tensor(az, z, -1.0, z, ALU.mult, ALU.max).then_inc(sem("z"), 1)
            dve.wait_ge(sem("z"), 2)
            nc.vector.tensor_scalar(az, az, ERF_P, 1.0, ALU.mult, ALU.add).then_inc(sem("z"), 1)
            dve.wait_ge(sem("z"), 3)
            nc.vector.reciprocal(tt, az).then_inc(sem("z"), 1)
            dve.wait_ge(sem("z"), 4)
            nc.vector.tensor_scalar(acc, tt, ERF_C[4], None, ALU.mult).then_inc(sem("z"), 1)
            for i in range(4):
                dve.wait_ge(sem("z"), 5 + i)
                nc.vector.scalar_tensor_tensor(acc, acc, ERF_C[3 - i], tt, ALU.add, ALU.mult).then_inc(sem("z"), 1)
            dve.wait_ge(sem("z"), 9)
            dve.wait_ge(sem("ze"), 1)
            nc.vector.scalar_tensor_tensor(acc, acc, 0.5, tp[:, 0:256], ALU.mult, ALU.mult).then_inc(sem("z"), 1)
            nc.vector.tensor_scalar(az, z, 0.0, -2.0, ALU.is_ge, ALU.mult).then_inc(sem("z"), 1)
            dve.wait_ge(sem("z"), 11)
            nc.vector.scalar_tensor_tensor(acc, az, 1.0, acc, ALU.add, ALU.mult).then_inc(sem("z"), 1)
            dve.wait_ge(sem("z"), 12)
            nc.vector.scalar_tensor_tensor(acc, az, -0.5, acc, ALU.mult, ALU.add).then_inc(sem("z"), 1)
            dve.wait_ge(sem("z"), 13)
            for odd in range(2):
                r = slice(odd * S, odd * S + S)
                ins = nc.vector.tensor_tensor(
                    tl[r, 2560:3072].rearrange("p (t n) -> p t n", t=TILES)[:, :, r],
                    acc[r, :].rearrange("p (t n) -> p t n", t=TILES),
                    cf[r, C_CAUSAL + odd * S:C_CAUSAL + odd * S + S].unsqueeze(1).to_broadcast([S, TILES, S]), ALU.mult)
            ins.then_inc(sem("attn"), 1)
            dve_residual(dve, "a4", bank(6))
            dve_ln(dve, "l5", xs, (sem("x_sum"), 5))
            dve.wait_ge(sem("yT5"), 2)
            nc.vector.tensor_tensor(yTl, bank(0), yTh, ALU.subtract).then_inc(sem("yTl"), 1)
            lg = tp[:, 0:32].rearrange("p (t e) -> p t e", e=EXPERTS)
            sc8 = tp[:, 32:64].rearrange("p (t e) -> p t e", e=EXPERTS)
            top = tp[:, 64:68]
            oh = tp[:, 68:100].rearrange("p (t e) -> p t e", e=EXPERTS)
            sel = tp[:, 100:136].rearrange("p (t e) -> p t e", e=SELS)
            oh16 = Pl[:, 0:32]
            sel16 = Pl[:, 32:32 + 4 * SELS]
            lp = bank(1)[:, 0:32].rearrange("p (t e) -> p t e", e=EXPERTS)
            dve.wait_ge(sem("rlog"), 1)
            nc.vector.tensor_reduce(top, lp, X, ALU.max).then_inc(sem("r"), 1)
            dve.wait_ge(sem("r"), 1)
            nc.vector.tensor_tensor(lg, lp, top.unsqueeze(2).to_broadcast([P, TILES, EXPERTS]), ALU.is_ge)\
                .then_inc(sem("r"), 1)
            dve.wait_ge(sem("r"), 2)
            nc.vector.tensor_tensor(sc8, lg, cf[:, C_FIRST:C_FIRST + EXPERTS].unsqueeze(1).to_broadcast(
                [P, TILES, EXPERTS]), ALU.mult).then_inc(sem("r"), 1)
            dve.wait_ge(sem("r"), 3)
            nc.vector.tensor_reduce(top, sc8, X, ALU.max).then_inc(sem("r"), 1)
            dve.wait_ge(sem("r"), 4)
            nc.vector.tensor_tensor(oh, sc8, top.unsqueeze(2).to_broadcast([P, TILES, EXPERTS]), ALU.is_equal)\
                .then_inc(sem("r"), 1)
            dve.wait_ge(sem("r"), 5)
            nc.vector.tensor_copy(oh16.rearrange("p (t e) -> p t e", e=EXPERTS), oh).then_inc(sem("oh"), 1)
            def split_hidden(k):
                dve.wait_ge(sem("hid_a"), k + 1)
                if k >= 4:
                    dve.wait_ge(sem("hid_used"), k - 3)
                nc.vector.tensor_copy(hid_hi[:, k % 4, :], hid32[:, k % 2, :]).then_inc(sem("hid_high"), 1)
                dve.wait_ge(sem("hid_high"), k + 1)
                nc.vector.tensor_tensor(hid_lo[:, k % 4, :], hid32[:, k % 2, :], hid_hi[:, k % 4, :], ALU.subtract)\
                    .then_inc(sem("hid_low"), 1)

            def choose(e):
                dve.wait_ge(sem("sel_s"), e + 1)
                dve.wait_ge(sem("hid_used"), HC * (e + 1))
                if e >= 3:
                    dve.wait_ge(sem("acc"), e - 2)
                o = total if e == 0 else prod[e % 2]
                nc.vector.scalar_tensor_tensor(o, bank(6 + e % 2), vcol[:, V_B2 + e:V_B2 + e + 1], sel_b[e % 2],
                                               ALU.add, ALU.mult).then_inc(sem("chosen"), 1)

            split_hidden(0)
            split_hidden(1)
            dve.wait_ge(sem("rank"), 1)
            rk = bank(0)[:, 0:32].rearrange("p (t e) -> p t e", e=EXPERTS)
            nc.vector.scalar_tensor_tensor(sel[:, :, 0:EXPERTS], rk, float(CAP), oh, ALU.is_le, ALU.mult)\
                .then_inc(sem("r"), 1)
            dve.wait_ge(sem("r"), 6)
            nc.vector.tensor_reduce(top, sel[:, :, 0:EXPERTS], X, ALU.add).then_inc(sem("r"), 1)
            dve.wait_ge(sem("r"), 7)
            nc.vector.tensor_scalar(sel[:, :, EXPERTS], top, -1.0, 1.0, ALU.mult, ALU.add).then_inc(sem("r"), 1)
            dve.wait_ge(sem("r"), 8)
            nc.vector.tensor_copy(sel16.rearrange("p (t e) -> p t e", e=SELS), sel).then_inc(sem("sel"), 1)
            for k in range(2, 4):
                split_hidden(k)
            dve.wait_ge(sem("selT"), 1)
            nc.vector.tensor_copy(selT16, bank(1).bitcast(F16)[0:SELS, 0:TOK]).then_inc(sem("selT_s"), 1)
            for k in range(4, SELS * HC):
                if k % HC == 2:
                    choose(k // HC - 1)
                split_hidden(k)
            choose(EXPERTS)
            dve_residual(dve, "a5", bank(1))
            dve.wait_ge(sem("x_sum"), 6)
            dve_residual(dve, "a6", bank(7))

        @block.tensor
        def _(pe):
            pe.wait_ge(sem("cf"), 16)
            pe.wait_ge(sem("w0_wqk"), 32)
            pe_weights_T(pe, "w0", range(4))
            pe_absorb(pe, "w0", 0, [bank(k) for k in range(4, 8)])
            for b in range(B):
                pe.wait_ge(sem(f"tail{b // 2}"), 64)
                if b >= 4:
                    pe.wait_ge(sem("ctx_tl"), b - 3)
                for c in range(TAILS):
                    _, n = chunk(TAIL0 + c)
                    ins = nc.tensor.transpose(bank(b % 4)[0:CD, c * P:c * P + n], tail_raw[0:n, b, c, :],
                                              ident[0:n, 0:n])
                ins.then_inc(sem("ctx_tp"), 1)
            pe.wait_ge(sem("vecs"), 2 * 16)
            pe.wait_ge(sem("abs"), 4)
            nc.tensor.matmul(bank(6)[0:1, 0:2 * S], emb[:, :], cf[0:BUCKETS, C_ONEHOT:C_ONEHOT + 2 * S],
                             start=True, stop=True).then_inc(sem("gp_p"), 1)
            nc.tensor.transpose(bank(7)[:, 0:VECS], vecs[0:VECS, :], ident[0:VECS, 0:VECS]).then_inc(sem("vT"), 1)
            pe.wait_ge(sem("w0_wvo"), 32)
            pe_weights_T(pe, "w0", range(4, 6), first=4)
            pe.wait_ge(sem("gp"), 1)
            pe.wait_ge(sem("vcol"), 1)
            pe.wait_ge(sem("flag_c"), 1)
            nc.tensor.transpose(bank(7)[0:1, 256:256 + S], flag_c[:, :], ident[0:S, 0:S]).then_inc(sem("flag_T"), 1)
            pe.wait_ge(sem("ln_rows"), nth("l0b"))
            pe_rows_T(pe, yn, bank(6), sem("ln_T"))
            pe.wait_ge(sem("ctx_tl"), B)
            pe.wait_ge(sem("yT0"), 1)
            pe.wait_ge(sem("fills"), 4)
            pe.wait_ge(sem("maskb"), 1)
            pe.wait_ge(sem("ones_rows"), 16)
            pe.wait_ge(sem("ch"), 16)
            either(pe, pe_attention)
            pe.wait_ge(sem("small"), 16 * 4)
            pe_rows_out(pe, "a0", 1)
            pe.wait_ge(sem("mid"), 16 * 5)
            pe_rows_T(pe, sraw, bank(2), sem("sT"))
            pe.wait_ge(sem("ln_rows"), nth("l1"))
            pe_rows_T(pe, yn, bank(0), sem("ln_T"))
            pe.wait_ge(sem("yT1"), 1)
            pe.wait_ge(sem("sTs"), 2)
            nc.tensor.matmul(bank(1), qkvT[:, 0:D], yT[:, :], start=True, stop=True).then_inc(sem("lq"), 1)
            for t in range(TILES):
                nc.tensor.matmul(bank(2 + t)[:, 0:2 * D], yT[:, t * P:(t + 1) * P], qkvT[:, D:3 * D],
                                 start=True, stop=True).then_inc(sem("lkv"), 1)
            kk = tq[:, 512:1024].rearrange("p (t n) -> p t n", t=TILES)
            vv = tq[:, 1024:1536].rearrange("p (t n) -> p t n", t=TILES)
            kvm = tq[:, 2048:3072].rearrange("p (b n) -> p b n", b=B)
            ksm = tq[:, 3072:4096].rearrange("p (b n) -> p b n", b=B)
            pe.wait_ge(sem("lkvs"), TILES)
            pe.wait_ge(sem("lqs"), 2)
            for odd in range(2):
                r = slice(S * odd, S * odd + S)
                for t in range(TILES):
                    ins = nc.tensor.matmul(bank(odd)[:, t * P:(t + 1) * P], kk[r, t, :], vv[r, t, :],
                                           start=True, stop=True)
                ins.then_inc(sem("kv"), 1)
                for t in range(TILES):
                    ins = nc.tensor.matmul(bank(2 + odd)[:, t:t + 1], kk[r, t, :], cf[r, C_ONE:C_ONE + 1],
                                           start=True, stop=True)
                ins.then_inc(sem("ks"), 1)
            pe.wait_ge(sem("kvm"), 2)
            for t in range(TILES):
                for odd in range(2):
                    b = 2 * t + odd
                    q = tq[:, odd * 1536 + t * P:odd * 1536 + (t + 1) * P]
                    nc.tensor.matmul(bank(4)[:, t * P:(t + 1) * P], kvm[:, b, :], q, start=not odd, stop=bool(odd))
                for odd in range(2):
                    b = 2 * t + odd
                    q = tq[:, odd * 1536 + t * P:odd * 1536 + (t + 1) * P]
                    ins = nc.tensor.matmul(bank(5)[:, t * P:(t + 1) * P], ksm[:, b, :], q, start=not odd, stop=bool(odd))
            ins.then_inc(sem("lden"), 1)
            pe.wait_ge(sem("w1_wqk"), 32)
            pe_weights_T(pe, "w1", range(4))
            nc.tensor.matmul(bank(6), ones1, rows1[:, 0:D].unsqueeze(1).to_broadcast([1, TILES, D]),
                             start=True, stop=True)
            pe.wait_ge(sem("rat"), 1)
            for t in range(TILES):
                ins = nc.tensor.matmul(bank(6)[:, t * P:(t + 1) * P], tl[:, 512 + t * P:512 + (t + 1) * P], projT[:, :],
                                       start=False, stop=True, skip_group_check=True)
            ins.then_inc(sem("y"), 1)
            pe.wait_ge(sem("wTs"), 6 + 4)
            pe.wait_ge(sem("w1_wvo"), 32)
            pe_weights_T(pe, "w1", (2, 3), first=4)
            pe.wait_ge(sem("fw"), 6)
            for k in range(3):
                for g in range(3):
                    ins = nc.tensor.transpose(bank(FB[k])[:, g * P:(g + 1) * P], ffraw[:, 3 * k + g, :], ident)
                ins.then_inc(sem("fwT"), 1)
            pe_absorb(pe, "w1", 0, (bank(0), bank(1)))
            pe.wait_ge(sem("ln_rows"), nth("l2"))
            pe_rows_T(pe, yn, bank(6), sem("ln_T"))
            pe.wait_ge(sem("fwTs"), 3)
            pe_scales(pe, 1, 1)
            pe.wait_ge(sem("fy"), 2)
            pe.wait_ge(sem("abs"), 8 + 4)
            for k in range(3):
                nc.tensor.matmul(bank(k), ffT[:, k, :], yT[:, :], start=True, stop=True).then_inc(sem("fg"), 1)
            for k in range(3):
                nc.tensor.matmul(bank(3 + k), ffT[:, 3 + k, :], yT[:, :], start=True, stop=True).then_inc(sem("fu"), 1)
            pe_scales(pe, 2, 2)
            pe.wait_ge(sem("g_step"), 6)
            pe_absorb(pe, "w1", 1, MISC)
            pe.wait_ge(sem("abs"), 8 + 8)
            pe_scales(pe, 1, 3)
            pe_scales(pe, 1, 4)
            pe.wait_ge(sem("fo"), 1)
            gs = tl[:, 1536:3072]
            for t in range(TILES):
                for k in range(FC):
                    ins = nc.tensor.matmul(bank(6)[:, t * P:(t + 1) * P], gs[:, k * TOK + t * P:k * TOK + (t + 1) * P],
                                           ffT[:, 6 + k, :], start=(k == 0), stop=(k == FC - 1))
            ins.then_inc(sem("y"), 1)
            pe.wait_ge(sem("abs"), 8 * 1 + 8)
            pe.wait_ge(sem("ln_rows"), nth("l3"))
            pe_rows_T(pe, yn, bank(6), sem("ln_T"))
            pe.wait_ge(sem("yT3"), 1)
            pe_attention(pe, att1)
            pe_rows_out(pe, "a3", 2)
            nc.tensor.matmul(bank(2), ones1, rows1[:, D:2 * D].unsqueeze(1).to_broadcast([1, TILES, D]),
                             start=True, stop=True)
            pe.wait_ge(sem("ln_rows"), nth("l4"))
            pe_rows_T(pe, yn, bank(0), sem("ln_T"))
            pe.wait_ge(sem("hank"), 16)
            nc.tensor.matmul(bank(7)[:, 0:S], cf[0:S, C_FLIP:C_FLIP + P], hank[:, :], start=True, stop=True)\
                .then_inc(sem("biasT"), 1)
            pe.wait_ge(sem("yT4"), 1)
            nc.tensor.matmul(bank(1), wqk1[:, 0, :], yT[:, :], start=True, stop=True).then_inc(sem("sqk"), 1)
            for t in range(TILES):
                ins = nc.tensor.matmul(bank(2)[:, t * P:(t + 1) * P], yT[:, t * P:(t + 1) * P], wqk1[:, 1, :],
                                       start=False, stop=True, skip_group_check=True)
            ins.then_inc(sem("sv"), 1)
            pe.wait_ge(sem("sqks"), 1)
            for t in range(TILES):
                c = slice(t * P, (t + 1) * P)
                ins = nc.tensor.matmul(bank(3)[:, c], tq[:, 1536 + t * P:1536 + (t + 1) * P],
                                       tq[:, 1024 + t * P:1024 + (t + 1) * P], start=True, stop=True)
            ins.then_inc(sem("sim"), 1)
            pe.wait_ge(sem("attn"), 1)
            pe.wait_ge(sem("fills"), 7)
            pe.wait_ge(sem("svr"), 1)
            for t in range(TILES):
                ins = nc.tensor.matmul(bank(6)[:, t * P:(t + 1) * P], tl[:, 2560 + t * P:2560 + (t + 1) * P],
                                       tl[:, 512 + t * P:512 + (t + 1) * P], start=True, stop=True)
            ins.then_inc(sem("y"), 1)
            o = bank(1)[:, 0:TILES * EXPERTS]
            nc.tensor.matmul(o, ones1, rows1[:, 2 * D:2 * D + EXPERTS].unsqueeze(1).to_broadcast([1, TILES, EXPERTS]), start=True, stop=True)
            pe.wait_ge(sem("ln_rows"), nth("l5"))
            pe_rows_T(pe, yn, bank(0), sem("ln_T"))
            pe.wait_ge(sem("yT5"), 1)
            for t in range(TILES):
                ins = nc.tensor.matmul(o[:, t * EXPERTS:(t + 1) * EXPERTS], yT[:, t * P:(t + 1) * P], rw[:, :],
                                       start=False, stop=True, skip_group_check=True)
            ins.then_inc(sem("rlog"), 1)

            def hidden(k):
                e, c = divmod(k, HC)
                at = slice(c * P, (c + 1) * P)
                o = bank(HB[k % 4])
                if c == 0:
                    pe.wait_ge(sem("w_low"), e + 1)
                if k >= 4:
                    pe.wait_ge(sem("hid_a"), k - 3)
                nc.tensor.matmul(o, whigh[e][:, at], yTh, start=True, stop=False)
                nc.tensor.matmul(o, whigh[e][:, at], yTl, start=False, stop=False)
                nc.tensor.matmul(o, wlow[e][:, at], yTh, start=False, stop=True).then_inc(sem("hid"), 1)

            def expert_out(k):
                e, c = divmod(k, HC)
                at = slice(HID + c * D, HID + (c + 1) * D)
                o = bank(6 + e % 2)
                if c == 0 and e >= 2:
                    pe.wait_ge(sem("chosen"), e - 1)
                pe.wait_ge(sem("hid_low"), k + 1)
                nc.tensor.matmul(o, whigh[e][:, at], hid_hi[:, k % 4, :], start=(c == 0), stop=False)
                nc.tensor.matmul(o, whigh[e][:, at], hid_lo[:, k % 4, :], start=False, stop=False)
                nc.tensor.matmul(o, wlow[e][:, at], hid_hi[:, k % 4, :], start=False, stop=(c == HC - 1))\
                    .then_inc(sem("hid_used"), 1)

            def selected(e):
                if e >= 2:
                    pe.wait_ge(sem("sel_s"), e - 1)
                nc.tensor.matmul(bank(e % 2), ch[0:SELS, H_ROW + e * P:H_ROW + (e + 1) * P], selT16,
                                 start=True, stop=True).then_inc(sem("sel_p"), 1)

            pe.wait_ge(sem("yTl"), 1)
            hidden(0)
            hidden(1)
            pe.wait_ge(sem("oh"), 1)
            for t in range(TILES):
                o = bank(0)[:, t * EXPERTS:(t + 1) * EXPERTS]
                for u in range(t):
                    nc.tensor.matmul(o, ch[:, H_ONES:H_ONES + P], Pl[:, u * EXPERTS:(u + 1) * EXPERTS],
                                     start=(u == 0), stop=False)
                ins = nc.tensor.matmul(o, ch[:, H_TRI:H_TRI + P], Pl[:, t * EXPERTS:(t + 1) * EXPERTS],
                                       start=(t == 0), stop=True)
            ins.then_inc(sem("rank"), 1)
            for k in range(2, SELS * HC):
                hidden(k)
                expert_out(k - 2)
                if k == 3:
                    pe.wait_ge(sem("sel"), 1)
                    for t in range(TILES):
                        ins = nc.tensor.transpose(bank(1).bitcast(F16)[0:SELS, t * P:(t + 1) * P],
                                                  Pl[:, 32 + t * SELS:32 + (t + 1) * SELS], ident16)
                    ins.then_inc(sem("selT"), 1)
                if k == HC + 1:
                    pe.wait_ge(sem("selT_s"), 1)
                if k > HC and k % HC == 1:
                    selected(k // HC - 1)
            selected(EXPERTS)
            expert_out(SELS * HC - 2)
            expert_out(SELS * HC - 1)
            pe.wait_ge(sem("acc"), EXPERTS - 1)
            for u in range(TILES):
                ins = nc.tensor.transpose(bank(1)[:, u * P:(u + 1) * P], total[:, u * P:(u + 1) * P], ident)
            ins.then_inc(sem("y"), 1)
            pe.wait_ge(sem("chosen"), SELS)
            for u in range(TILES):
                ins = nc.tensor.transpose(bank(7)[:, u * P:(u + 1) * P], prod[0][:, u * P:(u + 1) * P], ident)
            ins.then_inc(sem("y"), 1)


_INS = ['x', 'ctx_768', 'mask_1x1xSxS2_bk0', 'L0_xattn_ln_gamma', 'L0_xattn_ln_beta', 'L0_xattn_Wq',
        'L0_xattn_Wkv', 'L0_xattn_Wo', 'L0_xattn_bo', 'L0_attn_qkv_weight', 'L0_attn_proj_weight',
        'L0_attn_proj_bias', 'L0_ffn_w_gate', 'L0_ffn_w_up', 'L0_ffn_w_down', 'L1_xattn_Wq', 'L1_xattn_Wk',
        'L1_xattn_Wv', 'L1_xattn_Wo', 'L1_xattn_bo', 'L1_attn_Wqk', 'L1_attn_bqk', 'L1_attn_gamma',
        'L1_attn_beta', 'L1_attn_Wv', 'L1_attn_bv', 'L1_attn_rel_emb', 'L1_ffn_router_w', 'L1_ffn_router_b',
        'L1_ffn_w1', 'L1_ffn_b1', 'L1_ffn_w2', 'L1_ffn_b2', 'L1_ffn_ow1', 'L1_ffn_ob1', 'L1_ffn_ow2',
        'L1_ffn_ob2']


def kernel(**inputs):
    import numpy as _np
    import concourse.bacc as _bacc
    from concourse import mybir as _mybir
    from concourse.bass_utils import run_bass_kernel_spmd as _run

    nc = _bacc.Bacc("TRN2", target_bir_lowering=False, num_devices=1)
    arrays, args = {}, {}
    c, h = constants()
    given = {n: _np.ascontiguousarray(inputs[n]) for n in _INS} | {"cf": c, "ch": h}
    cat = lambda names, shape: _np.concatenate([_np.reshape(given.pop(n), shape) for n in names], axis=-2)
    given["columns"] = cat(["L0_xattn_ln_gamma", "L0_xattn_ln_beta", "L1_attn_bqk", "L1_attn_gamma", "L1_attn_beta",
                            "L1_ffn_b1", "L1_ffn_ob1", "L0_xattn_bo", "L1_xattn_bo", "L1_ffn_b2", "L1_ffn_ob2"],
                           (-1, D))
    given["rows"] = _np.concatenate([given.pop("L0_attn_proj_bias"), given.pop("L1_attn_bv"),
                                     given.pop("L1_ffn_router_b")])[None]
    given["ones"] = _np.ones((NSH, B * KPAD), _np.float16)
    for name, v in given.items():
        arrays[f"in_{name}_dram"] = v
        args[name] = nc.dram_tensor(f"in_{name}_dram", v.shape, _mybir.dt.from_np(v.dtype),
                                    kind="ExternalInput").ap()
    o = nc.dram_tensor("out_0_dram", (B, S, D), F32, kind="ExternalOutput").ap()
    perceiver(nc, args, o)
    r = _run(nc, [arrays], core_ids=[0])
    return r.results[0]["out_0_dram"]
```
